# Optimizing a Trainium2 kernel written in Bass

```python
import numpy as np
import jax
import jax.numpy as jnp

def _softmax(x, axis=-1):
    return jax.nn.softmax(x, axis=axis)

def _gelu(x):
    return jax.nn.gelu(x, approximate=True)

def _silu(x):
    return jax.nn.silu(x)

def _sigmoid(x):
    return jax.nn.sigmoid(x)

def _layernorm(x, axis=-1, eps=1e-05):
    m = jnp.mean(x, axis=axis, keepdims=True)
    v = jnp.var(x, axis=axis, keepdims=True)
    return (x - m) / jnp.sqrt(v + eps)

def _scatter_add(tgt, idx, src, axis=0):
    return tgt.at[idx].add(src)

def _segment_sum(src, seg, n):
    return jax.ops.segment_sum(src, seg, n)
kernel_name = 'mk_vit_tower_d1_tok_img768_r4_c9214a'

def setup_inputs(seed: int=0):
    np.random.seed(seed)
    _w = jnp.asarray

    def _rec_inputs():
        import jax
        import jax.numpy as jnp
        _rk = jax.random.key(seed)
        x = -7.10856e-05 + 0.999911 * jax.random.normal(jax.random.fold_in(_rk, 1), (4, 32, 128, 128), jnp.float32)
        return x
    x = _rec_inputs()

    def _L0_tok_setup():
        import jax, jax.numpy as jnp
        import numpy as np
        B, C, H, W = (8, 32, 128, 128)
        P = 8
        D = 128
        NH, DH = (8, 64)
        M = 512
        L = 2
        DOUT = 192
        INNER = NH * DH

        def _ln(x, g, b, eps=1e-05):
            mu = x.mean(-1, keepdims=True)
            xc = x - mu
            var = (xc * xc).mean(-1, keepdims=True)
            return xc * jax.lax.rsqrt(var + eps) * g + b

        def _forward(im, conv_w, conv_b, ln1_g, ln1_b, qkv_w, out_w, out_b, ln2_g, ln2_b, ff1_w, ff1_b, ff2_w, ff2_b, lnf_g, lnf_b, head_w, head_b):
            b, c, h, w = im.shape
            hp, wp = (h // P, w // P)
            patches = im.reshape(b, c, hp, P, wp, P)
            x = jnp.einsum('bchpwq,dcpq->bhwd', patches, conv_w)
            x = x.reshape(b, hp * wp, -1) + conv_b
            n = hp * wp
            scale = DH ** (-0.5)
            for i in range(ln1_g.shape[0]):
                y = _ln(x, ln1_g[i], ln1_b[i])
                qkv = y @ qkv_w[i]
                q, k, v = jnp.split(qkv, 3, axis=-1)
                to_heads = lambda t: t.reshape(b, n, NH, DH).transpose(0, 2, 1, 3)
                q, k, v = (to_heads(q), to_heads(k), to_heads(v))
                q = jax.nn.softmax(q, axis=-1) * scale
                k = jax.nn.softmax(k, axis=-2)
                ctx = jnp.einsum('bhnd,bhne->bhde', k, v)
                att = jnp.einsum('bhnd,bhde->bhne', q, ctx)
                att = att.transpose(0, 2, 1, 3).reshape(b, n, INNER)
                x = x + att @ out_w[i] + out_b[i]
                y = _ln(x, ln2_g[i], ln2_b[i])
                hdn = jax.nn.gelu(y @ ff1_w[i] + ff1_b[i], approximate=False)
                x = x + hdn @ ff2_w[i] + ff2_b[i]
            return _ln(x, lnf_g, lnf_b) @ head_w + head_b
        key = jax.random.key(seed)
        ks = iter(jax.random.split(key, 32))
        g = lambda shape, s=0.02: (jax.random.normal(next(ks), shape) * s).astype(jnp.float32)
        inp = {'im': jax.random.normal(next(ks), (B, C, H, W), dtype=jnp.float32), 'conv_w': g((D, C, P, P)), 'conv_b': jnp.zeros((D,), jnp.float32), 'ln1_g': jnp.ones((L, D), jnp.float32), 'ln1_b': jnp.zeros((L, D), jnp.float32), 'qkv_w': g((L, D, 3 * INNER)), 'out_w': g((L, INNER, D)), 'out_b': jnp.zeros((L, D), jnp.float32), 'ln2_g': jnp.ones((L, D), jnp.float32), 'ln2_b': jnp.zeros((L, D), jnp.float32), 'ff1_w': g((L, D, M)), 'ff1_b': jnp.zeros((L, M), jnp.float32), 'ff2_w': g((L, M, D)), 'ff2_b': jnp.zeros((L, D), jnp.float32), 'lnf_g': jnp.ones((D,), jnp.float32), 'lnf_b': jnp.zeros((D,), jnp.float32), 'head_w': g((D, DOUT)), 'head_b': jnp.zeros((DOUT,), jnp.float32)}
        return inp
    _L0_tok_all = _L0_tok_setup()
    _L0_tok_in = {k: v for k, v in _L0_tok_all.items() if k in ('conv_w', 'conv_b', 'ln1_g', 'ln1_b', 'qkv_w', 'out_w', 'out_b', 'ln2_g', 'ln2_b', 'ff1_w', 'ff1_b', 'ff2_w', 'ff2_b', 'lnf_g', 'lnf_b', 'head_w', 'head_b')}
    del _L0_tok_all

    def _L0_attn_setup():
        import jax, jax.numpy as jnp
        import numpy as np
        B, S, D, H = (64, 577, 192, 12)
        DH = D // H
        key = jax.random.key(seed)
        ks = jax.random.split(key, 9)
        sc = 0.02
        return {'x': jax.random.normal(ks[0], (B, S, D), jnp.float32), 'Wq': jax.random.normal(ks[1], (H, D, DH), jnp.float32) * sc, 'bq': jnp.zeros((H, DH), jnp.float32), 'Wk': jax.random.normal(ks[2], (H, D, DH), jnp.float32) * sc, 'bk': jnp.zeros((H, DH), jnp.float32), 'Wv': jax.random.normal(ks[3], (H, D, DH), jnp.float32) * sc, 'bv': jnp.zeros((H, DH), jnp.float32), 'Wo': jax.random.normal(ks[4], (D, D), jnp.float32) * sc, 'bo': jnp.zeros((D,), jnp.float32)}
    _L0_attn_all = _L0_attn_setup()
    _L0_attn_in = {k: v for k, v in _L0_attn_all.items() if k in ('Wq', 'bq', 'Wk', 'bk', 'Wv', 'bv', 'Wo', 'bo')}
    del _L0_attn_all

    def _L0_ffn_setup():
        import jax, jax.numpy as jnp
        import numpy as np
        DIM = 192
        HEADS = 12
        HD = DIM // HEADS
        MLP = 768
        RHD = 128
        RANK = 64
        BS = 2
        RESERVE = 1
        EPS = 1e-05

        def _ln(x, g, b):
            m = jnp.mean(x, axis=-1, keepdims=True)
            v = jnp.var(x, axis=-1, keepdims=True)
            return (x - m) / jnp.sqrt(v + EPS) * g + b

        def _gelu(t):
            return jax.nn.gelu(t, approximate=False)

        def _forward(x, wq, bq, wk, bk, wv, bv, wo, bo, ln1_g, ln1_b, ln2_g, ln2_b, fc1_w, fc1_b, fc2_w, fc2_b, r_ln_g, r_ln_b, r_in_w, r_in_b, r_o1_w, r_o1_b, r_o2_w, r_o2_b, r_o3_w, r_o3_b, lra_down, lra_up):
            B, N, _ = x.shape
            e = _gelu(_ln(x, r_ln_g, r_ln_b) @ r_in_w.T + r_in_b)
            g = jnp.mean(e[:, RESERVE:, :], axis=1, keepdims=True)
            f = jnp.concatenate([e, jnp.broadcast_to(g, e.shape)], axis=-1)
            h1 = _gelu(f @ r_o1_w.T + r_o1_b)
            h2 = _gelu(h1 @ r_o2_w.T + r_o2_b)
            logits = (h2 @ r_o3_w.T + r_o3_b).reshape(B, N, BS, 2)
            hard = jax.nn.one_hot(jnp.argmax(logits, axis=-1), 2, dtype=x.dtype)
            keep = jnp.broadcast_to(jnp.array([0.0, 1.0], dtype=x.dtype), hard[:, :RESERVE].shape)
            hard = hard.at[:, :RESERVE].set(keep)
            hard = jax.lax.stop_gradient(hard)
            bits = hard[..., 1]
            indices = (bits * jnp.array([2.0, 1.0], dtype=x.dtype)).sum(-1).astype(jnp.int32)
            indices = jax.lax.stop_gradient(indices)
            xa = _ln(x, ln1_g, ln1_b)
            q = (xa @ wq.T + bq).reshape(B, N, HEADS, HD).transpose(0, 2, 1, 3)
            k = (xa @ wk.T + bk).reshape(B, N, HEADS, HD).transpose(0, 2, 1, 3)
            v = (xa @ wv.T + bv).reshape(B, N, HEADS, HD).transpose(0, 2, 1, 3)
            s = jax.nn.softmax(jnp.einsum('bhqd,bhkd->bhqk', q, k) / np.float32(np.sqrt(HD)), axis=-1)
            o = jnp.einsum('bhqk,bhkd->bhqd', s, v).transpose(0, 2, 1, 3).reshape(B, N, DIM)
            o = o @ wo.T + bo
            h = x + bits[:, :, 0:1] * o
            xf = _ln(h, ln2_g, ln2_b)
            ff = _gelu(xf @ fc1_w.T + fc1_b) @ fc2_w.T + fc2_b
            out = h + bits[:, :, 1:2] * ff
            down = jnp.einsum('bnd,krd->bknr', out, lra_down)
            up = jnp.einsum('bknr,kdr->bknd', down, lra_up)
            sel = jax.nn.one_hot(indices, 3, dtype=x.dtype)
            out = out + jnp.einsum('bknd,bnk->bnd', up, sel)
            return out
        key = jax.random.key(seed)
        ks = iter(jax.random.split(key, 40))

        def w(shape, std=0.02):
            return (jax.random.normal(next(ks), shape) * std).astype(jnp.float32)
        B, N = (128, 197)
        inp = {'x': jax.random.normal(next(ks), (B, N, DIM), dtype=jnp.float32)}
        inp.update(wq=w((DIM, DIM)), bq=jnp.zeros((DIM,), jnp.float32), wk=w((DIM, DIM)), bk=jnp.zeros((DIM,), jnp.float32), wv=w((DIM, DIM)), bv=jnp.zeros((DIM,), jnp.float32), wo=w((DIM, DIM)), bo=jnp.zeros((DIM,), jnp.float32), ln1_g=jnp.ones((DIM,), jnp.float32), ln1_b=jnp.zeros((DIM,), jnp.float32), ln2_g=jnp.ones((DIM,), jnp.float32), ln2_b=jnp.zeros((DIM,), jnp.float32), fc1_w=w((MLP, DIM)), fc1_b=jnp.zeros((MLP,), jnp.float32), fc2_w=w((DIM, MLP)), fc2_b=jnp.zeros((DIM,), jnp.float32), r_ln_g=jnp.ones((DIM,), jnp.float32), r_ln_b=jnp.zeros((DIM,), jnp.float32), r_in_w=w((RHD, DIM)), r_in_b=jnp.zeros((RHD,), jnp.float32), r_o1_w=w((RHD, 2 * RHD)), r_o1_b=jnp.zeros((RHD,), jnp.float32), r_o2_w=w((RHD // 2, RHD)), r_o2_b=jnp.zeros((RHD // 2,), jnp.float32), r_o3_w=w((2 * BS, RHD // 2), 0.01), r_o3_b=jnp.array([0.0, 5.0, 0.0, 5.0], dtype=jnp.float32), lra_down=w((3, RANK, DIM), 0.01), lra_up=w((3, DIM, RANK), 0.01))
        return inp
    _L0_ffn_all = _L0_ffn_setup()
    _L0_ffn_in = {k: v for k, v in _L0_ffn_all.items() if k in ('wq', 'bq', 'wk', 'bk', 'wv', 'bv', 'wo', 'bo', 'ln1_g', 'ln1_b', 'ln2_g', 'ln2_b', 'fc1_w', 'fc1_b', 'fc2_w', 'fc2_b', 'r_ln_g', 'r_ln_b', 'r_in_w', 'r_in_b', 'r_o1_w', 'r_o1_b', 'r_o2_w', 'r_o2_b', 'r_o3_w', 'r_o3_b', 'lra_down', 'lra_up')}
    del _L0_ffn_all
    return {'x': x, 'L0_tok_conv_w': _L0_tok_in['conv_w'], 'L0_tok_conv_b': _L0_tok_in['conv_b'], 'L0_tok_ln1_g': _L0_tok_in['ln1_g'], 'L0_tok_ln1_b': _L0_tok_in['ln1_b'], 'L0_tok_qkv_w': _L0_tok_in['qkv_w'], 'L0_tok_out_w': _L0_tok_in['out_w'], 'L0_tok_out_b': _L0_tok_in['out_b'], 'L0_tok_ln2_g': _L0_tok_in['ln2_g'], 'L0_tok_ln2_b': _L0_tok_in['ln2_b'], 'L0_tok_ff1_w': _L0_tok_in['ff1_w'], 'L0_tok_ff1_b': _L0_tok_in['ff1_b'], 'L0_tok_ff2_w': _L0_tok_in['ff2_w'], 'L0_tok_ff2_b': _L0_tok_in['ff2_b'], 'L0_tok_lnf_g': _L0_tok_in['lnf_g'], 'L0_tok_lnf_b': _L0_tok_in['lnf_b'], 'L0_tok_head_w': _L0_tok_in['head_w'], 'L0_tok_head_b': _L0_tok_in['head_b'], 'L0_attn_Wq': _L0_attn_in['Wq'], 'L0_attn_bq': _L0_attn_in['bq'], 'L0_attn_Wk': _L0_attn_in['Wk'], 'L0_attn_bk': _L0_attn_in['bk'], 'L0_attn_Wv': _L0_attn_in['Wv'], 'L0_attn_bv': _L0_attn_in['bv'], 'L0_attn_Wo': _L0_attn_in['Wo'], 'L0_attn_bo': _L0_attn_in['bo'], 'L0_ffn_wq': _L0_ffn_in['wq'], 'L0_ffn_bq': _L0_ffn_in['bq'], 'L0_ffn_wk': _L0_ffn_in['wk'], 'L0_ffn_bk': _L0_ffn_in['bk'], 'L0_ffn_wv': _L0_ffn_in['wv'], 'L0_ffn_bv': _L0_ffn_in['bv'], 'L0_ffn_wo': _L0_ffn_in['wo'], 'L0_ffn_bo': _L0_ffn_in['bo'], 'L0_ffn_ln1_g': _L0_ffn_in['ln1_g'], 'L0_ffn_ln1_b': _L0_ffn_in['ln1_b'], 'L0_ffn_ln2_g': _L0_ffn_in['ln2_g'], 'L0_ffn_ln2_b': _L0_ffn_in['ln2_b'], 'L0_ffn_fc1_w': _L0_ffn_in['fc1_w'], 'L0_ffn_fc1_b': _L0_ffn_in['fc1_b'], 'L0_ffn_fc2_w': _L0_ffn_in['fc2_w'], 'L0_ffn_fc2_b': _L0_ffn_in['fc2_b'], 'L0_ffn_r_ln_g': _L0_ffn_in['r_ln_g'], 'L0_ffn_r_ln_b': _L0_ffn_in['r_ln_b'], 'L0_ffn_r_in_w': _L0_ffn_in['r_in_w'], 'L0_ffn_r_in_b': _L0_ffn_in['r_in_b'], 'L0_ffn_r_o1_w': _L0_ffn_in['r_o1_w'], 'L0_ffn_r_o1_b': _L0_ffn_in['r_o1_b'], 'L0_ffn_r_o2_w': _L0_ffn_in['r_o2_w'], 'L0_ffn_r_o2_b': _L0_ffn_in['r_o2_b'], 'L0_ffn_r_o3_w': _L0_ffn_in['r_o3_w'], 'L0_ffn_r_o3_b': _L0_ffn_in['r_o3_b'], 'L0_ffn_lra_down': _L0_ffn_in['lra_down'], 'L0_ffn_lra_up': _L0_ffn_in['lra_up']}

def reference(x, L0_tok_conv_w, L0_tok_conv_b, L0_tok_ln1_g, L0_tok_ln1_b, L0_tok_qkv_w, L0_tok_out_w, L0_tok_out_b, L0_tok_ln2_g, L0_tok_ln2_b, L0_tok_ff1_w, L0_tok_ff1_b, L0_tok_ff2_w, L0_tok_ff2_b, L0_tok_lnf_g, L0_tok_lnf_b, L0_tok_head_w, L0_tok_head_b, L0_attn_Wq, L0_attn_bq, L0_attn_Wk, L0_attn_bk, L0_attn_Wv, L0_attn_bv, L0_attn_Wo, L0_attn_bo, L0_ffn_wq, L0_ffn_bq, L0_ffn_wk, L0_ffn_bk, L0_ffn_wv, L0_ffn_bv, L0_ffn_wo, L0_ffn_bo, L0_ffn_ln1_g, L0_ffn_ln1_b, L0_ffn_ln2_g, L0_ffn_ln2_b, L0_ffn_fc1_w, L0_ffn_fc1_b, L0_ffn_fc2_w, L0_ffn_fc2_b, L0_ffn_r_ln_g, L0_ffn_r_ln_b, L0_ffn_r_in_w, L0_ffn_r_in_b, L0_ffn_r_o1_w, L0_ffn_r_o1_b, L0_ffn_r_o2_w, L0_ffn_r_o2_b, L0_ffn_r_o3_w, L0_ffn_r_o3_b, L0_ffn_lra_down, L0_ffn_lra_up):
    import jax
    import jax.numpy as jnp

    def _L0_tok_ref(im, conv_w, conv_b, ln1_g, ln1_b, qkv_w, out_w, out_b, ln2_g, ln2_b, ff1_w, ff1_b, ff2_w, ff2_b, lnf_g, lnf_b, head_w, head_b):
        import jax, jax.numpy as jnp
        import numpy as np
        B, C, H, W = (8, 32, 128, 128)
        P = 8
        D = 128
        NH, DH = (8, 64)
        M = 512
        L = 2
        DOUT = 192
        INNER = NH * DH

        def _ln(x, g, b, eps=1e-05):
            mu = x.mean(-1, keepdims=True)
            xc = x - mu
            var = (xc * xc).mean(-1, keepdims=True)
            return xc * jax.lax.rsqrt(var + eps) * g + b

        def _forward(im, conv_w, conv_b, ln1_g, ln1_b, qkv_w, out_w, out_b, ln2_g, ln2_b, ff1_w, ff1_b, ff2_w, ff2_b, lnf_g, lnf_b, head_w, head_b):
            b, c, h, w = im.shape
            hp, wp = (h // P, w // P)
            patches = im.reshape(b, c, hp, P, wp, P)
            x = jnp.einsum('bchpwq,dcpq->bhwd', patches, conv_w)
            x = x.reshape(b, hp * wp, -1) + conv_b
            n = hp * wp
            scale = DH ** (-0.5)
            for i in range(ln1_g.shape[0]):
                y = _ln(x, ln1_g[i], ln1_b[i])
                qkv = y @ qkv_w[i]
                q, k, v = jnp.split(qkv, 3, axis=-1)
                to_heads = lambda t: t.reshape(b, n, NH, DH).transpose(0, 2, 1, 3)
                q, k, v = (to_heads(q), to_heads(k), to_heads(v))
                q = jax.nn.softmax(q, axis=-1) * scale
                k = jax.nn.softmax(k, axis=-2)
                ctx = jnp.einsum('bhnd,bhne->bhde', k, v)
                att = jnp.einsum('bhnd,bhde->bhne', q, ctx)
                att = att.transpose(0, 2, 1, 3).reshape(b, n, INNER)
                x = x + att @ out_w[i] + out_b[i]
                y = _ln(x, ln2_g[i], ln2_b[i])
                hdn = jax.nn.gelu(y @ ff1_w[i] + ff1_b[i], approximate=False)
                x = x + hdn @ ff2_w[i] + ff2_b[i]
            return _ln(x, lnf_g, lnf_b) @ head_w + head_b
        return _forward(im, conv_w, conv_b, ln1_g, ln1_b, qkv_w, out_w, out_b, ln2_g, ln2_b, ff1_w, ff1_b, ff2_w, ff2_b, lnf_g, lnf_b, head_w, head_b)

    def _L0_attn_ref(x, Wq, bq, Wk, bk, Wv, bv, Wo, bo):
        import jax, jax.numpy as jnp
        import numpy as np
        B, S, D, H = (64, 577, 192, 12)
        DH = D // H
        q = jnp.einsum('bsd,hde->bhse', x, Wq) + bq[None, :, None, :]
        k = jnp.einsum('bsd,hde->bhse', x, Wk) + bk[None, :, None, :]
        v = jnp.einsum('bsd,hde->bhse', x, Wv) + bv[None, :, None, :]
        scale = np.float32(1.0 / np.sqrt(DH))
        scores = jnp.einsum('bhqe,bhke->bhqk', q, k) * scale
        probs = jax.nn.softmax(scores, axis=2)
        ctx = jnp.einsum('bhqk,bhke->bhqe', probs, v)
        ctx = ctx.transpose(0, 2, 1, 3).reshape(x.shape[0], x.shape[1], H * DH)
        return ctx @ Wo + bo

    def _L0_ffn_ref(x, wq, bq, wk, bk, wv, bv, wo, bo, ln1_g, ln1_b, ln2_g, ln2_b, fc1_w, fc1_b, fc2_w, fc2_b, r_ln_g, r_ln_b, r_in_w, r_in_b, r_o1_w, r_o1_b, r_o2_w, r_o2_b, r_o3_w, r_o3_b, lra_down, lra_up):
        import jax, jax.numpy as jnp
        import numpy as np
        DIM = 192
        HEADS = 12
        HD = DIM // HEADS
        MLP = 768
        RHD = 128
        RANK = 64
        BS = 2
        RESERVE = 1
        EPS = 1e-05

        def _ln(x, g, b):
            m = jnp.mean(x, axis=-1, keepdims=True)
            v = jnp.var(x, axis=-1, keepdims=True)
            return (x - m) / jnp.sqrt(v + EPS) * g + b

        def _gelu(t):
            return jax.nn.gelu(t, approximate=False)

        def _forward(x, wq, bq, wk, bk, wv, bv, wo, bo, ln1_g, ln1_b, ln2_g, ln2_b, fc1_w, fc1_b, fc2_w, fc2_b, r_ln_g, r_ln_b, r_in_w, r_in_b, r_o1_w, r_o1_b, r_o2_w, r_o2_b, r_o3_w, r_o3_b, lra_down, lra_up):
            B, N, _ = x.shape
            e = _gelu(_ln(x, r_ln_g, r_ln_b) @ r_in_w.T + r_in_b)
            g = jnp.mean(e[:, RESERVE:, :], axis=1, keepdims=True)
            f = jnp.concatenate([e, jnp.broadcast_to(g, e.shape)], axis=-1)
            h1 = _gelu(f @ r_o1_w.T + r_o1_b)
            h2 = _gelu(h1 @ r_o2_w.T + r_o2_b)
            logits = (h2 @ r_o3_w.T + r_o3_b).reshape(B, N, BS, 2)
            hard = jax.nn.one_hot(jnp.argmax(logits, axis=-1), 2, dtype=x.dtype)
            keep = jnp.broadcast_to(jnp.array([0.0, 1.0], dtype=x.dtype), hard[:, :RESERVE].shape)
            hard = hard.at[:, :RESERVE].set(keep)
            hard = jax.lax.stop_gradient(hard)
            bits = hard[..., 1]
            indices = (bits * jnp.array([2.0, 1.0], dtype=x.dtype)).sum(-1).astype(jnp.int32)
            indices = jax.lax.stop_gradient(indices)
            xa = _ln(x, ln1_g, ln1_b)
            q = (xa @ wq.T + bq).reshape(B, N, HEADS, HD).transpose(0, 2, 1, 3)
            k = (xa @ wk.T + bk).reshape(B, N, HEADS, HD).transpose(0, 2, 1, 3)
            v = (xa @ wv.T + bv).reshape(B, N, HEADS, HD).transpose(0, 2, 1, 3)
            s = jax.nn.softmax(jnp.einsum('bhqd,bhkd->bhqk', q, k) / np.float32(np.sqrt(HD)), axis=-1)
            o = jnp.einsum('bhqk,bhkd->bhqd', s, v).transpose(0, 2, 1, 3).reshape(B, N, DIM)
            o = o @ wo.T + bo
            h = x + bits[:, :, 0:1] * o
            xf = _ln(h, ln2_g, ln2_b)
            ff = _gelu(xf @ fc1_w.T + fc1_b) @ fc2_w.T + fc2_b
            out = h + bits[:, :, 1:2] * ff
            down = jnp.einsum('bnd,krd->bknr', out, lra_down)
            up = jnp.einsum('bknr,kdr->bknd', down, lra_up)
            sel = jax.nn.one_hot(indices, 3, dtype=x.dtype)
            out = out + jnp.einsum('bknd,bnk->bnd', up, sel)
            return out
        return _forward(x, wq, bq, wk, bk, wv, bv, wo, bo, ln1_g, ln1_b, ln2_g, ln2_b, fc1_w, fc1_b, fc2_w, fc2_b, r_ln_g, r_ln_b, r_in_w, r_in_b, r_o1_w, r_o1_b, r_o2_w, r_o2_b, r_o3_w, r_o3_b, lra_down, lra_up)
    h = _L0_tok_ref(x, L0_tok_conv_w, L0_tok_conv_b, L0_tok_ln1_g, L0_tok_ln1_b, L0_tok_qkv_w, L0_tok_out_w, L0_tok_out_b, L0_tok_ln2_g, L0_tok_ln2_b, L0_tok_ff1_w, L0_tok_ff1_b, L0_tok_ff2_w, L0_tok_ff2_b, L0_tok_lnf_g, L0_tok_lnf_b, L0_tok_head_w, L0_tok_head_b)
    h = h + _L0_attn_ref(_layernorm(h, axis=-1), L0_attn_Wq, L0_attn_bq, L0_attn_Wk, L0_attn_bk, L0_attn_Wv, L0_attn_bv, L0_attn_Wo, L0_attn_bo)
    h = h + _L0_ffn_ref(_layernorm(h, axis=-1), L0_ffn_wq, L0_ffn_bq, L0_ffn_wk, L0_ffn_bk, L0_ffn_wv, L0_ffn_bv, L0_ffn_wo, L0_ffn_bo, L0_ffn_ln1_g, L0_ffn_ln1_b, L0_ffn_ln2_g, L0_ffn_ln2_b, L0_ffn_fc1_w, L0_ffn_fc1_b, L0_ffn_fc2_w, L0_ffn_fc2_b, L0_ffn_r_ln_g, L0_ffn_r_ln_b, L0_ffn_r_in_w, L0_ffn_r_in_b, L0_ffn_r_o1_w, L0_ffn_r_o1_b, L0_ffn_r_o2_w, L0_ffn_r_o2_b, L0_ffn_r_o3_w, L0_ffn_r_o3_b, L0_ffn_lra_down, L0_ffn_lra_up)
    return h

_drawn_inputs = setup_inputs


def setup_inputs(seed=0):
    import zlib

    import numpy as np

    out = dict(_drawn_inputs(seed))
    spreads = {'L0_tok_conv_b': (0.0, 0.1),
     'L0_tok_ln1_g': (1.0, 0.6),
     'L0_tok_ln1_b': (0.0, 0.8),
     'L0_tok_out_b': (0.0, 0.1),
     'L0_tok_ln2_g': (1.0, 0.6),
     'L0_tok_ln2_b': (0.0, 0.8),
     'L0_tok_ff1_b': (0.0, 0.3),
     'L0_tok_ff2_b': (0.0, 0.1),
     'L0_tok_lnf_g': (1.0, 0.2),
     'L0_tok_lnf_b': (0.0, 0.1),
     'L0_tok_head_b': (0.0, 0.1),
     'L0_attn_bq': (0.0, 0.8),
     'L0_attn_bk': (0.0, 0.8),
     'L0_attn_bv': (0.0, 0.1),
     'L0_attn_bo': (0.0, 0.1),
     'L0_ffn_bq': (0.0, 0.8),
     'L0_ffn_bk': (0.0, 0.8),
     'L0_ffn_bv': (0.0, 0.359),
     'L0_ffn_bo': (0.0, 0.1),
     'L0_ffn_ln1_g': (1.0, 0.6),
     'L0_ffn_ln1_b': (0.0, 0.8),
     'L0_ffn_ln2_g': (1.0, 0.6),
     'L0_ffn_ln2_b': (0.0, 0.8),
     'L0_ffn_fc1_b': (0.0, 0.31),
     'L0_ffn_fc2_b': (0.0, 0.1),
     'L0_ffn_r_ln_g': (1.0, 0.2),
     'L0_ffn_r_ln_b': (0.0, 0.1),
     'L0_ffn_r_in_b': (0.0, 0.1),
     'L0_ffn_r_o1_b': (0.0, 0.1),
     'L0_ffn_r_o2_b': (0.0, 0.1)}
    factors = {'L0_tok_qkv_w': 8.0,
     'L0_tok_out_w': 8.0,
     'L0_attn_Wq': 8.0,
     'L0_attn_Wk': 8.0,
     'L0_ffn_wq': 8.0,
     'L0_ffn_wk': 8.0}
    for name, (base, spread) in spreads.items():
        noise = np.random.default_rng([zlib.crc32(name.encode()), seed]).standard_normal(out[name].shape)
        drawn = base * np.exp(spread * noise) if base else spread * noise
        out[name] = jnp.asarray(drawn.astype(out[name].dtype))
    for name, factor in factors.items():
        out[name] = (out[name] * factor).astype(out[name].dtype)
    return out
```

```python
import numpy as np
import concourse.bass as bass
from concourse import mybir
from contextlib import ExitStack

B, C_IN, IMG, PATCH = 4, 32, 128, 8
N = (IMG // PATCH) ** 2
P = 128
TPB = N // P
NT = B * TPB
D = 128
L, NH, DH, M = 2, 8, 64, 512
INNER = NH * DH
PAIRS = INNER // P
KC = C_IN * PATCH * PATCH // P
KG = 4
E = 192
EH = E // 2
AH, AD = 12, 16
G = 3
HID = 768
HM = HID // P
RH, RL, NA = 128, 64, 3
EPS = 1e-5
MAXROW = 16

COL = {}
_at = 0
for _name, _n in [("conv_b", 1), ("lnf_g", 1), ("lnf_b", 1), ("bq1", G), ("bk1", G), ("r_g", 2), ("r_b", 2),
                  ("g1", 2), ("b1", 2), ("g2", 2), ("b2", 2), ("r_in_b", 1), ("o1_b", 1), ("o2_b", 1),
                  ("bq2", G), ("bk2", G), ("fc1_b", HM)]:
    COL[_name] = (_at, _n)
    _at += _n
NCOL = _at
LCOL = {"ln1_g": (0, 1), "ln1_b": (1, 1), "ln2_g": (2, 1), "ln2_b": (3, 1), "ff1_b": (4, PAIRS)}
NLCOL = 4 + PAIRS
ROW = {}
_at = 0
for _name, _n in [("head_b", E), ("bv1", E), ("bo1", E), ("bv2", E), ("bo2", E), ("fc2_b", E), ("o3_b", 4)]:
    ROW[_name] = (_at, _n)
    _at += _n
NROW = _at

PRE = [("conv", h) for h in range(2)] + [("embed", b) for b in range(B)]
BODY = [(s, b) for s in ("ln1T", "k", "q", "v", "kT", "ctx", "qT", "ctxw", "att", "ln2T", "ff1", "ff2")
        for b in range(B)]


def tail_order():
    o = [(s, b) for s in ("lnfT", "head", "a1.xT", "a1.q", "a1.k", "a1.v") for b in range(B)]
    for b in range(B + 1):
        for u in range(6):
            if b < B:
                o.append(("a1.s", 6 * b + u))
            if u == 1 and b > 0:
                o.append(("a1.pv", b - 1))
            if b == B and u == 1:
                break
    o += [(s, b) for s in ("a1.o", "zT", "r1") for b in range(B)]
    o += [("rg", 0)]
    o += [(s, b) for s in ("a2.q", "r2", "a2.k", "r3", "a2.v", "r4") for b in range(B)]
    for b in range(-1, B):
        for u in range(6):
            if b + 1 < B:
                o.append(("a2.m", 6 * (b + 1) + u))
            if b >= 0:
                o.append(("a2.s", 6 * b + u))
            if u == 2 and b > 0:
                o.append(("a2.pv", b - 1))
        if b + 1 < B:
            o.append(("a2.mT", b + 1))
    o.append(("a2.pv", B - 1))
    o += [(s, b) for s in ("a2.cT", "a2.nT", "a2.o", "hT") for b in range(B)]
    o += [("fc1", x) for x in range(2 * B)]
    o += [(s, b) for s in ("fc2", "outT", "down", "selT", "up") for b in range(B)]
    return o


TAIL = tail_order()
NSLOT = 4


def build(nc, im, cw, wl, lcols, lrows, cols, rows, ident_d, w_head, w_a1, wo_a1, w_a2, wo_a2,
          w_r, w_ro, w_fc1, w_fc2, w_down, w_up, out):
    f32 = mybir.dt.float32
    ALU = mybir.AluOpType
    ACT = mybir.ActivationFunctionType
    X = mybir.AxisListType.X

    ctx = ExitStack()
    with ctx:
        def sb(name, n):
            return ctx.enter_context(nc.sbuf_tensor(name, [P, n], f32))

        names = sorted({n for n, _ in PRE + BODY + TAIL})
        full = {n: ctx.enter_context(nc.semaphore("full_" + n.replace(".", "_"))) for n in names}
        done = {n: ctx.enter_context(nc.semaphore("done_" + n.replace(".", "_"))) for n in names}

        def sem(name):
            return ctx.enter_context(nc.semaphore(name))

        big = sb("big", 16384)
        mid = sb("mid", 12288)
        image = big[:, :].rearrange("p (h k t) -> p h k t", h=2, k=KC)
        ekT = big[:, 0:4096].rearrange("p (b a n) -> p b a n", b=B, a=PAIRS)
        hidT = ekT
        vv = big[:, 4096:8192].rearrange("p (t f) -> p t f", t=NT)
        qs = big[:, 8192:12288].rearrange("p (t h d) -> p t h d", t=NT, h=NH)
        qT = big[:, 12288:16384].rearrange("p (b a n) -> p b a n", b=B, a=PAIRS)
        conv_w = mid[:, 0:KC * D].rearrange("p (k d) -> p k d", k=KC)
        embT = mid[:, 8192:9216]
        ek = mid[:, 0:4096].rearrange("p (t f) -> p t f", t=NT)
        ctxT = mid[:, 4096:6144].rearrange("p (b a d) -> p b a d", b=B, a=PAIRS)
        ctxw = mid[:, 6144:8192].rearrange("p (b a d) -> p b a d", b=B, a=PAIRS)
        yT = mid[:, 9216:10240].rearrange("p (b n) -> p b n", b=B)
        probs = big[:, 0:12288].rearrange("p (z u r x n) -> p z u r x n", z=2, u=6, r=2, x=2)
        xaT = big[0:EH, 0:2048].rearrange("p (b c n) -> p b c n", b=B, c=2)
        eT = big[:, 6144:7168].rearrange("p (b n) -> p b n", b=B)
        h1T = big[:, 7168:8192].rearrange("p (b n) -> p b n", b=B)
        h2T = big[0:RL, 8192:9216].rearrange("p (b n) -> p b n", b=B)
        hid2T = big[:, 0:6144].rearrange("p (b m n) -> p b m n", b=B, m=HM)
        xT = big[0:EH, 12288:14336].rearrange("p (b c n) -> p b c n", b=B, c=2)
        catt = big[:, 14336:15872].rearrange("p (t f) -> p t f", t=NT)
        aqT = mid[:, 0:3072].rearrange("p (b g n) -> p b g n", b=B, g=G)
        akT = mid[:, 3072:6144].rearrange("p (b g n) -> p b g n", b=B, g=G)
        av = mid[:, 6144:9216].rearrange("p (t g j e) -> p t g j e", t=NT, g=G, j=4)
        actxT = mid[:, 9216:12288].rearrange("p (b g n) -> p b g n", b=B, g=G)
        negmax = mid[:, 9216:12288].rearrange("p (b t g j e) -> p b t g j e", b=B, t=TPB, g=G, j=4)
        xs = sb("xs", NT * D)[:, :].rearrange("p (t d) -> p t d", t=NT)
        nrm = sb("nrm", NT * E)[:, :].rearrange("p (t d) -> p t d", t=NT)
        hs = sb("hs", NT * E)[:, :].rearrange("p (t d) -> p t d", t=NT)
        zs = sb("zs", NT * E)[:, :].rearrange("p (t d) -> p t d", t=NT)
        os_ = sb("os", NT * E)[:, :].rearrange("p (t d) -> p t d", t=NT)
        lw = sb("lw", 3 * INNER + INNER + M + M)
        w_qkv = lw[:, 0:1536]
        w_out = lw[:, 1536:2048].rearrange("p (a d) -> p a d", a=PAIRS)
        w_ff1 = lw[:, 2048:2560]
        w_ff2 = lw[:, 2560:3072].rearrange("p (m d) -> p m d", m=PAIRS)
        lc = sb("lc", NLCOL)
        lr = sb("lr", 2 * D)
        colp = sb("colp", NCOL)
        rowp = sb("rowp", NROW)
        ident = sb("identity", P)
        headw = sb("headw", E)
        a_w = [sb(f"a{n}_w", 2 * (2 * G * P + E)) for n in (1, 2)]
        a_wqkv = [w[0:EH, :].rearrange("p (c f) -> p c f", c=2) for w in a_w]
        a1_wo = sb("a1_wo", G * E)[:, :].rearrange("p (g f) -> p g f", g=G)
        a2_wo = sb("a2_wo", 2 * E)[0:EH, :].rearrange("p (c f) -> p c f", c=2)
        rinw = sb("rinw", 2 * RH)[0:EH, :].rearrange("p (c f) -> p c f", c=2)
        row_ = sb("row", 2 * RH + RL + 4)
        fc1w = sb("fc1w", 2 * HID)[0:EH, :].rearrange("p (c f) -> p c f", c=2)
        fc2w = sb("fc2w", HM * E)[:, :].rearrange("p (m f) -> p m f", m=HM)
        downw = sb("downw", 2 * E)[0:EH, :].rearrange("p (c f) -> p c f", c=2)
        upw = sb("upw", 2 * E)[0:EH, :].rearrange("p (c f) -> p c f", c=2)
        stats = sb("stats", NT * 6)[:, :].rearrange("p (t s) -> p t s", t=NT)
        moments = sb("moments", NT * 2)[:, :].rearrange("p (t s) -> p t s", t=NT)
        vareps = sb("vareps", NT)
        rstd = sb("rstd", NT)
        minushalf = sb("minushalf", TPB)
        epsilon = sb("epsilon", TPB)
        pause = sb("pause", 1)
        nkmax = sb("nkmax", B * PAIRS)[:, :].rearrange("p (b a) -> p b a", b=B)
        ksum = sb("ksum", B * PAIRS)[:, :].rearrange("p (b a) -> p b a", b=B)
        krec = sb("krec", B * PAIRS)[:, :].rearrange("p (b a) -> p b a", b=B)
        qmax = sb("qmax", NT * NH)[:, :].rearrange("p (t h) -> p t h", t=NT)
        qsum = sb("qsum", NT * NH)[:, :].rearrange("p (t h) -> p t h", t=NT)
        qrec = sb("qrec", NT * NH)[:, :].rearrange("p (t h) -> p t h", t=NT)
        sneg = sb("sneg", B * 24)[:, :].rearrange("p (b u x) -> p b u x", b=B, u=6)
        smax = sb("smax", B * 24)[:, :].rearrange("p (b u x) -> p b u x", b=B, u=6)
        ssum = sb("ssum", B * 24)[:, :].rearrange("p (b u x) -> p b u x", b=B, u=6)
        srec = sb("srec", B * 24)[:, :].rearrange("p (b u x) -> p b u x", b=B, u=6)
        crec = sb("crec", NT * AH)[:, :].rearrange("p (t g j) -> p t g j", t=NT, g=G)
        emean = sb("emean", B)
        h1bias = sb("h1bias", B)
        logits = sb("logits", NT * 4)[:, :].rearrange("p (t k c) -> p t k c", t=NT, k=2)
        bits = sb("bits", NT * 2)[:, :].rearrange("p (t k) -> p t k", t=NT)
        nbits = sb("nbits", NT * 2)[:, :].rearrange("p (t k) -> p t k", t=NT)
        sel = sb("sel", NT * NA)[:, :].rearrange("p (t k) -> p t k", t=NT)

        psum = ctx.enter_context(nc.psum_tensor("psum", [P, NSLOT * 1024], f32))

        def col(name, k=0, n=P):
            return colp[0:n, COL[name][0] + k:COL[name][0] + k + 1]

        def cols_of(name):
            return colp[:, COL[name][0]:COL[name][0] + COL[name][1]]

        def lcol(name, k=0):
            return lc[:, LCOL[name][0] + k:LCOL[name][0] + k + 1]

        def row(name, *shape):
            r = rowp[:, ROW[name][0]:ROW[name][0] + ROW[name][1]]
            return r.unsqueeze(1).broadcast_to([P, TPB, ROW[name][1]])

        def tiles(b):
            return slice(TPB * b, TPB * (b + 1))

        place, before = {}, {}
        for seq, start in ((PRE, 0), (BODY, len(PRE)), (TAIL, len(PRE) + len(BODY))):
            for k, unit in enumerate(seq):
                place[unit] = (start + k) % NSLOT
                if k >= NSLOT:
                    before[unit] = seq[k - NSLOT]

        def slot(name, k):
            s = place[(name, k)]
            return psum[:, 1024 * s:1024 * (s + 1)]

        def take(pe, name, k, layer=None):
            if (name, k) in before:
                who, n = before[(name, k)]
                pe.wait_ge(done[who], n + 1 if layer is None else layer * B + (n + 1))
            return slot(name, k)

        image_in = [[sem(f"image_in{h}{k}") for k in range(KC // KG)] for h in range(2)]
        conv_w_in = [sem(f"conv_w_in{k}") for k in range(KC // KG)]
        ident_in, params_in, rows_in = sem("ident_in"), sem("params_in"), sem("rows_in")
        qkv_in, out_in, ff1_in, ff2_in, lc_in = (sem(n) for n in ("qkv_in", "out_in", "ff1_in", "ff2_in", "lc_in"))
        head_in, a1_in, a2_in, r_in, fc1_in, fc2_in, ad_in = (
            sem(n) for n in ("head_in", "a1_in", "a2_in", "r_in", "fc1_in", "fc2_in", "ad_in"))
        half_set, ctxT_zeroed, av_zeroed = sem("half_set"), sem("ctxT_zeroed"), sem("av_zeroed")
        ln_stats, ln_moments, ln_eps, ln_rstd, normed = (
            sem(n) for n in ("ln_stats", "ln_moments", "ln_eps", "ln_rstd", "normed"))
        attbias_added, ffbias_added = sem("attbias_added"), sem("ffbias_added")
        nkmax_set, ksum_inv = sem("nkmax_set"), sem("ksum_inv")
        qmax_set, qexp_set, qsum_set, qrec_set, qs_set = (
            sem(n) for n in ("qmax_set", "qexp_set", "qsum_set", "qrec_set", "qs_set"))
        sneg_set, smax_set, srec_set, av_set = sem("sneg_set"), sem("smax_set"), sem("srec_set"), sem("av_set")
        hbias_added, xnormed = sem("hbias_added"), sem("xnormed")
        esum_set, emean_set, logits_set, bits_set, sel_set, nb_set = (
            sem(n) for n in ("esum_set", "emean_set", "logits_set", "bits_set", "sel_set", "nb_set"))
        bits_cmp = sem("bits_cmp")
        negmax_zeroed, ones_set, crec_set = sem("negmax_zeroed"), sem("ones_set"), sem("crec_set")
        dve_tmp = sem("dve_tmp")
        xa_set = sem("xa_set")
        hout_set, result_set, stored = sem("hout_set"), sem("result_set"), sem("stored")

        block = ctx.enter_context(nc.Block())

        @block.sync
        def _(sp):
            for h in range(2):
                for k in range(KC // KG):
                    if h == 0:
                        sp.dma_start(conv_w[:, KG * k:KG * (k + 1), :], cw[k]).then_inc(conv_w_in[k], 16)
                    sp.dma_start(image[:, h, KG * k:KG * (k + 1), :], im[h, k]).then_inc(image_in[h][k], 16)
            sp.dma_start(w_qkv, wl[0, :, 0:1536]).then_inc(qkv_in, 16)
            sp.dma_start(lw[:, 1536:2048], wl[0, :, 1536:2048]).then_inc(out_in, 16)
            sp.dma_start(w_ff1, wl[0, :, 2048:2560]).then_inc(ff1_in, 16)
            sp.dma_start(lw[:, 2560:3072], wl[0, :, 2560:3072]).then_inc(ff2_in, 16)
            sp.dma_start(headw[:, :], w_head).then_inc(head_in, 16)
            sp.dma_start(a_wqkv[0], w_a1).then_inc(a1_in, 16)
            sp.dma_start(a1_wo, wo_a1).then_inc(a1_in, 16)
            sp.dma_start(rinw, w_r).then_inc(r_in, 16)
            sp.dma_start(row_[:, :], w_ro).then_inc(r_in, 16)
            sp.dma_start(a_wqkv[1], w_a2).then_inc(a2_in, 16)
            sp.dma_start(a2_wo, wo_a2).then_inc(a2_in, 16)
            sp.dma_start(fc1w, w_fc1).then_inc(fc1_in, 16)
            sp.dma_start(fc2w, w_fc2).then_inc(fc2_in, 16)
            sp.dma_start(downw, w_down).then_inc(ad_in, 16)
            sp.dma_start(upw, w_up).then_inc(ad_in, 16)
            with sp.Fori(0, L - 1) as i:
                sp.wait_ge(full["v"], i * B + B)
                sp.dma_start(w_qkv, wl[i + 1, :, 0:1536]).then_inc(qkv_in, 16)
                sp.wait_ge(full["ctxw"], i * B + B)
                sp.wait_ge(attbias_added, i * B + B)
                sp.dma_start(lw[:, 1536:2048], wl[i + 1, :, 1536:2048]).then_inc(out_in, 16)
                sp.dma_start(lr[:, 0:D], lrows[i + 1, 0:D].partition_broadcast(P)).then_inc(out_in, 16)
                sp.wait_ge(done["ff1"], i * B + B)
                sp.dma_start(lc[:, :], lcols[i + 1]).then_inc(lc_in, 16)
                sp.dma_start(w_ff1, wl[i + 1, :, 2048:2560]).then_inc(ff1_in, 16)
                sp.wait_ge(full["ff2"], i * B + B)
                sp.wait_ge(ffbias_added, i * B + B)
                sp.dma_start(lw[:, 2560:3072], wl[i + 1, :, 2560:3072]).then_inc(ff2_in, 16)
                sp.dma_start(lr[:, D:2 * D], lrows[i + 1, D:2 * D].partition_broadcast(P)).then_inc(ff2_in, 16)
            for b in range(B):
                sp.wait_ge(result_set, b + 1)
                sp.dma_start(out[b], os_[:, tiles(b), :]).then_inc(stored, 16)
            sp.wait_ge(stored, 16 * B)

        @block.gpsimd
        def _(pool):
            nc.gpsimd.memset(epsilon[:, :], EPS)
            nc.gpsimd.memset(minushalf[:, :], -0.5).then_inc(half_set, 1)
            pool.wait_ge(half_set, 1)

            def inverse_std(k):
                b = k % B
                pool.wait_ge(ln_moments, k + 1)
                nc.gpsimd.tensor_tensor(vareps[:, tiles(b)], moments[:, tiles(b), 1], epsilon[:, :],
                                        ALU.add).then_inc(ln_eps, 1)
                pool.wait_ge(ln_eps, k + 1)
                nc.gpsimd.tensor_tensor(rstd[:, tiles(b)], vareps[:, tiles(b)], minushalf[:, :],
                                        ALU.pow).then_inc(ln_rstd, 1)

            for b in range(B):
                inverse_std(b)
            pool.wait_ge(full["conv"], 2)
            nc.gpsimd.memset(mid[:, 4096:6144], 0.0).then_inc(ctxT_zeroed, 1)
            pool.wait_ge(rows_in, 48)
            with pool.Fori(0, L) as i:
                pool.wait_ge(out_in, i * 32 + 16)
                for b in range(B):
                    pool.wait_ge(normed, i * (2 * B) + b + 1)
                    nc.gpsimd.tensor_tensor(xs[:, tiles(b), :], xs[:, tiles(b), :],
                                            lr[:, 0:D].unsqueeze(1).broadcast_to([P, TPB, D]),
                                            ALU.add).then_inc(attbias_added, 1)
                for b in range(B):
                    pool.wait_ge(qrec_set, i * B + b + 1)
                    nc.gpsimd.tensor_tensor(qs[:, tiles(b), :, :], qs[:, tiles(b), :, :],
                                            qrec[:, tiles(b), :].unsqueeze(3).broadcast_to([P, TPB, NH, DH]),
                                            ALU.mult).then_inc(qs_set, 1)
                for b in range(B):
                    pool.wait_ge(ln_moments, i * (2 * B) + B + b + 1)
                    nc.gpsimd.tensor_tensor(vareps[:, tiles(b)], moments[:, tiles(b), 1], epsilon[:, :],
                                            ALU.add).then_inc(ln_eps, 1)
                    pool.wait_ge(ln_eps, i * (2 * B) + B + b + 1)
                    nc.gpsimd.tensor_tensor(rstd[:, tiles(b)], vareps[:, tiles(b)], minushalf[:, :],
                                            ALU.pow).then_inc(ln_rstd, 1)
                for b in range(B):
                    pool.wait_ge(normed, i * (2 * B) + B + b + 1)
                    if b == 0:
                        pool.wait_ge(ff2_in, i * 32 + 16)
                    nc.gpsimd.tensor_tensor(xs[:, tiles(b), :], xs[:, tiles(b), :],
                                            lr[:, D:2 * D].unsqueeze(1).broadcast_to([P, TPB, D]),
                                            ALU.add).then_inc(ffbias_added, 1)
                for b in range(B):
                    pool.wait_ge(ln_moments, i * (2 * B) + 2 * B + b + 1)
                    nc.gpsimd.tensor_tensor(vareps[:, tiles(b)], moments[:, tiles(b), 1], epsilon[:, :],
                                            ALU.add).then_inc(ln_eps, 1)
                    pool.wait_ge(ln_eps, i * (2 * B) + 2 * B + b + 1)
                    nc.gpsimd.tensor_tensor(rstd[:, tiles(b)], vareps[:, tiles(b)], minushalf[:, :],
                                            ALU.pow).then_inc(ln_rstd, 1)
            k0 = B * (2 * L + 1)
            pool.wait_ge(full["att"], L * B)
            nc.gpsimd.memset(mid[:, 6144:9216], 0.0).then_inc(av_zeroed, 1)
            for b in range(B):
                inverse_std(k0 + b)
            for b in range(B):
                pool.wait_ge(normed, k0 + b + 1)
                nc.gpsimd.tensor_tensor(hs[:, tiles(b), :], hs[:, tiles(b), :], row("bo1"),
                                        ALU.add).then_inc(hbias_added, 1)
            for b in range(B):
                inverse_std(k0 + B + b)
            for b in range(B):
                inverse_std(k0 + 2 * B + b)
            for b in range(B):
                pool.wait_ge(full["a1.pv"], B)
                nc.gpsimd.memset(av[:, tiles(b), :, :, MAXROW:MAXROW + 1], 1.0).then_inc(ones_set, 1)
            pool.wait_ge(full["a1.o"], B)
            nc.gpsimd.memset(mid[:, 9216:12288], 0.0).then_inc(negmax_zeroed, 1)
            pool.wait_ge(bits_set, 1)
            nc.gpsimd.tensor_scalar(nbits, bits, -1.0, 1.0, ALU.mult, ALU.add).then_inc(nb_set, 1)
            pool.wait_ge(nb_set, 1)
            nc.gpsimd.tensor_tensor(sel[:, :, 0], nbits[:, :, 0], nbits[:, :, 1], ALU.mult)
            nc.gpsimd.tensor_tensor(sel[:, :, 1], nbits[:, :, 0], bits[:, :, 1], ALU.mult)
            nc.gpsimd.tensor_tensor(sel[:, :, 2], bits[:, :, 0], nbits[:, :, 1], ALU.mult).then_inc(sel_set, 1)
            for b in range(B):
                inverse_std(k0 + 3 * B + b)
            for b in range(B):
                pool.wait_ge(done["fc2"], b + 1)
                nc.gpsimd.tensor_tensor(hs[:, tiles(b), :], hs[:, tiles(b), :], os_[:, tiles(b), :],
                                        ALU.add).then_inc(hout_set, 1)

        @block.scalar
        def _(act):
            act.dma_start(ident[:, :], ident_d).then_inc(ident_in, 16)
            act.dma_start(colp[:, :], cols).then_inc(params_in, 16)
            act.dma_start(rowp[:, :], rows.partition_broadcast(P)).then_inc(rows_in, 16)
            act.dma_start(lr[:, 0:D], lrows[0, 0:D].partition_broadcast(P)).then_inc(rows_in, 16)
            act.dma_start(lr[:, D:2 * D], lrows[0, D:2 * D].partition_broadcast(P)).then_inc(rows_in, 16)
            act.dma_start(lc[:, :], lcols[0]).then_inc(lc_in, 16)
            act.wait_ge(params_in, 16)
            for h in range(2):
                act.wait_ge(full["conv"], h + 1)
                nc.scalar.activation(embT[:, 512 * h:512 * (h + 1)], slot("conv", h)[:, 0:512], ACT.Identity,
                                     bias=col("conv_b")).then_inc(done["conv"], 1)
            with act.Fori(0, L) as i:
                act.wait_ge(lc_in, i * 16 + 16)
                for b in range(B):
                    act.wait_ge(full["ln1T"], i * B + (b + 1))
                    nc.scalar.activation(yT[:, b, :], slot("ln1T", b)[:, 0:N], ACT.Identity, scale=lcol("ln1_g"),
                                         bias=lcol("ln1_b")).then_inc(done["ln1T"], 1)
                for b in range(B):
                    act.wait_ge(nkmax_set, i * B + (b + 1))
                    for a in range(PAIRS):
                        last = nc.scalar.activation(ekT[:, b, a, :], slot("k", b)[:, N * a:N * (a + 1)], ACT.Exp,
                                                    bias=nkmax[:, b, a:a + 1], accum_out=ksum[:, b, a:a + 1])
                    last.then_inc(done["k"], 1)
                for b in range(B):
                    act.wait_ge(done["q"], i * B + (b + 1))
                    nc.scalar.activation(qs[:, tiles(b), :, :], qs[:, tiles(b), :, :], ACT.Exp).then_inc(qexp_set, 1)
                for b in range(B):
                    act.wait_ge(full["v"], i * B + (b + 1))
                    nc.scalar.copy(vv[:, tiles(b), :],
                                   slot("v", b).rearrange("p (t f) -> p t f", t=TPB)).then_inc(done["v"], 1)
                for b in range(B):
                    act.wait_ge(full["kT"], i * B + (b + 1))
                    nc.scalar.copy(ek[:, tiles(b), :],
                                   slot("kT", b).rearrange("p (t f) -> p t f", t=TPB)).then_inc(done["kT"], 1)
                for b in range(B):
                    act.wait_ge(full["qT"], i * B + (b + 1))
                    nc.scalar.copy(qT[:, b, :, :],
                                   slot("qT", b).rearrange("p (a n) -> p a n", a=PAIRS)).then_inc(done["qT"], 1)
                for b in range(B):
                    act.wait_ge(full["ln2T"], i * B + (b + 1))
                    nc.scalar.activation(yT[:, b, :], slot("ln2T", b)[:, 0:N], ACT.Identity, scale=lcol("ln2_g"),
                                         bias=lcol("ln2_b")).then_inc(done["ln2T"], 1)
                for b in range(B):
                    act.wait_ge(full["ff1"], i * B + (b + 1))
                    for m in range(PAIRS):
                        last = nc.scalar.activation(hidT[:, b, m, :], slot("ff1", b)[:, N * m:N * (m + 1)], ACT.Gelu,
                                                    bias=lcol("ff1_b", m))
                    last.then_inc(done["ff1"], 1)
            for b in range(B):
                act.wait_ge(full["lnfT"], b + 1)
                nc.scalar.activation(yT[:, b, :], slot("lnfT", b)[:, 0:N], ACT.Identity, scale=col("lnf_g"),
                                     bias=col("lnf_b")).then_inc(done["lnfT"], 1)
            for b in range(B):
                act.wait_ge(full["a1.xT"], b + 1)
                nc.scalar.copy(xT[:, b, :, :],
                               slot("a1.xT", b)[0:EH, 0:2 * N].rearrange("p (c n) -> p c n", c=2)
                               ).then_inc(done["a1.xT"], 1)
            for b in range(B):
                for u in range(6):
                    act.wait_ge(smax_set, 6 * b + u + 1)
                    s = slot("a1.s", 6 * b + u).rearrange("p (r x n) -> p r x n", r=2, x=2)
                    for r in range(2):
                        for x in range(2):
                            y = 2 * r + x
                            last = nc.scalar.activation(probs[:, b % 2, u, r, x, :], s[:, r, x, :], ACT.Exp,
                                                        bias=smax[:, b, u, y:y + 1], scale=AD ** -0.5,
                                                        accum_out=ssum[:, b, u, y:y + 1])
                    last.then_inc(done["a1.s"], 1)
            for b in range(B):
                act.wait_ge(full["zT"], b + 1)
                for c in range(2):
                    last = nc.scalar.activation(xT[:, b, c, :], slot("zT", b)[0:EH, N * c:N * (c + 1)], ACT.Identity,
                                                scale=col("r_g", c, EH), bias=col("r_b", c, EH))
                last.then_inc(xnormed, 1)
            for b in range(B):
                act.wait_ge(full["r1"], b + 1)
                nc.scalar.activation(eT[:, b, :], slot("r1", b)[:, 0:N], ACT.Gelu,
                                     bias=col("r_in_b")).then_inc(done["r1"], 1)
            for b in range(B):
                act.wait_ge(full["r2"], b + 1)
                if b == 0:
                    act.wait_ge(done["rg"], 1)
                nc.scalar.activation(h1T[:, b, :], slot("r2", b)[:, 0:N], ACT.Gelu,
                                     bias=h1bias[:, b:b + 1]).then_inc(done["r2"], 1)
            for b in range(B):
                act.wait_ge(full["r3"], b + 1)
                nc.scalar.activation(h2T[:, b, :], slot("r3", b)[0:RL, 0:N], ACT.Gelu,
                                     bias=col("o2_b", 0, RL)).then_inc(done["r3"], 1)
            for b in range(B):
                for u in range(6):
                    act.wait_ge(full["a2.s"], 6 * b + u + 1)
                    nc.scalar.activation(probs[:, b % 2, u, :, :, :],
                                         slot("a2.s", 6 * b + u).rearrange("p (r x n) -> p r x n", r=2, x=2),
                                         ACT.Exp, scale=AD ** -0.5).then_inc(done["a2.s"], 1)
            for b in range(B):
                act.wait_ge(full["a2.nT"], b + 1)
                nc.scalar.copy(xT[:, b, :, :],
                               slot("a2.nT", b)[0:EH, 0:2 * N].rearrange("p (c n) -> p c n", c=2)
                               ).then_inc(done["a2.nT"], 1)
            for b in range(B):
                act.wait_ge(full["hT"], b + 1)
                for c in range(2):
                    last = nc.scalar.activation(xT[:, b, c, :], slot("hT", b)[0:EH, N * c:N * (c + 1)], ACT.Identity,
                                                scale=col("g2", c, EH), bias=col("b2", c, EH))
                last.then_inc(done["hT"], 1)
            for x in range(2 * B):
                b, m0 = x // 2, 3 * (x % 2)
                act.wait_ge(full["fc1"], x + 1)
                for m in range(3):
                    last = nc.scalar.activation(hid2T[:, b, m0 + m, :], slot("fc1", x)[:, N * m:N * (m + 1)],
                                                ACT.Gelu, bias=col("fc1_b", m0 + m))
                last.then_inc(done["fc1"], 1)
            for b in range(B):
                act.wait_ge(full["outT"], b + 1)
                nc.scalar.copy(xT[:, b, :, :],
                               slot("outT", b)[0:EH, 0:2 * N].rearrange("p (c n) -> p c n", c=2)
                               ).then_inc(done["outT"], 1)
            for b in range(B):
                act.wait_ge(full["selT"], b + 1)
                nc.scalar.copy(xT[:, b, :, :],
                               slot("selT", b)[0:EH, 0:2 * N].rearrange("p (c n) -> p c n", c=2)
                               ).then_inc(done["selT"], 1)

        @block.vector
        def _(dve):
            def norm_stats(k, b, src):
                for t in range(TPB):
                    last = nc.vector.bn_stats(stats[:, TPB * b + t, :], src[:, TPB * b + t, :])
                last.then_inc(ln_stats, 1)
                dve.wait_ge(ln_stats, k)
                nc.vector.memset(pause[:, :], 0.0)
                for t in range(TPB):
                    last = nc.vector.bn_aggr(moments[:, TPB * b + t, :], stats[:, TPB * b + t, :])
                last.then_inc(ln_moments, 1)

            def normalise(k, b, dst, src):
                dve.wait_ge(ln_rstd, k)
                for t in range(TPB * b, TPB * (b + 1)):
                    last = nc.vector.tensor_scalar(dst[:, t, :], src[:, t, :], moments[:, t, 0:1], rstd[:, t:t + 1],
                                                   ALU.subtract, ALU.mult)
                last.then_inc(normed, 1)

            for b in range(B):
                dve.wait_ge(full["embed"], b + 1)
                nc.vector.tensor_copy(xs[:, tiles(b), :],
                                      slot("embed", b)[:, 0:TPB * D].rearrange("p (t d) -> p t d", t=TPB)
                                      ).then_inc(done["embed"], 1)
                dve.wait_ge(done["embed"], b + 1)
                norm_stats(b + 1, b, xs)
                if b > 0:
                    normalise(b, b - 1, nrm[:, :, 0:D], xs)
            normalise(B, B - 1, nrm[:, :, 0:D], xs)
            dve.wait_ge(ctxT_zeroed, 1)

            with dve.Fori(0, L) as i:
                for b in range(B):
                    dve.wait_ge(full["k"], i * B + (b + 1))
                    nc.vector.tensor_reduce(nkmax[:, b, :], slot("k", b).rearrange("p (a n) -> p a n", a=PAIRS), X,
                                            ALU.max, negate=True).then_inc(nkmax_set, 1)
                for b in range(B):
                    dve.wait_ge(full["q"], i * B + (b + 1))
                    q = slot("q", b).rearrange("p (t h d) -> p t h d", t=TPB, h=NH)
                    nc.vector.tensor_reduce(qmax[:, tiles(b), :], q, X, ALU.max).then_inc(qmax_set, 1)
                    dve.wait_ge(qmax_set, i * B + (b + 1))
                    nc.vector.tensor_tensor(qs[:, tiles(b), :, :], q,
                                            qmax[:, tiles(b), :].unsqueeze(3).broadcast_to([P, TPB, NH, DH]),
                                            ALU.subtract).then_inc(done["q"], 1)
                for b in range(B):
                    dve.wait_ge(qexp_set, i * B + (b + 1))
                    nc.vector.tensor_reduce(qsum[:, tiles(b), :], qs[:, tiles(b), :, :], X,
                                            ALU.add).then_inc(qsum_set, 1)
                    dve.wait_ge(qsum_set, i * B + (b + 1))
                    nc.vector.reciprocal(qrec[:, tiles(b), :], qsum[:, tiles(b), :]).then_inc(dve_tmp, 1)
                    dve.wait_ge(dve_tmp, i * B + (b + 1))
                    nc.vector.tensor_scalar(qrec[:, tiles(b), :], qrec[:, tiles(b), :], DH ** -0.5, None,
                                            ALU.mult).then_inc(qrec_set, 1)
                for b in range(B):
                    dve.wait_ge(full["ctx"], i * B + (b + 1))
                    c = slot("ctx", b)[:, 0:PAIRS * P].rearrange("p (a d) -> p a d", a=PAIRS)
                    nc.vector.tensor_copy(ctxT[0:DH, b, :, 0:DH], c[0:DH, :, 0:DH])
                    nc.vector.tensor_copy(ctxT[DH:P, b, :, DH:P], c[DH:P, :, DH:P]).then_inc(done["ctx"], 1)
                for b in range(B):
                    nc.vector.reciprocal(krec[:, b, :], ksum[:, b, :]).then_inc(ksum_inv, 1)
                    dve.wait_ge(ksum_inv, i * B + (b + 1))
                    dve.wait_ge(full["ctxw"], i * B + (b + 1))
                    nc.vector.tensor_tensor(ctxw[:, b, :, :],
                                            slot("ctxw", b)[:, 0:PAIRS * D].rearrange("p (a d) -> p a d", a=PAIRS),
                                            krec[:, b, :].unsqueeze(2).broadcast_to([P, PAIRS, D]),
                                            ALU.mult).then_inc(done["ctxw"], 1)
                for name, added, k0 in (("att", attbias_added, B), ("ff2", ffbias_added, 2 * B)):
                    for b in range(B):
                        dve.wait_ge(added, i * B + (b + 1))
                        dve.wait_ge(full[name], i * B + (b + 1))
                        nc.vector.tensor_tensor(xs[:, tiles(b), :],
                                                slot(name, b)[:, 0:TPB * D].rearrange("p (t d) -> p t d", t=TPB),
                                                xs[:, tiles(b), :], ALU.add).then_inc(done[name], 1)
                        dve.wait_ge(done[name], i * B + (b + 1))
                        norm_stats(i * (2 * B) + (k0 + b + 1), b, xs)
                        if b > 0:
                            normalise(i * (2 * B) + (k0 + b), b - 1, nrm[:, :, 0:D], xs)
                    normalise(i * (2 * B) + (k0 + B), B - 1, nrm[:, :, 0:D], xs)

            k0 = B * (2 * L + 1)
            for b in range(B):
                dve.wait_ge(full["head"], b + 1)
                nc.vector.tensor_tensor(hs[:, tiles(b), :],
                                        slot("head", b)[:, :].rearrange("p (t f) -> p t f", t=TPB)[:, :, 0:E],
                                        row("head_b"), ALU.add).then_inc(done["head"], 1)
                dve.wait_ge(done["head"], b + 1)
                norm_stats(k0 + b + 1, b, hs)
                if b > 0:
                    normalise(k0 + b, b - 1, nrm, hs)
            normalise(k0 + B, B - 1, nrm, hs)

            def qkv_biases(a):
                for name, dst in ((".q", aqT), (".k", akT)):
                    for b in range(B):
                        dve.wait_ge(full[a + name], b + 1)
                        nc.vector.tensor_tensor(dst[:, b, :, :],
                                                slot(a + name, b)[:, 0:G * N].rearrange("p (g n) -> p g n", g=G),
                                                cols_of("b" + name[1] + a[1]).unsqueeze(2).broadcast_to([P, G, N]),
                                                ALU.add).then_inc(done[a + name], 1)

            def v_bias(a):
                for b in range(B):
                    dve.wait_ge(full[a + ".v"], b + 1)
                    for t in range(TPB):
                        v = slot(a + ".v", b)[:, 512 * t:512 * t + E]
                        last = nc.vector.tensor_tensor(
                            av[:, TPB * b + t, :, :, 0:AD].rearrange("p g j e -> p (g j) e"),
                            v.rearrange("p (h e) -> p h e", h=AH),
                            rowp[:, ROW["bv" + a[1]][0]:ROW["bv" + a[1]][0] + E].rearrange("p (h e) -> p h e", h=AH),
                            ALU.add)
                    last.then_inc(done[a + ".v"], 1)

            def a1_context(b):
                dve.wait_ge(full["a1.pv"], b + 1)
                nc.vector.tensor_copy(actxT[:, b, :, :],
                                      slot("a1.pv", b)[:, 0:G * N].rearrange("p (g n) -> p g n", g=G)
                                      ).then_inc(done["a1.pv"], 1)

            qkv_biases("a1")
            dve.wait_ge(av_zeroed, 1)
            v_bias("a1")
            for b in range(B + 1):
                for u in range(6):
                    if b < B:
                        dve.wait_ge(full["a1.s"], 6 * b + u + 1)
                        nc.vector.tensor_reduce(sneg[:, b, u, :],
                                                slot("a1.s", 6 * b + u).rearrange("p (y n) -> p y n", y=4), X,
                                                ALU.max, negate=True).then_inc(sneg_set, 1)
                        dve.wait_ge(sneg_set, 6 * b + u + 1)
                        nc.vector.tensor_scalar(smax[:, b, u, :], sneg[:, b, u, :], AD ** -0.5, None,
                                                ALU.mult).then_inc(smax_set, 1)
                    if u == 0 and b > 0:
                        dve.wait_ge(done["a1.s"], 6 * b)
                        nc.vector.reciprocal(srec[:, b - 1, :, :], ssum[:, b - 1, :, :]).then_inc(srec_set, 1)
                        dve.wait_ge(srec_set, b)
                        s = srec[:, b - 1, :, :].rearrange("p u x -> p (u x)")
                        for t in range(TPB):
                            v = av[:, TPB * (b - 1) + t, :, :, 0:AD]
                            r01 = s[:, 8 * t:8 * t + 8].rearrange("p (j g) -> p g j", g=2)
                            r2 = s[:, 16:24].rearrange("p (j x) -> p j x", x=2)[:, :, t]
                            for g in range(2):
                                nc.vector.tensor_tensor(v[:, g, :, :], v[:, g, :, :],
                                                        r01[:, g, :].unsqueeze(2).broadcast_to([P, 4, AD]), ALU.mult)
                            last = nc.vector.tensor_tensor(v[:, 2, :, :], v[:, 2, :, :],
                                                           r2.unsqueeze(2).broadcast_to([P, 4, AD]), ALU.mult)
                        last.then_inc(av_set, 1)
                    if u == 3 and b > 0:
                        a1_context(b - 1)

            def residual_norm(name, b, k, dst):
                pass

            for b in range(B):
                dve.wait_ge(hbias_added, b + 1)
                dve.wait_ge(full["a1.o"], b + 1)
                nc.vector.tensor_tensor(hs[:, tiles(b), :],
                                        slot("a1.o", b)[:, :].rearrange("p (t f) -> p t f", t=TPB)[:, :, 0:E],
                                        hs[:, tiles(b), :], ALU.add).then_inc(done["a1.o"], 1)
                dve.wait_ge(done["a1.o"], b + 1)
                norm_stats(k0 + B + b + 1, b, hs)
                if b > 0:
                    normalise(k0 + B + b, b - 1, zs, hs)
            normalise(k0 + 2 * B, B - 1, zs, hs)
            for b in range(B):
                dve.wait_ge(normed, k0 + B + b + 1)
                norm_stats(k0 + 2 * B + b + 1, b, zs)
                if b > 0:
                    normalise(k0 + 2 * B + b, b - 1, nrm, zs)
            normalise(k0 + 3 * B, B - 1, nrm, zs)
            for b in range(B):
                dve.wait_ge(xnormed, b + 1)
                for c in range(2):
                    last = nc.vector.tensor_scalar(xaT[:, b, c, :], slot("zT", b)[0:EH, N * c:N * (c + 1)],
                                                   col("g1", c, EH), col("b1", c, EH), ALU.mult, ALU.add)
                last.then_inc(done["zT"], 1)
            for b in range(B):
                dve.wait_ge(done["r1"], b + 1)
                last = nc.vector.tensor_reduce(emean[:, b:b + 1], eT[:, b, 1:N], X, ALU.add)
            last.then_inc(esum_set, 1)
            dve.wait_ge(esum_set, 1)
            nc.vector.tensor_scalar(emean[:, :], emean[:, :], 1.0 / (N - 1), None, ALU.mult).then_inc(emean_set, 1)
            dve.wait_ge(full["rg"], 1)
            nc.vector.tensor_scalar(h1bias[:, :], slot("rg", 0)[:, 0:B], col("o1_b"), None,
                                    ALU.add).then_inc(done["rg"], 1)
            qkv_biases("a2")
            dve.wait_ge(ones_set, B)
            v_bias("a2")
            for b in range(B):
                dve.wait_ge(full["r4"], b + 1)
                for t in range(TPB):
                    last = nc.vector.tensor_tensor(
                        logits[:, TPB * b + t, :, :].rearrange("p k c -> p (k c)"), slot("r4", b)[:, 4 * t:4 * t + 4],
                        rowp[:, ROW["o3_b"][0]:ROW["o3_b"][0] + 4], ALU.add)
                last.then_inc(done["r4"], 1)
            dve.wait_ge(done["r4"], B)
            nc.vector.tensor_tensor(bits, logits[:, :, :, 1], logits[:, :, :, 0], ALU.is_gt).then_inc(bits_cmp, 1)
            dve.wait_ge(bits_cmp, 1)
            for b in range(B):
                last = nc.vector.memset(bits[0:1, TPB * b, :], 1.0)
            last.then_inc(bits_set, 1)

            def a2_context(b):
                dve.wait_ge(full["a2.pv"], b + 1)
                nc.vector.tensor_copy(actxT[:, b, :, :],
                                      slot("a2.pv", b)[:, 0:G * N].rearrange("p (g n) -> p g n", g=G)
                                      ).then_inc(done["a2.pv"], 1)

            dve.wait_ge(negmax_zeroed, 1)
            for b in range(-1, B):
                for u in range(6):
                    if b + 1 < B:
                        dve.wait_ge(full["a2.m"], 6 * (b + 1) + u + 1)
                        s = slot("a2.m", 6 * (b + 1) + u).rearrange("p (r x n) -> p r x n", r=2, x=2)
                        j = 2 * (u % 2)
                        if u < 4:
                            dst = negmax[:, b + 1, u // 2, 0:2, j:j + 2, MAXROW].rearrange("p g j -> p j g")
                        else:
                            dst = negmax[:, b + 1, :, 2, j:j + 2, MAXROW].rearrange("p t j -> p j t")
                        nc.vector.tensor_reduce(dst, s, X, ALU.max, negate=True).then_inc(done["a2.m"], 1)
                    if u == 3 and b > 0:
                        a2_context(b - 1)
                if b + 1 < B:
                    dve.wait_ge(full["a2.mT"], b + 2)
                    nc.vector.tensor_tensor(aqT[:, b + 1, :, :],
                                            slot("a2.mT", b + 1)[:, 0:G * N].rearrange("p (g n) -> p g n", g=G),
                                            aqT[:, b + 1, :, :], ALU.add).then_inc(done["a2.mT"], 1)
            a2_context(B - 1)
            for b in range(B):
                dve.wait_ge(full["a2.cT"], b + 1)
                for t in range(TPB):
                    c = slot("a2.cT", b)[:, 512 * t:512 * t + G * P].rearrange("p (h e) -> p h e", h=AH)
                    last = nc.vector.reciprocal(crec[:, TPB * b + t, :, :].rearrange("p g j -> p (g j)"),
                                                c[:, :, MAXROW])
                last.then_inc(crec_set, 1)
                dve.wait_ge(crec_set, b + 1)
                for t in range(TPB):
                    c = slot("a2.cT", b)[:, 512 * t:512 * t + G * P].rearrange("p (h e) -> p h e", h=AH)
                    last = nc.vector.tensor_tensor(
                        catt[:, TPB * b + t, :].rearrange("p (h e) -> p h e", h=AH), c[:, :, 0:AD],
                        crec[:, TPB * b + t, :, :].rearrange("p g j -> p (g j)").unsqueeze(2)
                        .broadcast_to([P, AH, AD]), ALU.mult)
                last.then_inc(done["a2.cT"], 1)
            for b in range(B):
                dve.wait_ge(full["a2.o"], b + 1)
                nc.vector.tensor_tensor(os_[:, tiles(b), :],
                                        slot("a2.o", b)[:, :].rearrange("p (t f) -> p t f", t=TPB)[:, :, 0:E],
                                        row("bo2"), ALU.add).then_inc(done["a2.o"], 1)
                dve.wait_ge(done["a2.o"], b + 1)
                for t in range(TPB * b, TPB * (b + 1)):
                    last = nc.vector.scalar_tensor_tensor(out=os_[:, t, :], in0=os_[:, t, :], scalar=bits[:, t, 0:1],
                                                          in1=zs[:, t, :], op0=ALU.mult, op1=ALU.add)
                last.then_inc(dve_tmp, 1)
                dve.wait_ge(dve_tmp, L * B + b + 1)
                norm_stats(k0 + 3 * B + b + 1, b, os_)
                if b > 0:
                    normalise(k0 + 3 * B + b, b - 1, nrm, os_)
            normalise(k0 + 4 * B, B - 1, nrm, os_)
            for b in range(B):
                dve.wait_ge(full["fc2"], b + 1)
                nc.vector.tensor_tensor(zs[:, tiles(b), :],
                                        slot("fc2", b)[:, :].rearrange("p (t f) -> p t f", t=TPB)[:, :, 0:E],
                                        row("fc2_b"), ALU.add).then_inc(dve_tmp, 1)
                dve.wait_ge(dve_tmp, L * B + B + b + 1)
                for t in range(TPB * b, TPB * (b + 1)):
                    last = nc.vector.scalar_tensor_tensor(out=os_[:, t, :], in0=zs[:, t, :], scalar=bits[:, t, 1:2],
                                                          in1=os_[:, t, :], op0=ALU.mult, op1=ALU.add)
                last.then_inc(done["fc2"], 1)
            dve.wait_ge(sel_set, 1)
            for b in range(B):
                dve.wait_ge(full["down"], b + 1)
                for t in range(TPB):
                    last = nc.vector.tensor_tensor(
                        nrm[:, TPB * b + t, :].rearrange("p (k r) -> p k r", k=NA),
                        slot("down", b)[:, 512 * t:512 * t + E].rearrange("p (k r) -> p k r", k=NA),
                        sel[:, TPB * b + t, :].unsqueeze(2).broadcast_to([P, NA, E // NA]), ALU.mult)
                last.then_inc(done["down"], 1)
            for b in range(B):
                dve.wait_ge(full["up"], b + 1)
                dve.wait_ge(hout_set, b + 1)
                nc.vector.tensor_tensor(os_[:, tiles(b), :],
                                        slot("up", b)[:, :].rearrange("p (t f) -> p t f", t=TPB)[:, :, 0:E],
                                        hs[:, tiles(b), :], ALU.add).then_inc(result_set, 1)

        @block.tensor
        def _(pe):
            mm, tr = nc.tensor.matmul, nc.tensor.transpose

            for h in range(2):
                s = take(pe, "conv", h)
                for k in range(KC):
                    if k % KG == 0:
                        if h == 0:
                            pe.wait_ge(conv_w_in[k // KG], 16)
                        pe.wait_ge(image_in[h][k // KG], 16)
                    last = mm(s[:, 0:512], conv_w[:, k, :], image[:, h, k, :], start=(k == 0), stop=(k == KC - 1))
                last.then_inc(full["conv"], 1)
            pe.wait_ge(ident_in, 16)
            for b in range(B):
                s = take(pe, "embed", b)
                pe.wait_ge(done["conv"], b // 2 + 1)
                for t in range(TPB):
                    at = N * b + P * t
                    last = tr(s[:, P * t:P * (t + 1)], embT[:, at:at + P], ident[:, :])
                last.then_inc(full["embed"], 1)

            def norm_128(b, s, name):
                for t in range(TPB):
                    last = tr(s[:, P * t:P * (t + 1)], nrm[:, TPB * b + t, 0:D], ident[:, :])
                last.then_inc(full[name], 1)

            with pe.Fori(0, L) as i:
                for b in range(B):
                    s = take(pe, "ln1T", b, i)
                    pe.wait_ge(normed, i * (2 * B) + (b + 1))
                    norm_128(b, s, "ln1T")
                pe.wait_ge(qkv_in, i * 16 + 16)
                for b in range(B):
                    s = take(pe, "k", b, i)
                    pe.wait_ge(done["ln1T"], i * B + (b + 1))
                    for a in range(PAIRS):
                        at = INNER + P * a
                        last = mm(s[:, N * a:N * (a + 1)], w_qkv[:, at:at + P], yT[:, b, :], start=True, stop=True)
                    last.then_inc(full["k"], 1)
                for name, at in (("q", 0), ("v", 2 * INNER)):
                    for b in range(B):
                        s = take(pe, name, b, i)
                        for t in range(TPB):
                            last = mm(s[:, INNER * t:INNER * (t + 1)], yT[:, b, P * t:P * (t + 1)],
                                      w_qkv[:, at:at + INNER], start=True, stop=True)
                        last.then_inc(full[name], 1)
                for b in range(B):
                    s = take(pe, "kT", b, i)
                    pe.wait_ge(done["k"], i * B + (b + 1))
                    for t in range(TPB):
                        for a in range(PAIRS):
                            at = INNER * t + P * a
                            last = tr(s[:, at:at + P], ekT[:, b, a, P * t:P * (t + 1)], ident[:, :])
                    last.then_inc(full["kT"], 1)
                for b in range(B):
                    s = take(pe, "ctx", b, i)
                    pe.wait_ge(done["v"], i * B + (b + 1))
                    pe.wait_ge(done["kT"], i * B + (b + 1))
                    for a in range(PAIRS):
                        for t in range(TPB):
                            f = slice(P * a, P * (a + 1))
                            last = mm(s[:, f], vv[:, TPB * b + t, f], ek[:, TPB * b + t, f], start=(t == 0),
                                      stop=(t == TPB - 1))
                    last.then_inc(full["ctx"], 1)
                for b in range(B):
                    s = take(pe, "qT", b, i)
                    pe.wait_ge(qs_set, i * B + (b + 1))
                    for a in range(PAIRS):
                        for t in range(TPB):
                            q = qs[:, TPB * b + t, 2 * a:2 * a + 2, :].rearrange("p h d -> p (h d)")
                            at = N * a + P * t
                            last = tr(s[:, at:at + P], q, ident[:, :])
                    last.then_inc(full["qT"], 1)
                pe.wait_ge(out_in, i * 32 + 16)
                for b in range(B):
                    s = take(pe, "ctxw", b, i)
                    pe.wait_ge(done["ctx"], i * B + (b + 1))
                    for a in range(PAIRS):
                        last = mm(s[:, D * a:D * (a + 1)], ctxT[:, b, a, :], w_out[:, a, :], start=True, stop=True)
                    last.then_inc(full["ctxw"], 1)
                for b in range(B):
                    s = take(pe, "att", b, i)
                    pe.wait_ge(done["qT"], i * B + (b + 1))
                    pe.wait_ge(done["ctxw"], i * B + (b + 1))
                    for t in range(TPB):
                        for a in range(PAIRS):
                            last = mm(s[:, D * t:D * (t + 1)], qT[:, b, a, P * t:P * (t + 1)], ctxw[:, b, a, :],
                                      start=(a == 0), stop=(a == PAIRS - 1))
                    last.then_inc(full["att"], 1)
                for b in range(B):
                    s = take(pe, "ln2T", b, i)
                    pe.wait_ge(normed, i * (2 * B) + (B + b + 1))
                    norm_128(b, s, "ln2T")
                pe.wait_ge(ff1_in, i * 16 + 16)
                for b in range(B):
                    s = take(pe, "ff1", b, i)
                    pe.wait_ge(done["ln2T"], i * B + (b + 1))
                    for m in range(PAIRS):
                        last = mm(s[:, N * m:N * (m + 1)], w_ff1[:, P * m:P * (m + 1)], yT[:, b, :], start=True,
                                  stop=True)
                    last.then_inc(full["ff1"], 1)
                pe.wait_ge(ff2_in, i * 32 + 16)
                for b in range(B):
                    s = take(pe, "ff2", b, i)
                    pe.wait_ge(done["ff1"], i * B + (b + 1))
                    for t in range(TPB):
                        for m in range(PAIRS):
                            last = mm(s[:, D * t:D * (t + 1)], hidT[:, b, m, P * t:P * (t + 1)], w_ff2[:, m, :],
                                      start=(m == 0), stop=(m == PAIRS - 1))
                    last.then_inc(full["ff2"], 1)

            k0 = B * (2 * L + 1)
            for b in range(B):
                s = take(pe, "lnfT", b)
                pe.wait_ge(normed, 2 * L * B + b + 1)
                norm_128(b, s, "lnfT")
            pe.wait_ge(head_in, 16)
            for b in range(B):
                s = take(pe, "head", b)
                pe.wait_ge(done["lnfT"], b + 1)
                for t in range(TPB):
                    last = mm(s[:, 512 * t:512 * t + E], yT[:, b, P * t:P * (t + 1)], headw[:, :], start=True,
                              stop=True)
                last.then_inc(full["head"], 1)

            def transposed(name, src, ready):
                for b in range(B):
                    s = take(pe, name, b)
                    ready(b)
                    for c in range(2):
                        for t in range(TPB):
                            at = N * c + P * t
                            last = tr(s[0:EH, at:at + P], src[:, TPB * b + t, EH * c:EH * (c + 1)], ident[:, :])
                    last.then_inc(full[name], 1)

            def features_out(name, w, at, groups, src, ready):
                for b in range(B):
                    s = take(pe, name, b)
                    ready(b)
                    for g in range(groups):
                        for c in range(2):
                            last = mm(s[:, N * g:N * (g + 1)], w[:, c, at + P * g:at + P * (g + 1)], src[:, b, c, :],
                                      start=(c == 0), stop=(c == 1))
                    last.then_inc(full[name], 1)

            def tokens_out(name, w, src, ready):
                for b in range(B):
                    s = take(pe, name, b)
                    ready(b)
                    for t in range(TPB):
                        for c in range(2):
                            last = mm(s[:, 512 * t:512 * t + E], src[:, b, c, P * t:P * (t + 1)], w[:, c, :],
                                      start=(c == 0), stop=(c == 1))
                    last.then_inc(full[name], 1)

            def scores(name, b, u, stationary, moving):
                s = take(pe, name, 6 * b + u)
                for x in range(2):
                    for r in range(2):
                        j = 2 * (u % 2) + r
                        g, t = (x, u // 2) if u < 4 else (2, x)
                        rows_ = slice(32 * j, 32 * j + 32)
                        at = 512 * r + N * x
                        last = mm(s[:, at:at + N], stationary[rows_, b, g, P * t:P * (t + 1)], moving[rows_, b, g, :],
                                  start=True, stop=True)
                last.then_inc(full[name], 1)

            def context(name, b):
                s = take(pe, name, b)
                pe.wait_ge(done[name[:2] + ".s"], 6 * (b + 1))
                for g in range(G):
                    for t in range(TPB):
                        for j in range(4):
                            u, x = (2 * t + j // 2, g) if g < 2 else (4 + j // 2, t)
                            last = mm(s[32 * j:32 * j + 32, N * g:N * (g + 1)], av[:, TPB * b + t, g, j, :],
                                      probs[:, b % 2, u, j % 2, x, :], start=(t == 0), stop=(t == TPB - 1))
                last.then_inc(full[name], 1)

            transposed("a1.xT", nrm, lambda b: pe.wait_ge(normed, k0 + b + 1))
            pe.wait_ge(a1_in, 32)
            features_out("a1.q", a_wqkv[0], 0, G, xT, lambda b: pe.wait_ge(done["a1.xT"], b + 1))
            features_out("a1.k", a_wqkv[0], G * P, G, xT, lambda b: None)
            tokens_out("a1.v", a_wqkv[0][:, :, 2 * G * P:], xT, lambda b: None)
            for b in range(B + 1):
                if b < B:
                    pe.wait_ge(done["a1.q"], b + 1)
                    pe.wait_ge(done["a1.k"], b + 1)
                for u in range(6):
                    if b < B:
                        scores("a1.s", b, u, akT, aqT)
                    if u == 1 and b > 0:
                        pe.wait_ge(av_set, b)
                        context("a1.pv", b - 1)
            for b in range(B):
                s = take(pe, "a1.o", b)
                pe.wait_ge(done["a1.pv"], b + 1)
                for t in range(TPB):
                    for g in range(G):
                        last = mm(s[:, 512 * t:512 * t + E], actxT[:, b, g, P * t:P * (t + 1)], a1_wo[:, g, :],
                                  start=(g == 0), stop=(g == G - 1))
                last.then_inc(full["a1.o"], 1)
            transposed("zT", nrm, lambda b: pe.wait_ge(normed, k0 + 2 * B + b + 1))
            pe.wait_ge(r_in, 32)
            features_out("r1", rinw, 0, 1, xT, lambda b: pe.wait_ge(xnormed, b + 1))
            s = take(pe, "rg", 0)
            pe.wait_ge(emean_set, 1)
            mm(s[:, 0:B], row_[:, RH:2 * RH], emean[:, :], start=True, stop=True).then_inc(full["rg"], 1)
            pe.wait_ge(a2_in, 32)
            features_out("a2.q", a_wqkv[1], 0, G, xaT, lambda b: pe.wait_ge(done["zT"], b + 1))
            for b in range(B):
                s = take(pe, "r2", b)
                pe.wait_ge(done["r1"], b + 1)
                mm(s[:, 0:N], row_[:, 0:RH], eT[:, b, :], start=True, stop=True).then_inc(full["r2"], 1)
            features_out("a2.k", a_wqkv[1], G * P, G, xaT, lambda b: None)
            for b in range(B):
                s = take(pe, "r3", b)
                pe.wait_ge(done["r2"], b + 1)
                mm(s[0:RL, 0:N], row_[:, 2 * RH:2 * RH + RL], h1T[:, b, :], start=True,
                   stop=True).then_inc(full["r3"], 1)
            tokens_out("a2.v", a_wqkv[1][:, :, 2 * G * P:], xaT, lambda b: None)
            for b in range(B):
                s = take(pe, "r4", b)
                pe.wait_ge(done["r3"], b + 1)
                for t in range(TPB):
                    last = mm(s[:, 4 * t:4 * t + 4], h2T[:, b, P * t:P * (t + 1)],
                              row_[0:RL, 2 * RH + RL:2 * RH + RL + 4], start=True, stop=True)
                last.then_inc(full["r4"], 1)
            for b in range(-1, B):
                if b + 1 < B:
                    pe.wait_ge(done["a2.q"], b + 2)
                    pe.wait_ge(done["a2.k"], b + 2)
                if b >= 0:
                    pe.wait_ge(done["a2.mT"], b + 1)
                for u in range(6):
                    if b + 1 < B:
                        scores("a2.m", b + 1, u, aqT, akT)
                    if b >= 0:
                        scores("a2.s", b, u, akT, aqT)
                    if u == 2 and b > 0:
                        pe.wait_ge(done["a2.v"], b)
                        context("a2.pv", b - 1)
                if b + 1 < B:
                    s = take(pe, "a2.mT", b + 1)
                    pe.wait_ge(done["a2.m"], 6 * (b + 2))
                    for g in range(G):
                        for t in range(TPB):
                            at = N * g + P * t
                            last = tr(s[:, at:at + P],
                                      negmax[:, b + 1, t, g, :, :].rearrange("p j e -> p (j e)"), ident[:, :])
                    last.then_inc(full["a2.mT"], 1)
            pe.wait_ge(done["a2.v"], B)
            context("a2.pv", B - 1)
            for b in range(B):
                s = take(pe, "a2.cT", b)
                pe.wait_ge(done["a2.pv"], b + 1)
                for t in range(TPB):
                    for g in range(G):
                        at = 512 * t + P * g
                        last = tr(s[:, at:at + P], actxT[:, b, g, P * t:P * (t + 1)], ident[:, :])
                last.then_inc(full["a2.cT"], 1)
            transposed("a2.nT", catt, lambda b: pe.wait_ge(done["a2.cT"], b + 1))
            tokens_out("a2.o", a2_wo, xT, lambda b: pe.wait_ge(done["a2.nT"], b + 1))
            transposed("hT", nrm, lambda b: pe.wait_ge(normed, k0 + 3 * B + b + 1))
            pe.wait_ge(fc1_in, 16)
            for x in range(2 * B):
                b, m0 = x // 2, 3 * (x % 2)
                s = take(pe, "fc1", x)
                pe.wait_ge(done["hT"], b + 1)
                for m in range(3):
                    for c in range(2):
                        last = mm(s[:, N * m:N * (m + 1)], fc1w[:, c, P * (m0 + m):P * (m0 + m + 1)], xT[:, b, c, :],
                                  start=(c == 0), stop=(c == 1))
                last.then_inc(full["fc1"], 1)
            pe.wait_ge(fc2_in, 16)
            for b in range(B):
                s = take(pe, "fc2", b)
                pe.wait_ge(done["fc1"], 2 * (b + 1))
                for t in range(TPB):
                    for m in range(HM):
                        last = mm(s[:, 512 * t:512 * t + E], hid2T[:, b, m, P * t:P * (t + 1)], fc2w[:, m, :],
                                  start=(m == 0), stop=(m == HM - 1))
                last.then_inc(full["fc2"], 1)
            transposed("outT", os_, lambda b: pe.wait_ge(done["fc2"], b + 1))
            pe.wait_ge(ad_in, 32)
            tokens_out("down", downw, xT, lambda b: pe.wait_ge(done["outT"], b + 1))
            transposed("selT", nrm, lambda b: pe.wait_ge(done["down"], b + 1))
            tokens_out("up", upw, xT, lambda b: pe.wait_ge(done["selT"], b + 1))


def spread(w):
    w = w.reshape(w.shape[:-1] + (AH, AD))
    wide = np.zeros(w.shape[:-1] + (32,), w.dtype)
    wide[..., :AD] = w
    return wide.reshape(w.shape[:-2] + (AH * 32,))


def halves(w):
    return np.ascontiguousarray(w.reshape(2, EH, -1).transpose(1, 0, 2))


def columns(v, n):
    c = np.zeros((P, n), v.dtype)
    c[:v.size // n] = v.reshape(n, -1).T
    return c


def kernel(**inputs):
    import concourse.bacc as bacc
    from concourse.bass_utils import run_bass_kernel_spmd

    v = {k: np.asarray(a) for k, a in inputs.items()}
    t = {k[len("L0_tok_"):]: a for k, a in v.items() if k.startswith("L0_tok_")}
    a = {k[len("L0_attn_"):]: x for k, x in v.items() if k.startswith("L0_attn_")}
    f = {k[len("L0_ffn_"):]: x for k, x in v.items() if k.startswith("L0_ffn_")}
    hp = IMG // PATCH
    im = v["x"].reshape(B, C_IN, hp, PATCH, hp, PATCH).transpose(1, 3, 5, 0, 2, 4).reshape(KC // KG, KG, P, 2, 512)
    im = np.ascontiguousarray(im.transpose(3, 0, 2, 1, 4))
    cw = t["conv_w"].reshape(D, KC // KG, KG, P).transpose(1, 3, 2, 0)
    wl = np.concatenate([
        t["qkv_w"],
        t["out_w"].reshape(L, PAIRS, P, D).transpose(0, 2, 1, 3).reshape(L, P, INNER),
        t["ff1_w"],
        t["ff2_w"].reshape(L, PAIRS, P, D).transpose(0, 2, 1, 3).reshape(L, P, M)], axis=2)
    lcols = np.stack([np.concatenate([columns(t["ln1_g"][i], 1), columns(t["ln1_b"][i], 1), columns(t["ln2_g"][i], 1),
                                      columns(t["ln2_b"][i], 1), columns(t["ff1_b"][i], PAIRS)], axis=1)
                      for i in range(L)])
    lrows = np.concatenate([t["out_b"], t["ff2_b"]], axis=1)

    def key_bias(x):
        wide = spread(x).reshape(AH, 32)
        wide[:, MAXROW] = 1.0
        return wide.reshape(-1)

    col_values = {"conv_b": t["conv_b"], "lnf_g": t["lnf_g"], "lnf_b": t["lnf_b"], "bq1": spread(a["bq"].reshape(-1)),
                  "bk1": spread(a["bk"].reshape(-1)), "r_g": f["r_ln_g"], "r_b": f["r_ln_b"], "g1": f["ln1_g"],
                  "b1": f["ln1_b"], "g2": f["ln2_g"], "b2": f["ln2_b"], "r_in_b": f["r_in_b"], "o1_b": f["r_o1_b"],
                  "o2_b": f["r_o2_b"], "bq2": spread(f["bq"]), "bk2": key_bias(f["bk"]), "fc1_b": f["fc1_b"]}
    cols = np.concatenate([columns(col_values[n], COL[n][1]) for n in COL], axis=1)
    row_values = {"head_b": t["head_b"], "bv1": a["bv"].reshape(-1), "bo1": a["bo"], "bv2": f["bv"], "bo2": f["bo"],
                  "fc2_b": f["fc2_b"], "o3_b": f["r_o3_b"]}
    rows = np.concatenate([row_values[n] for n in ROW])
    wide = lambda w: spread(w.transpose(1, 0, 2).reshape(E, E))
    w_a1 = halves(np.concatenate([wide(a["Wq"]), wide(a["Wk"]), a["Wv"].transpose(1, 0, 2).reshape(E, E)], axis=1))
    wo_a1 = spread(a["Wo"].T).T.reshape(G, P, E).transpose(1, 0, 2)
    w_a2 = halves(np.concatenate([spread(f["wq"].T), spread(f["wk"].T), f["wv"].T], axis=1))
    w_ro = np.concatenate([f["r_o1_w"].T[:RH], f["r_o1_w"].T[RH:], f["r_o2_w"].T,
                           np.concatenate([f["r_o3_w"].T, np.zeros((RH - RL, 4), np.float32)])], axis=1)
    arrays = {
        "im": im, "cw": cw, "wl": wl, "lcols": lcols, "lrows": lrows, "cols": cols, "rows": rows,
        "ident": np.eye(P, dtype=np.float32), "w_head": t["head_w"], "w_a1": w_a1, "wo_a1": wo_a1, "w_a2": w_a2,
        "wo_a2": halves(f["wo"].T), "w_r": halves(f["r_in_w"].T), "w_ro": w_ro, "w_fc1": halves(f["fc1_w"].T),
        "w_fc2": f["fc2_w"].T.reshape(HM, P, E).transpose(1, 0, 2), "w_down": halves(f["lra_down"].reshape(E, E).T),
        "w_up": halves(f["lra_up"].transpose(0, 2, 1).reshape(E, E))}
    arrays = {k: np.ascontiguousarray(x) for k, x in arrays.items()}
    nc = bacc.Bacc("TRN2", target_bir_lowering=False, num_devices=1)
    args = [nc.dram_tensor(k, x.shape, mybir.dt.from_np(x.dtype), kind="ExternalInput").ap()
            for k, x in arrays.items()]
    args.append(nc.dram_tensor("out", (B, P, TPB, E), mybir.dt.float32, kind="ExternalOutput").ap())
    build(nc, *args)
    r = run_bass_kernel_spmd(nc, [arrays], core_ids=[0])
    got = r.results[0]["out"]
    return np.ascontiguousarray(got.transpose(0, 2, 1, 3)).reshape(B, N, E)
```

```python
import numpy as np
import concourse.bass as bass
from concourse import mybir
from contextlib import ExitStack

B, C_IN, IMG, PATCH = 4, 32, 128, 8
N = (IMG // PATCH) ** 2
P = 128
TPB = N // P
NT = B * TPB
D = 128
L, NH, DH, M = 2, 8, 64, 512
INNER = NH * DH
PAIRS = INNER // P
KC = C_IN * PATCH * PATCH // P
KG = 2
E = 192
EH = E // 2
AH, AD = 12, 16
G = 3
AP2 = AH // 2
HID = 768
HM = HID // P
RH, RL, NA = 128, 64, 3
EPS = 1e-5
SUMROW = 16
MAXROW = 48

COL = {}
_at = 0
for _name, _n in [("conv_b", 1), ("lnf_g", 1), ("lnf_b", 1), ("qkb1", G), ("r_g", 2), ("r_b", 2),
                  ("g1", 2), ("b1", 2), ("g2", 2), ("b2", 2), ("r_in_b", 1), ("o1_b", 1), ("o2_b", 1),
                  ("qkb2", G), ("maxrows", 1), ("fc1_b", HM)]:
    COL[_name] = (_at, _n)
    _at += _n
NCOL = _at
LCOL = {"ln1_g": (0, 1), "ln1_b": (1, 1), "ln2_g": (2, 1), "ln2_b": (3, 1), "ff1_b": (4, PAIRS)}
NLCOL = 4 + PAIRS
ROW = {}
_at = 0
for _name, _n in [("head_b", E), ("bv1", E), ("bo1", E), ("bv2", E), ("bo2", E), ("fc2_b", E), ("o3_b", 4)]:
    ROW[_name] = (_at, _n)
    _at += _n
NROW = _at

PRE = [("conv", 0), ("conv", 1)] + [("embed", b) for b in range(B)]
LN1K = [("ln1T", 0), ("ln1T", 1), ("k", 0), ("ln1T", 2), ("k", 1), ("ln1T", 3), ("k", 2), ("k", 3)]
LN2F = [("ln2T", 0), ("ln2T", 1), ("ff1", 0), ("ln2T", 2), ("ff1", 1), ("ln2T", 3), ("ff1", 2), ("ff1", 3)]
BODY = (LN1K + [(s, b) for s in ("q", "v", "kT", "ctx", "qT", "ctxw", "att") for b in range(B)] + LN2F
        + [("ff2", b) for b in range(B)])

A1_FIRST = [("xT", 0, 0), ("xT", 0, 1), ("qk", 0, 0), ("v", 0, 0), ("xT", 0, 2), ("rep", 0, 0), ("rep", 1, 0),
            ("rep", 2, 0), ("xT", 0, 3)]
A1_STEP = [("s", 0, 0), ("scale", 0, -1), ("qk", 0, 1), ("s", 1, 0), ("v", 0, 1), ("o", 0, -2), ("s", 2, 0),
           ("rep", 0, 1), ("z", 0, -2), ("s", 3, 0), ("rep", 1, 1), ("pv", 0, -1), ("s", 4, 0), ("zn", 0, -2),
           ("rep", 2, 1), ("s", 5, 0), ("pvout", 0, -1)]
A2_FIRST = [("zT", 0, 0), ("zT", 0, 1), ("r1", 0, 0), ("qk", 0, 0), ("zT", 0, 2), ("r1", 0, 1), ("v", 0, 0),
            ("zT", 0, 3), ("r1", 0, 2), ("rep", 0, 0), ("r1", 0, 3), ("rep", 1, 0), ("rep", 2, 0), ("rg", 0, 0),
            ("m", 0, 0), ("r2", 0, 0), ("m", 1, 0), ("r2", 0, 1), ("m", 2, 0), ("r2", 0, 2), ("qk", 0, 1),
            ("r2", 0, 3), ("m", 3, 0), ("r3", 0, 0), ("r3", 0, 1), ("m", 4, 0), ("r3", 0, 2), ("r3", 0, 3),
            ("v", 0, 1), ("r4", 0, 0), ("m", 5, 0), ("r4", 0, 1), ("r4", 0, 2), ("r4", 0, 3), ("nm", 0, 0),
            ("rep", 0, 1), ("rep", 1, 1), ("rep", 2, 1), ("mT", 0, 0), ("mT", 1, 0)]
A2_STEP = [("pvout", 0, -1), ("s", 0, 0), ("s", 1, 0), ("m", 0, 1), ("cT", 0, -1), ("s", 2, 0), ("m", 1, 1),
           ("s", 3, 0), ("m", 2, 1), ("qk", 0, 2), ("nT", 0, -1), ("s", 4, 0), ("m", 3, 1), ("o", 0, -1),
           ("s", 5, 0), ("m", 4, 1), ("v", 0, 2), ("m", 5, 1), ("nm", 0, 1), ("rep", 0, 2), ("hn", 0, -1),
           ("rep", 1, 2), ("rep", 2, 2), ("mT", 0, 1), ("mT", 1, 1), ("pv", 0, 0)]
PER_BATCH = {"s": 6, "m": 6, "rep": 3, "mT": 2}
NO_UNIT = ("scale", "z", "zn", "pvout", "nm", "hn")


def steps(first, step, count):
    out = [(part, u, d) for part, u, d in first]
    for b in range(count):
        out += [(part, u, b + d) for part, u, d in step if 0 <= b + d < B]
    return out


A1 = steps(A1_FIRST, A1_STEP, B + 2)
A2 = steps(A2_FIRST, A2_STEP, B + 1)


def unit(part, u, b):
    return PER_BATCH.get(part, 1) * b + u


TAIL = ([(s, b) for s in ("lnfT", "head") for b in range(B)]
        + [("a1." + part, unit(part, u, b)) for part, u, b in A1 if part not in NO_UNIT]
        + [("a2." + part, unit(part, u, b)) for part, u, b in A2 if part not in NO_UNIT]
        + [("hT", b) for b in range(B)] + [("fc1", x) for x in range(2 * B)]
        + [(s, b) for s in ("fc2", "outT", "down", "selT", "up") for b in range(B)])
NSLOT = 4
NORM_BATCH = [b for _ in range(2 * L + 2) for b in range(B)] + [b for b in range(B) for _ in range(2)] + list(range(B))


def build(nc, im0, im1, cw, wl, lcols, lrows, cols, rows, ident_d, selectors, w_head, w_a1, wo_a1, w_a2, wo_a2,
          w_r, w_ro, w_fc1, w_fc2, w_down, w_up, out):
    f32, f32r = mybir.dt.float32, mybir.dt.float32r
    ALU = mybir.AluOpType
    ACT = mybir.ActivationFunctionType
    X = mybir.AxisListType.X

    ctx = ExitStack()
    with ctx:
        def sb(name, n, dtype=f32):
            return ctx.enter_context(nc.sbuf_tensor(name, [P, n], dtype))

        names = sorted({n for n, _ in PRE + BODY + TAIL})
        full = {n: ctx.enter_context(nc.semaphore("full_" + n.replace(".", "_"))) for n in names}
        done = {n: ctx.enter_context(nc.semaphore("done_" + n.replace(".", "_"))) for n in names}

        def sem(name):
            return ctx.enter_context(nc.semaphore(name))

        big = sb("big", 16384)
        mid = sb("mid", 10240)
        image = big[:, :].rearrange("p (h k t) -> p h k t", h=2, k=KC)
        ekT = big[:, 0:4096].rearrange("p (b a n) -> p b a n", b=B, a=PAIRS)
        hidT = ekT
        vv = big[:, 4096:8192].rearrange("p (t f) -> p t f", t=NT)
        qs = big[:, 8192:12288].rearrange("p (t h d) -> p t h d", t=NT, h=NH)
        qT = big[:, 12288:16384].rearrange("p (b a n) -> p b a n", b=B, a=PAIRS)
        conv_w = mid[:, 0:KC * D].rearrange("p (k d) -> p k d", k=KC)
        embT = mid[:, 8192:9216]
        ek = mid[:, 0:4096].rearrange("p (t f) -> p t f", t=NT)
        ctxT = mid[:, 4096:6144].rearrange("p (b a d) -> p b a d", b=B, a=PAIRS)
        ctxw = mid[:, 6144:8192].rearrange("p (b a d) -> p b a d", b=B, a=PAIRS)
        yT = mid[:, 9216:10240].rearrange("p (b n) -> p b n", b=B)
        probs = big[:, 0:12288].rearrange("p (z u r x n) -> p z u r x n", z=2, u=6, r=2, x=2)
        eT = big[:, 6144:7168].rearrange("p (b n) -> p b n", b=B)
        h1T = big[:, 7168:8192].rearrange("p (b n) -> p b n", b=B)
        h2T = big[0:RL, 8192:9216].rearrange("p (b n) -> p b n", b=B)
        hid2T = big[:, 0:6144].rearrange("p (b m n) -> p b m n", b=B, m=HM)
        xT = big[0:EH, 12288:14336].rearrange("p (b c n) -> p b c n", b=B, c=2)
        negmax = big[:, 14336:15872].rearrange("p (t h e) -> p t h e", t=TPB, h=AH)
        av = mid[:, 0:3072].rearrange("p (t h e) -> p t h e", t=NT, h=AH)
        actxT = mid[:, 3072:6144].rearrange("p (b g n) -> p b g n", b=B, g=G)
        xaT = mid[0:EH, 6144:8192].rearrange("p (b c n) -> p b c n", b=B, c=2)
        catt = mid[:, 8192:9728].rearrange("p (t f) -> p t f", t=NT)
        xs_flat = sb("xs", NT * D)
        xs = xs_flat[:, :].rearrange("p (t d) -> p t d", t=NT)
        qkf = xs_flat[:, 0:G * N].rearrange("p (g n) -> p g n", g=G)
        nrm = sb("nrm", NT * E)[:, :].rearrange("p (t d) -> p t d", t=NT)
        hs = sb("hs", NT * E)[:, :].rearrange("p (t d) -> p t d", t=NT)
        zs_flat = sb("zs", NT * E)
        zs = zs_flat[:, :].rearrange("p (t d) -> p t d", t=NT)
        sel_f32 = zs_flat[:, 0:1024]
        selr = sb("selr", 1024, f32r)[:, :].rearrange("p (v k m) -> p v k m", v=2, k=4)
        qk_parts = sb("qk_parts", 2 * G * N, f32r)[:, :].rearrange("p (o g n) -> p o g n", o=2, g=G)
        qk_wide = sb("qk_wide", 2 * 2 * AP2 * N, f32r)[:, :].rearrange("p (z a n) -> p z a n", z=2, a=2 * AP2)
        os_ = sb("os", NT * E)[:, :].rearrange("p (t d) -> p t d", t=NT)
        lw = sb("lw", 3 * INNER + INNER + M + M)
        w_qkv = lw[:, 0:1536]
        w_out = lw[:, 1536:2048].rearrange("p (a d) -> p a d", a=PAIRS)
        w_ff1 = lw[:, 2048:2560]
        w_ff2 = lw[:, 2560:3072].rearrange("p (m d) -> p m d", m=PAIRS)
        lc = sb("lc", NLCOL)
        lr = sb("lr", 2 * D)
        colp = sb("colp", NCOL)
        rowp = sb("rowp", NROW)
        ident = sb("identity", P)
        headw = sb("headw", E)
        a_w = [sb(f"a{n}_w", 2 * 3 * E) for n in (1, 2)]
        a_wqkv = [w[0:EH, :].rearrange("p (c f) -> p c f", c=2) for w in a_w]
        a1_wo = sb("a1_wo", G * E)[:, :].rearrange("p (g f) -> p g f", g=G)
        a2_wo = sb("a2_wo", 2 * E)[0:EH, :].rearrange("p (c f) -> p c f", c=2)
        rinw = sb("rinw", 2 * RH)[0:EH, :].rearrange("p (c f) -> p c f", c=2)
        row_ = sb("row", 2 * RH + RL + 4)
        fc1w = lw[0:EH, 0:2 * HID].rearrange("p (c f) -> p c f", c=2)
        fc2w = lw[:, 2 * HID:2 * HID + HM * E].rearrange("p (m f) -> p m f", m=HM)
        downw = sb("downw", 2 * E)[0:EH, :].rearrange("p (c f) -> p c f", c=2)
        upw = sb("upw", 2 * E)[0:EH, :].rearrange("p (c f) -> p c f", c=2)
        stats = sb("stats", NT * 6)[:, :].rearrange("p (t s) -> p t s", t=NT)
        moments = sb("moments", NT * 2)[:, :].rearrange("p (t s) -> p t s", t=NT)
        vareps = sb("vareps", NT)
        rstd = sb("rstd", NT)
        minushalf = sb("minushalf", TPB)
        epsilon = sb("epsilon", TPB)
        pause = sb("pause", 1)
        nkmax = sb("nkmax", B * PAIRS)[:, :].rearrange("p (b a) -> p b a", b=B)
        ksum = sb("ksum", B * PAIRS)[:, :].rearrange("p (b a) -> p b a", b=B)
        krec = sb("krec", B * PAIRS)[:, :].rearrange("p (b a) -> p b a", b=B)
        qmax = sb("qmax", NT * NH)[:, :].rearrange("p (t h) -> p t h", t=NT)
        qsum = sb("qsum", NT * NH)[:, :].rearrange("p (t h) -> p t h", t=NT)
        qrec = sb("qrec", NT * NH)[:, :].rearrange("p (t h) -> p t h", t=NT)
        smax = sb("smax", B * 24)[:, :].rearrange("p (b t h) -> p b t h", b=B, t=TPB)
        ssum = sb("ssum", B * 24)[:, :].rearrange("p (b t h) -> p b t h", b=B, t=TPB)
        srec = sb("srec", B * 24)[:, :].rearrange("p (b t h) -> p b t h", b=B, t=TPB)
        crec = sb("crec", NT * AH)[:, :].rearrange("p (t h) -> p t h", t=NT)
        emean = sb("emean", B)
        h1bias = sb("h1bias", B)
        logits = sb("logits", NT * 4)[:, :].rearrange("p (t k c) -> p t k c", t=NT, k=2)
        bits = sb("bits", NT * 2)[:, :].rearrange("p (t k) -> p t k", t=NT)
        nbits = sb("nbits", NT * 2)[:, :].rearrange("p (t k) -> p t k", t=NT)
        sel = sb("sel", NT * NA)[:, :].rearrange("p (t k) -> p t k", t=NT)

        psum = ctx.enter_context(nc.psum_tensor("psum", [P, NSLOT * 1024], f32))

        def col(name, k=0, n=P):
            return colp[0:n, COL[name][0] + k:COL[name][0] + k + 1]

        def cols_of(name):
            return colp[:, COL[name][0]:COL[name][0] + COL[name][1]]

        def lcol(name, k=0):
            return lc[:, LCOL[name][0] + k:LCOL[name][0] + k + 1]

        def row(name, *shape):
            r = rowp[:, ROW[name][0]:ROW[name][0] + ROW[name][1]]
            return r.unsqueeze(1).broadcast_to([P, TPB, ROW[name][1]])

        def tiles(b):
            return slice(TPB * b, TPB * (b + 1))

        place, before = {}, {}
        for seq, start in ((PRE, 0), (BODY, len(PRE)), (TAIL, len(PRE) + len(BODY))):
            for k, key in enumerate(seq):
                place[key] = (start + k) % NSLOT
                if k >= NSLOT:
                    before[key] = seq[k - NSLOT]

        def slot(name, k):
            s = place[(name, k)]
            return psum[:, 1024 * s:1024 * (s + 1)]

        def take(pe, name, k, layer=None, source=None):
            who, n = before.get((name, k), (None, 0))
            if who is not None:
                last = max(n, k) if who == source else n
                pe.wait_ge(done[who], last + 1 if layer is None else layer * B + (last + 1))
            elif (name, k) not in PRE:
                at = BODY.index((name, k)) if layer is not None else TAIL.index((name, k))
                pe.wait_ge(ln_stats, 2 * L * B + at + 1 if layer is None else layer * (2 * B) + (at + 1))
            if source is not None and source != who:
                pe.wait_ge(done[source], k + 1 if layer is None else layer * B + (k + 1))
            return slot(name, k)

        first_in = [sem(f"first_in{k}") for k in range(KC // KG)]
        second_in = [sem(f"second_in{k}") for k in range(2)]
        ident_in, params_in, rows_in = sem("ident_in"), sem("params_in"), sem("rows_in")
        qkv_in, out_in, ff1_in, ff2_in, lc_in = (sem(n) for n in ("qkv_in", "out_in", "ff1_in", "ff2_in", "lc_in"))
        a1_in, a2_in, fc_in, ad_in = (sem(n) for n in ("a1_in", "a2_in", "fc_in", "ad_in"))
        half_set, ctxT_zeroed, av_zeroed = sem("half_set"), sem("ctxT_zeroed"), sem("av_zeroed")
        ln_stats, ln_moments, ln_eps, ln_rstd, normed = (
            sem(n) for n in ("ln_stats", "ln_moments", "ln_eps", "ln_rstd", "normed"))
        attbias_added, ffbias_added = sem("attbias_added"), sem("ffbias_added")
        nkmax_set, ksum_inv = sem("nkmax_set"), sem("ksum_inv")
        qmax_set, qexp_set, qsum_set, qrec_set, qs_set = (
            sem(n) for n in ("qmax_set", "qexp_set", "qsum_set", "qrec_set", "qs_set"))
        smax_set, srec_set, av_set = sem("smax_set"), sem("srec_set"), sem("av_set")
        sel_in, sel_cast, hi_set, parts_set = sem("sel_in"), sem("sel_cast"), sem("hi_set"), sem("parts_set")
        nmhi_set, nm_set = sem("nmhi_set"), sem("nm_set")
        hbias_added, xnormed = sem("hbias_added"), sem("xnormed")
        esum_set, emean_set, logits_set, bits_set, sel_set, nb_set = (
            sem(n) for n in ("esum_set", "emean_set", "logits_set", "bits_set", "sel_set", "nb_set"))
        bits_cmp = sem("bits_cmp")
        negmax_zeroed, ones_set, crec_set = sem("negmax_zeroed"), sem("ones_set"), sem("crec_set")
        dve_tmp = sem("dve_tmp")
        xa_set = sem("xa_set")
        hout_set, result_set, stored = sem("hout_set"), sem("result_set"), sem("stored")

        block = ctx.enter_context(nc.Block())

        @block.sync
        def _(sp):
            for k in range(KC // KG):
                sp.dma_start(image[:, 0, KG * k:KG * (k + 1), :], im0[k]).then_inc(first_in[k], 16)
            for k in range(2):
                sp.dma_start(image[:, 1, KC // 2 * k:KC // 2 * (k + 1), :], im1[k]).then_inc(second_in[k], 16)
            sp.dma_start(w_qkv, wl[0, :, 0:1536]).then_inc(qkv_in, 16)
            sp.dma_start(lw[:, 1536:2048], wl[0, :, 1536:2048]).then_inc(out_in, 16)
            sp.dma_start(w_ff1, wl[0, :, 2048:2560]).then_inc(ff1_in, 16)
            sp.dma_start(lw[:, 2560:3072], wl[0, :, 2560:3072]).then_inc(ff2_in, 16)
            sp.dma_start(headw[:, :], w_head).then_inc(a1_in, 16)
            sp.dma_start(a_wqkv[0], w_a1).then_inc(a1_in, 16)
            sp.dma_start(a1_wo, wo_a1).then_inc(a1_in, 16)
            sp.dma_start(rinw, w_r).then_inc(a2_in, 16)
            sp.dma_start(row_[:, :], w_ro).then_inc(a2_in, 16)
            sp.dma_start(a_wqkv[1], w_a2).then_inc(a2_in, 16)
            sp.dma_start(a2_wo, wo_a2).then_inc(a2_in, 16)
            sp.dma_start(downw, w_down).then_inc(ad_in, 16)
            sp.dma_start(upw, w_up).then_inc(ad_in, 16)
            with sp.Fori(0, L - 1) as i:
                sp.wait_ge(full["v"], i * B + B)
                sp.dma_start(w_qkv, wl[i + 1, :, 0:1536]).then_inc(qkv_in, 16)
                sp.wait_ge(full["ctxw"], i * B + B)
                sp.wait_ge(attbias_added, i * B + B)
                sp.dma_start(lw[:, 1536:2048], wl[i + 1, :, 1536:2048]).then_inc(out_in, 16)
                sp.dma_start(lr[:, 0:D], lrows[i + 1, 0:D].partition_broadcast(P)).then_inc(out_in, 16)
                sp.wait_ge(done["ff1"], i * B + B)
                sp.dma_start(lc[:, :], lcols[i + 1]).then_inc(lc_in, 16)
                sp.dma_start(w_ff1, wl[i + 1, :, 2048:2560]).then_inc(ff1_in, 16)
                sp.wait_ge(full["ff2"], i * B + B)
                sp.wait_ge(ffbias_added, i * B + B)
                sp.dma_start(lw[:, 2560:3072], wl[i + 1, :, 2560:3072]).then_inc(ff2_in, 16)
                sp.dma_start(lr[:, D:2 * D], lrows[i + 1, D:2 * D].partition_broadcast(P)).then_inc(ff2_in, 16)
            sp.wait_ge(full["ff2"], L * B)
            sp.dma_start(fc1w, w_fc1).then_inc(fc_in, 16)
            sp.dma_start(fc2w, w_fc2).then_inc(fc_in, 16)
            for b in range(B):
                sp.wait_ge(result_set, b + 1)
                sp.dma_start(out[b], os_[:, tiles(b), :]).then_inc(stored, 16)
            sp.wait_ge(stored, 16 * B)

        @block.gpsimd
        def _(pool):
            nc.gpsimd.memset(epsilon[:, :], EPS)
            nc.gpsimd.memset(minushalf[:, :], -0.5).then_inc(half_set, 1)
            pool.wait_ge(half_set, 1)

            def inverse_std(k):
                b = NORM_BATCH[k]
                pool.wait_ge(ln_moments, k + 1)
                nc.gpsimd.tensor_tensor(vareps[:, tiles(b)], moments[:, tiles(b), 1], epsilon[:, :],
                                        ALU.add).then_inc(ln_eps, 1)
                pool.wait_ge(ln_eps, k + 1)
                nc.gpsimd.tensor_tensor(rstd[:, tiles(b)], vareps[:, tiles(b)], minushalf[:, :],
                                        ALU.pow).then_inc(ln_rstd, 1)

            for b in range(B):
                inverse_std(b)
            pool.wait_ge(full["conv"], 2)
            nc.gpsimd.memset(mid[:, 4096:6144], 0.0).then_inc(ctxT_zeroed, 1)
            pool.wait_ge(rows_in, 48)
            with pool.Fori(0, L) as i:
                pool.wait_ge(out_in, i * 32 + 16)
                for b in range(B):
                    pool.wait_ge(normed, i * (2 * B) + b + 1)
                    nc.gpsimd.tensor_tensor(xs[:, tiles(b), :], xs[:, tiles(b), :],
                                            lr[:, 0:D].unsqueeze(1).broadcast_to([P, TPB, D]),
                                            ALU.add).then_inc(attbias_added, 1)
                for b in range(B):
                    pool.wait_ge(qrec_set, i * B + b + 1)
                    nc.gpsimd.tensor_tensor(qs[:, tiles(b), :, :], qs[:, tiles(b), :, :],
                                            qrec[:, tiles(b), :].unsqueeze(3).broadcast_to([P, TPB, NH, DH]),
                                            ALU.mult).then_inc(qs_set, 1)
                for b in range(B):
                    pool.wait_ge(ln_moments, i * (2 * B) + B + b + 1)
                    nc.gpsimd.tensor_tensor(vareps[:, tiles(b)], moments[:, tiles(b), 1], epsilon[:, :],
                                            ALU.add).then_inc(ln_eps, 1)
                    pool.wait_ge(ln_eps, i * (2 * B) + B + b + 1)
                    nc.gpsimd.tensor_tensor(rstd[:, tiles(b)], vareps[:, tiles(b)], minushalf[:, :],
                                            ALU.pow).then_inc(ln_rstd, 1)
                for b in range(B):
                    pool.wait_ge(normed, i * (2 * B) + B + b + 1)
                    if b == 0:
                        pool.wait_ge(ff2_in, i * 32 + 16)
                    nc.gpsimd.tensor_tensor(xs[:, tiles(b), :], xs[:, tiles(b), :],
                                            lr[:, D:2 * D].unsqueeze(1).broadcast_to([P, TPB, D]),
                                            ALU.add).then_inc(ffbias_added, 1)
                for b in range(B):
                    pool.wait_ge(ln_moments, i * (2 * B) + 2 * B + b + 1)
                    nc.gpsimd.tensor_tensor(vareps[:, tiles(b)], moments[:, tiles(b), 1], epsilon[:, :],
                                            ALU.add).then_inc(ln_eps, 1)
                    pool.wait_ge(ln_eps, i * (2 * B) + 2 * B + b + 1)
                    nc.gpsimd.tensor_tensor(rstd[:, tiles(b)], vareps[:, tiles(b)], minushalf[:, :],
                                            ALU.pow).then_inc(ln_rstd, 1)
            k0 = B * (2 * L + 1)
            pool.wait_ge(full["ctxw"], L * B)
            nc.gpsimd.memset(mid[:, 0:3072], 0.0).then_inc(av_zeroed, 1)
            pool.wait_ge(full["att"], L * B)
            nc.gpsimd.memset(negmax, 0.0).then_inc(negmax_zeroed, 1)
            for b in range(B):
                inverse_std(k0 + b)
            for b in range(B):
                pool.wait_ge(normed, k0 + b + 1)
                nc.gpsimd.tensor_tensor(hs[:, tiles(b), :], hs[:, tiles(b), :], row("bo1"),
                                        ALU.add).then_inc(hbias_added, 1)
            for b in range(2 * B):
                inverse_std(k0 + B + b)
            pool.wait_ge(full["a1.pv"], B)
            nc.gpsimd.memset(av[:, :, :, SUMROW:SUMROW + 1], 1.0).then_inc(ones_set, 1)
            pool.wait_ge(bits_set, 1)
            nc.gpsimd.tensor_scalar(nbits, bits, -1.0, 1.0, ALU.mult, ALU.add).then_inc(nb_set, 1)
            pool.wait_ge(nb_set, 1)
            nc.gpsimd.tensor_tensor(sel[:, :, 0], nbits[:, :, 0], nbits[:, :, 1], ALU.mult)
            nc.gpsimd.tensor_tensor(sel[:, :, 1], nbits[:, :, 0], bits[:, :, 1], ALU.mult)
            nc.gpsimd.tensor_tensor(sel[:, :, 2], bits[:, :, 0], nbits[:, :, 1], ALU.mult).then_inc(sel_set, 1)
            for b in range(B):
                inverse_std(k0 + 3 * B + b)
            for b in range(B):
                pool.wait_ge(done["fc2"], b + 1)
                nc.gpsimd.tensor_tensor(hs[:, tiles(b), :], hs[:, tiles(b), :], os_[:, tiles(b), :],
                                        ALU.add).then_inc(hout_set, 1)

        @block.scalar
        def _(act):
            for k in range(KC // KG):
                act.dma_start(conv_w[:, KG * k:KG * (k + 1), :], cw[k]).then_inc(first_in[k], 16)
            act.dma_start(ident[:, :], ident_d).then_inc(ident_in, 16)
            act.dma_start(sel_f32, selectors).then_inc(sel_in, 16)
            act.dma_start(colp[:, :], cols).then_inc(params_in, 16)
            act.dma_start(rowp[:, :], rows.partition_broadcast(P)).then_inc(rows_in, 16)
            act.dma_start(lr[:, 0:D], lrows[0, 0:D].partition_broadcast(P)).then_inc(rows_in, 16)
            act.dma_start(lr[:, D:2 * D], lrows[0, D:2 * D].partition_broadcast(P)).then_inc(rows_in, 16)
            act.dma_start(lc[:, :], lcols[0]).then_inc(lc_in, 16)
            act.wait_ge(params_in, 16)
            for h in range(2):
                act.wait_ge(full["conv"], h + 1)
                nc.scalar.activation(embT[:, 512 * h:512 * (h + 1)], slot("conv", h)[:, 0:512], ACT.Identity,
                                     bias=col("conv_b")).then_inc(done["conv"], 1)
            with act.Fori(0, L) as i:
                act.wait_ge(lc_in, i * 16 + 16)
                for name, b in LN1K:
                    if name == "ln1T":
                        act.wait_ge(full["ln1T"], i * B + (b + 1))
                        nc.scalar.activation(yT[:, b, :], slot("ln1T", b)[:, 0:N], ACT.Identity, scale=lcol("ln1_g"),
                                             bias=lcol("ln1_b")).then_inc(done["ln1T"], 1)
                    else:
                        act.wait_ge(nkmax_set, i * B + (b + 1))
                        for a in range(PAIRS):
                            last = nc.scalar.activation(ekT[:, b, a, :], slot("k", b)[:, N * a:N * (a + 1)], ACT.Exp,
                                                        bias=nkmax[:, b, a:a + 1], accum_out=ksum[:, b, a:a + 1])
                        last.then_inc(done["k"], 1)
                for b in range(B):
                    act.wait_ge(done["q"], i * B + (b + 1))
                    nc.scalar.activation(qs[:, tiles(b), :, :], qs[:, tiles(b), :, :], ACT.Exp).then_inc(qexp_set, 1)
                for b in range(B):
                    act.wait_ge(full["v"], i * B + (b + 1))
                    nc.scalar.copy(vv[:, tiles(b), :],
                                   slot("v", b).rearrange("p (t f) -> p t f", t=TPB)).then_inc(done["v"], 1)
                for b in range(B):
                    act.wait_ge(full["kT"], i * B + (b + 1))
                    nc.scalar.copy(ek[:, tiles(b), :],
                                   slot("kT", b).rearrange("p (t f) -> p t f", t=TPB)).then_inc(done["kT"], 1)
                for b in range(B):
                    act.wait_ge(full["qT"], i * B + (b + 1))
                    nc.scalar.copy(qT[:, b, :, :],
                                   slot("qT", b).rearrange("p (a n) -> p a n", a=PAIRS)).then_inc(done["qT"], 1)
                for name, b in LN2F:
                    if name == "ln2T":
                        act.wait_ge(full["ln2T"], i * B + (b + 1))
                        nc.scalar.activation(yT[:, b, :], slot("ln2T", b)[:, 0:N], ACT.Identity, scale=lcol("ln2_g"),
                                             bias=lcol("ln2_b")).then_inc(done["ln2T"], 1)
                    else:
                        act.wait_ge(full["ff1"], i * B + (b + 1))
                        for m in range(PAIRS):
                            last = nc.scalar.activation(hidT[:, b, m, :], slot("ff1", b)[:, N * m:N * (m + 1)],
                                                        ACT.Gelu, bias=lcol("ff1_b", m))
                        last.then_inc(done["ff1"], 1)
            for b in range(B):
                act.wait_ge(full["lnfT"], b + 1)
                nc.scalar.activation(yT[:, b, :], slot("lnfT", b)[:, 0:N], ACT.Identity, scale=col("lnf_g"),
                                     bias=col("lnf_b")).then_inc(done["lnfT"], 1)

            def copy_halves(name, b):
                act.wait_ge(full[name], b + 1)
                nc.scalar.copy(xT[:, b, :, :], slot(name, b)[0:EH, 0:2 * N].rearrange("p (c n) -> p c n", c=2)
                               ).then_inc(done[name], 1)

            for part, u, b in A1:
                if part == "xT":
                    copy_halves("a1.xT", b)
                elif part == "s":
                    act.wait_ge(smax_set, unit("s", u, b) + 1)
                    s = slot("a1.s", unit("s", u, b)).rearrange("p (r x n) -> p r x n", r=2, x=2)
                    for r in range(2):
                        for x in range(2):
                            h = 4 * (u % G) + 2 * x + r
                            last = nc.scalar.activation(probs[:, b % 2, u, r, x, :], s[:, r, x, :], ACT.Exp,
                                                        bias=smax[:, b, u // G, h:h + 1],
                                                        accum_out=ssum[:, b, u // G, h:h + 1])
                    last.then_inc(done["a1.s"], 1)
            for part, u, b in A2:
                if part == "zT":
                    act.wait_ge(full["a2.zT"], b + 1)
                    for c in range(2):
                        last = nc.scalar.activation(xT[:, b, c, :], slot("a2.zT", b)[0:EH, N * c:N * (c + 1)],
                                                    ACT.Identity, scale=col("r_g", c, EH), bias=col("r_b", c, EH))
                    last.then_inc(xnormed, 1)
                elif part == "r1":
                    act.wait_ge(full["a2.r1"], b + 1)
                    nc.scalar.activation(eT[:, b, :], slot("a2.r1", b)[:, 0:N], ACT.Gelu,
                                         bias=col("r_in_b")).then_inc(done["a2.r1"], 1)
                elif part == "r2":
                    act.wait_ge(full["a2.r2"], b + 1)
                    act.wait_ge(done["a2.rg"], 1)
                    nc.scalar.activation(h1T[:, b, :], slot("a2.r2", b)[:, 0:N], ACT.Gelu,
                                         bias=h1bias[:, b:b + 1]).then_inc(done["a2.r2"], 1)
                elif part == "r3":
                    act.wait_ge(full["a2.r3"], b + 1)
                    nc.scalar.activation(h2T[:, b, :], slot("a2.r3", b)[0:RL, 0:N], ACT.Gelu,
                                         bias=col("o2_b", 0, RL)).then_inc(done["a2.r3"], 1)
                elif part == "rep":
                    k = unit("rep", u, b)
                    act.wait_ge(full["a2.rep"], k + 1)
                    s = slot("a2.rep", k).rearrange("p (a n) -> p a n", a=4)
                    nq = (4, 2, 0)[u]
                    for a0, a1, bias in ((0, nq, 0.0), (nq, 4, col("maxrows"))):
                        if a1 > a0:
                            last = nc.scalar.activation(qk_wide[:, b % 2, 4 * u + a0:4 * u + a1, :], s[:, a0:a1, :],
                                                        ACT.Identity, bias=bias)
                    last.then_inc(done["a2.rep"], 1)
                elif part == "s":
                    k = unit("s", u, b)
                    act.wait_ge(full["a2.s"], k + 1)
                    nc.scalar.activation(probs[:, b % 2, u, :, :, :],
                                         slot("a2.s", k).rearrange("p (r x n) -> p r x n", r=2, x=2),
                                         ACT.Exp).then_inc(done["a2.s"], 1)
                elif part == "nT":
                    copy_halves("a2.nT", b)
            for b in range(B):
                act.wait_ge(full["hT"], b + 1)
                for c in range(2):
                    last = nc.scalar.activation(xT[:, b, c, :], slot("hT", b)[0:EH, N * c:N * (c + 1)], ACT.Identity,
                                                scale=col("g2", c, EH), bias=col("b2", c, EH))
                last.then_inc(done["hT"], 1)
            for x in range(2 * B):
                b, m0 = x // 2, 3 * (x % 2)
                act.wait_ge(full["fc1"], x + 1)
                for m in range(3):
                    last = nc.scalar.activation(hid2T[:, b, m0 + m, :], slot("fc1", x)[:, N * m:N * (m + 1)],
                                                ACT.Gelu, bias=col("fc1_b", m0 + m))
                last.then_inc(done["fc1"], 1)
            for b in range(B):
                act.wait_ge(full["outT"], b + 1)
                nc.scalar.copy(xT[:, b, :, :],
                               slot("outT", b)[0:EH, 0:2 * N].rearrange("p (c n) -> p c n", c=2)
                               ).then_inc(done["outT"], 1)
            for b in range(B):
                act.wait_ge(full["selT"], b + 1)
                nc.scalar.copy(xT[:, b, :, :],
                               slot("selT", b)[0:EH, 0:2 * N].rearrange("p (c n) -> p c n", c=2)
                               ).then_inc(done["selT"], 1)

        @block.vector
        def _(dve):
            def norm_stats(k, b, src):
                for t in range(TPB):
                    last = nc.vector.bn_stats(stats[:, TPB * b + t, :], src[:, TPB * b + t, :])
                last.then_inc(ln_stats, 1)
                dve.wait_ge(ln_stats, k)
                nc.vector.memset(pause[:, :], 0.0)
                for t in range(TPB):
                    last = nc.vector.bn_aggr(moments[:, TPB * b + t, :], stats[:, TPB * b + t, :])
                last.then_inc(ln_moments, 1)

            def normalise(k, b, dst, src):
                dve.wait_ge(ln_rstd, k)
                for t in range(TPB * b, TPB * (b + 1)):
                    last = nc.vector.tensor_scalar(dst[:, t, :], src[:, t, :], moments[:, t, 0:1], rstd[:, t:t + 1],
                                                   ALU.subtract, ALU.mult)
                last.then_inc(normed, 1)

            for b in range(B):
                dve.wait_ge(full["embed"], b + 1)
                nc.vector.tensor_copy(xs[:, tiles(b), :],
                                      slot("embed", b)[:, 0:TPB * D].rearrange("p (t d) -> p t d", t=TPB)
                                      ).then_inc(done["embed"], 1)
                dve.wait_ge(done["embed"], b + 1)
                norm_stats(b + 1, b, xs)
                if b > 0:
                    normalise(b, b - 1, nrm[:, :, 0:D], xs)
            normalise(B, B - 1, nrm[:, :, 0:D], xs)
            dve.wait_ge(ctxT_zeroed, 1)
            dve.wait_ge(sel_in, 16)
            nc.vector.tensor_copy(selr.rearrange("p v k m -> p (v k m)"), sel_f32).then_inc(sel_cast, 1)

            with dve.Fori(0, L) as i:
                for b in range(B):
                    dve.wait_ge(full["k"], i * B + (b + 1))
                    nc.vector.tensor_reduce(nkmax[:, b, :], slot("k", b).rearrange("p (a n) -> p a n", a=PAIRS), X,
                                            ALU.max, negate=True).then_inc(nkmax_set, 1)
                for b in range(B):
                    dve.wait_ge(full["q"], i * B + (b + 1))
                    q = slot("q", b).rearrange("p (t h d) -> p t h d", t=TPB, h=NH)
                    nc.vector.tensor_reduce(qmax[:, tiles(b), :], q, X, ALU.max).then_inc(qmax_set, 1)
                    dve.wait_ge(qmax_set, i * B + (b + 1))
                    nc.vector.tensor_tensor(qs[:, tiles(b), :, :], q,
                                            qmax[:, tiles(b), :].unsqueeze(3).broadcast_to([P, TPB, NH, DH]),
                                            ALU.subtract).then_inc(done["q"], 1)
                for b in range(B):
                    dve.wait_ge(qexp_set, i * B + (b + 1))
                    nc.vector.tensor_reduce(qsum[:, tiles(b), :], qs[:, tiles(b), :, :], X,
                                            ALU.add).then_inc(qsum_set, 1)
                    dve.wait_ge(qsum_set, i * B + (b + 1))
                    nc.vector.reciprocal(qrec[:, tiles(b), :], qsum[:, tiles(b), :]).then_inc(dve_tmp, 1)
                    dve.wait_ge(dve_tmp, i * B + (b + 1))
                    nc.vector.tensor_scalar(qrec[:, tiles(b), :], qrec[:, tiles(b), :], DH ** -0.5, None,
                                            ALU.mult).then_inc(qrec_set, 1)
                for b in range(B):
                    dve.wait_ge(full["ctx"], i * B + (b + 1))
                    c = slot("ctx", b)[:, 0:PAIRS * P].rearrange("p (a d) -> p a d", a=PAIRS)
                    nc.vector.tensor_copy(ctxT[0:DH, b, :, 0:DH], c[0:DH, :, 0:DH])
                    nc.vector.tensor_copy(ctxT[DH:P, b, :, DH:P], c[DH:P, :, DH:P]).then_inc(done["ctx"], 1)
                for b in range(B):
                    nc.vector.reciprocal(krec[:, b, :], ksum[:, b, :]).then_inc(ksum_inv, 1)
                    dve.wait_ge(ksum_inv, i * B + (b + 1))
                    dve.wait_ge(full["ctxw"], i * B + (b + 1))
                    nc.vector.tensor_tensor(ctxw[:, b, :, :],
                                            slot("ctxw", b)[:, 0:PAIRS * D].rearrange("p (a d) -> p a d", a=PAIRS),
                                            krec[:, b, :].unsqueeze(2).broadcast_to([P, PAIRS, D]),
                                            ALU.mult).then_inc(done["ctxw"], 1)
                for name, added, k0 in (("att", attbias_added, B), ("ff2", ffbias_added, 2 * B)):
                    for b in range(B):
                        dve.wait_ge(added, i * B + (b + 1))
                        dve.wait_ge(full[name], i * B + (b + 1))
                        nc.vector.tensor_tensor(xs[:, tiles(b), :],
                                                slot(name, b)[:, 0:TPB * D].rearrange("p (t d) -> p t d", t=TPB),
                                                xs[:, tiles(b), :], ALU.add).then_inc(done[name], 1)
                        dve.wait_ge(done[name], i * B + (b + 1))
                        norm_stats(i * (2 * B) + (k0 + b + 1), b, xs)
                        if b > 0:
                            normalise(i * (2 * B) + (k0 + b), b - 1, nrm[:, :, 0:D], xs)
                    normalise(i * (2 * B) + (k0 + B), B - 1, nrm[:, :, 0:D], xs)

            k0 = B * (2 * L + 1)
            for b in range(B):
                dve.wait_ge(full["head"], b + 1)
                nc.vector.tensor_tensor(hs[:, tiles(b), :],
                                        slot("head", b)[:, :].rearrange("p (t f) -> p t f", t=TPB)[:, :, 0:E],
                                        row("head_b"), ALU.add).then_inc(done["head"], 1)
                dve.wait_ge(done["head"], b + 1)
                norm_stats(k0 + b + 1, b, hs)
                if b > 0:
                    normalise(k0 + b, b - 1, nrm, hs)
            normalise(k0 + B, B - 1, nrm, hs)


            def split_qk(a, b):
                name = a + ".qk"
                before_this = b + (B if a == "a2" else 0)
                dve.wait_ge(full[name], b + 1)
                if before_this > 0:
                    dve.wait_ge(parts_set, before_this)
                    if b > 0:
                        dve.wait_ge(full[a + ".rep"], 3 * b)
                nc.vector.tensor_tensor(qkf, slot(name, b)[:, 0:G * N].rearrange("p (g n) -> p g n", g=G),
                                        cols_of("qkb" + a[1]).unsqueeze(2).broadcast_to([P, G, N]),
                                        ALU.add).then_inc(done[name], 1)
                dve.wait_ge(done[name], b + 1)
                nc.vector.tensor_copy(qk_parts[:, 0, :, :], qkf).then_inc(hi_set, 1)
                dve.wait_ge(hi_set, before_this + 1)
                nc.vector.tensor_tensor(qk_parts[:, 1, :, :], qkf, qk_parts[:, 0, :, :].bitcast(f32),
                                        ALU.subtract).then_inc(parts_set, 1)

            def v_bias(a, b):
                dve.wait_ge(full[a + ".v"], b + 1)
                at = ROW["bv" + a[1]][0]
                for t in range(TPB):
                    last = nc.vector.tensor_tensor(
                        av[:, TPB * b + t, :, 0:AD],
                        slot(a + ".v", b)[:, 512 * t:512 * t + E].rearrange("p (h e) -> p h e", h=AH),
                        rowp[:, at:at + E].rearrange("p (h e) -> p h e", h=AH), ALU.add)
                last.then_inc(done[a + ".v"], 1)

            def negative_max(a, part, u, b, dst, ready):
                k = unit(part, u, b)
                dve.wait_ge(full[a + "." + part], k + 1)
                nc.vector.tensor_reduce(dst[:, b, u // G, 4 * (u % G):4 * (u % G) + 4].rearrange("p (x r) -> p r x", x=2),
                                        slot(a + "." + part, k).rearrange("p (r x n) -> p r x n", r=2, x=2), X,
                                        ALU.max, negate=True).then_inc(ready, 1)

            def context_out(a, b):
                dve.wait_ge(full[a + ".pv"], b + 1)
                nc.vector.tensor_copy(actxT[:, b, :, :],
                                      slot(a + ".pv", b)[:, 0:G * N].rearrange("p (g n) -> p g n", g=G)
                                      ).then_inc(done[a + ".pv"], 1)

            dve.wait_ge(av_zeroed, 1)
            for part, u, b in A1:
                if part == "qk":
                    split_qk("a1", b)
                elif part == "v":
                    v_bias("a1", b)
                elif part == "rep":
                    k = unit("rep", u, b)
                    dve.wait_ge(full["a1.rep"], k + 1)
                    nc.vector.tensor_copy(qk_wide[:, b % 2, 4 * u:4 * u + 4, :],
                                          slot("a1.rep", k).rearrange("p (a n) -> p a n", a=4)
                                          ).then_inc(done["a1.rep"], 1)
                elif part == "s":
                    negative_max("a1", "s", u, b, smax, smax_set)
                elif part == "scale":
                    dve.wait_ge(done["a1.s"], 6 * (b + 1))
                    nc.vector.reciprocal(srec[:, b, :, :], ssum[:, b, :, :]).then_inc(srec_set, 1)
                    dve.wait_ge(srec_set, b + 1)
                    nc.vector.tensor_tensor(
                        av[:, tiles(b), :, 0:AD], av[:, tiles(b), :, 0:AD],
                        srec[:, b, :, :].unsqueeze(3).broadcast_to([P, TPB, AH, AD]), ALU.mult).then_inc(av_set, 1)
                elif part == "pvout":
                    context_out("a1", b)
                elif part == "o":
                    dve.wait_ge(hbias_added, b + 1)
                    dve.wait_ge(full["a1.o"], b + 1)
                    nc.vector.tensor_tensor(hs[:, tiles(b), :],
                                            slot("a1.o", b)[:, :].rearrange("p (t f) -> p t f", t=TPB)[:, :, 0:E],
                                            hs[:, tiles(b), :], ALU.add).then_inc(done["a1.o"], 1)
                    dve.wait_ge(done["a1.o"], b + 1)
                    norm_stats(k0 + B + 2 * b + 1, b, hs)
                elif part == "z":
                    normalise(k0 + B + 2 * b + 1, b, zs, hs)
                    dve.wait_ge(normed, k0 + B + 2 * b + 1)
                    norm_stats(k0 + B + 2 * b + 2, b, zs)
                elif part == "zn":
                    normalise(k0 + B + 2 * b + 2, b, nrm, zs)

            dve.wait_ge(ones_set, 1)
            dve.wait_ge(negmax_zeroed, 1)
            for part, u, b in A2:
                if part == "zT":
                    dve.wait_ge(xnormed, b + 1)
                    for c in range(2):
                        last = nc.vector.tensor_scalar(xaT[:, b, c, :], slot("a2.zT", b)[0:EH, N * c:N * (c + 1)],
                                                       col("g1", c, EH), col("b1", c, EH), ALU.mult, ALU.add)
                    last.then_inc(done["a2.zT"], 1)
                elif part == "rg":
                    for bb in range(B):
                        dve.wait_ge(done["a2.r1"], bb + 1)
                        last = nc.vector.tensor_reduce(emean[:, bb:bb + 1], eT[:, bb, 1:N], X, ALU.add)
                    last.then_inc(esum_set, 1)
                    dve.wait_ge(esum_set, 1)
                    nc.vector.tensor_scalar(emean[:, :], emean[:, :], 1.0 / (N - 1), None,
                                            ALU.mult).then_inc(emean_set, 1)
                    dve.wait_ge(full["a2.rg"], 1)
                    nc.vector.tensor_scalar(h1bias[:, :], slot("a2.rg", 0)[:, 0:B], col("o1_b"), None,
                                            ALU.add).then_inc(done["a2.rg"], 1)
                elif part == "r4":
                    dve.wait_ge(full["a2.r4"], b + 1)
                    for t in range(TPB):
                        last = nc.vector.tensor_tensor(
                            logits[:, TPB * b + t, :, :].rearrange("p k c -> p (k c)"),
                            slot("a2.r4", b)[:, 4 * t:4 * t + 4],
                            rowp[:, ROW["o3_b"][0]:ROW["o3_b"][0] + 4], ALU.add)
                    last.then_inc(done["a2.r4"], 1)
                    if b == B - 1:
                        dve.wait_ge(done["a2.r4"], B)
                        nc.vector.tensor_tensor(bits, logits[:, :, :, 1], logits[:, :, :, 0],
                                                ALU.is_gt).then_inc(bits_cmp, 1)
                        dve.wait_ge(bits_cmp, 1)
                        for bb in range(B):
                            last = nc.vector.memset(bits[0:1, TPB * bb, :], 1.0)
                        last.then_inc(bits_set, 1)
                elif part == "qk":
                    split_qk("a2", b)
                elif part == "v":
                    v_bias("a2", b)
                elif part == "m":
                    negative_max("a2", "m", u, b, smax, done["a2.m"])
                elif part == "nm":
                    dve.wait_ge(done["a2.m"], 6 * (b + 1))
                    if b > 0:
                        dve.wait_ge(full["a2.mT"], 2 * b)
                    nc.vector.tensor_copy(negmax[:, :, :, MAXROW].bitcast(f32r),
                                          smax[:, b, :, :]).then_inc(nmhi_set, 1)
                    dve.wait_ge(nmhi_set, b + 1)
                    nc.vector.tensor_tensor(negmax[:, :, :, MAXROW + 1], smax[:, b, :, :], negmax[:, :, :, MAXROW],
                                            ALU.subtract).then_inc(nm_set, 1)
                elif part == "mT":
                    k = unit("mT", u, b)
                    dve.wait_ge(full["a2.mT"], k + 1)
                    a0, n = (0, 4) if u == 0 else (4, 2)
                    q = qk_wide[:, b % 2, a0:a0 + n, :]
                    nc.vector.tensor_tensor(q, slot("a2.mT", k)[:, 0:N * n].rearrange("p (a n) -> p a n", a=n),
                                            q.bitcast(f32), ALU.add).then_inc(done["a2.mT"], 1)
                elif part == "pvout":
                    context_out("a2", b)
                elif part == "cT":
                    dve.wait_ge(full["a2.cT"], b + 1)
                    for t in range(TPB):
                        c = slot("a2.cT", b)[:, 512 * t:512 * t + G * P].rearrange("p (h e) -> p h e", h=AH)
                        last = nc.vector.reciprocal(crec[:, TPB * b + t, :], c[:, :, SUMROW])
                    last.then_inc(crec_set, 1)
                    dve.wait_ge(crec_set, b + 1)
                    for t in range(TPB):
                        c = slot("a2.cT", b)[:, 512 * t:512 * t + G * P].rearrange("p (h e) -> p h e", h=AH)
                        last = nc.vector.tensor_tensor(
                            catt[:, TPB * b + t, :].rearrange("p (h e) -> p h e", h=AH), c[:, :, 0:AD],
                            crec[:, TPB * b + t, :].unsqueeze(2).broadcast_to([P, AH, AD]), ALU.mult)
                    last.then_inc(done["a2.cT"], 1)
                elif part == "o":
                    dve.wait_ge(full["a2.o"], b + 1)
                    nc.vector.tensor_tensor(os_[:, tiles(b), :],
                                            slot("a2.o", b)[:, :].rearrange("p (t f) -> p t f", t=TPB)[:, :, 0:E],
                                            row("bo2"), ALU.add).then_inc(done["a2.o"], 1)
                    dve.wait_ge(done["a2.o"], b + 1)
                    for t in range(TPB * b, TPB * (b + 1)):
                        last = nc.vector.scalar_tensor_tensor(out=os_[:, t, :], in0=os_[:, t, :],
                                                              scalar=bits[:, t, 0:1], in1=zs[:, t, :],
                                                              op0=ALU.mult, op1=ALU.add)
                    last.then_inc(dve_tmp, 1)
                    dve.wait_ge(dve_tmp, L * B + b + 1)
                    norm_stats(k0 + 3 * B + b + 1, b, os_)
                elif part == "hn":
                    normalise(k0 + 3 * B + b + 1, b, nrm, os_)
            for b in range(B):
                dve.wait_ge(full["fc2"], b + 1)
                nc.vector.tensor_tensor(zs[:, tiles(b), :],
                                        slot("fc2", b)[:, :].rearrange("p (t f) -> p t f", t=TPB)[:, :, 0:E],
                                        row("fc2_b"), ALU.add).then_inc(dve_tmp, 1)
                dve.wait_ge(dve_tmp, L * B + B + b + 1)
                for t in range(TPB * b, TPB * (b + 1)):
                    last = nc.vector.scalar_tensor_tensor(out=os_[:, t, :], in0=zs[:, t, :], scalar=bits[:, t, 1:2],
                                                          in1=os_[:, t, :], op0=ALU.mult, op1=ALU.add)
                last.then_inc(done["fc2"], 1)
            dve.wait_ge(sel_set, 1)
            for b in range(B):
                dve.wait_ge(full["down"], b + 1)
                for t in range(TPB):
                    last = nc.vector.tensor_tensor(
                        nrm[:, TPB * b + t, :].rearrange("p (k r) -> p k r", k=NA),
                        slot("down", b)[:, 512 * t:512 * t + E].rearrange("p (k r) -> p k r", k=NA),
                        sel[:, TPB * b + t, :].unsqueeze(2).broadcast_to([P, NA, E // NA]), ALU.mult)
                last.then_inc(done["down"], 1)
            for b in range(B):
                dve.wait_ge(full["up"], b + 1)
                dve.wait_ge(hout_set, b + 1)
                nc.vector.tensor_tensor(os_[:, tiles(b), :],
                                        slot("up", b)[:, :].rearrange("p (t f) -> p t f", t=TPB)[:, :, 0:E],
                                        hs[:, tiles(b), :], ALU.add).then_inc(result_set, 1)

        @block.tensor
        def _(pe):
            mm, tr = nc.tensor.matmul, nc.tensor.transpose

            def patch_products(h, ks):
                for k in ks:
                    if h == 0 and k % KG == 0:
                        pe.wait_ge(first_in[k // KG], 32)
                    if h == 1 and k % (KC // 2) == 0:
                        pe.wait_ge(second_in[k // (KC // 2)], 16)
                    last = mm(slot("conv", h)[:, 0:512], conv_w[:, k, :], image[:, h, k, :], start=(k == 0),
                              stop=(k == KC - 1))
                return last

            def embedding_tokens(b):
                s = take(pe, "embed", b)
                pe.wait_ge(done["conv"], b // 2 + 1)
                for t in range(TPB):
                    at = N * b + P * t
                    last = tr(s[:, P * t:P * (t + 1)], embT[:, at:at + P], ident[:, :])
                last.then_inc(full["embed"], 1)

            patch_products(0, range(KC)).then_inc(full["conv"], 1)
            patch_products(1, range(KC // 2))
            pe.wait_ge(ident_in, 16)
            embedding_tokens(0)
            embedding_tokens(1)
            patch_products(1, range(KC // 2, KC)).then_inc(full["conv"], 1)
            embedding_tokens(2)
            embedding_tokens(3)

            def norm_128(b, s, name):
                for t in range(TPB):
                    last = tr(s[:, P * t:P * (t + 1)], nrm[:, TPB * b + t, 0:D], ident[:, :])
                last.then_inc(full[name], 1)

            with pe.Fori(0, L) as i:
                for name, b in LN1K:
                    s = take(pe, name, b, i, "ln1T" if name == "k" else None)
                    if name == "ln1T":
                        pe.wait_ge(normed, i * (2 * B) + (b + 1))
                        norm_128(b, s, "ln1T")
                    else:
                        if b == 0:
                            pe.wait_ge(qkv_in, i * 16 + 16)
                        for a in range(PAIRS):
                            at = INNER + P * a
                            last = mm(s[:, N * a:N * (a + 1)], w_qkv[:, at:at + P], yT[:, b, :], start=True,
                                      stop=True)
                        last.then_inc(full["k"], 1)
                for name, at in (("q", 0), ("v", 2 * INNER)):
                    for b in range(B):
                        s = take(pe, name, b, i)
                        for t in range(TPB):
                            last = mm(s[:, INNER * t:INNER * (t + 1)], yT[:, b, P * t:P * (t + 1)],
                                      w_qkv[:, at:at + INNER], start=True, stop=True)
                        last.then_inc(full[name], 1)
                for b in range(B):
                    s = take(pe, "kT", b, i)
                    pe.wait_ge(done["k"], i * B + (b + 1))
                    for t in range(TPB):
                        for a in range(PAIRS):
                            at = INNER * t + P * a
                            last = tr(s[:, at:at + P], ekT[:, b, a, P * t:P * (t + 1)], ident[:, :])
                    last.then_inc(full["kT"], 1)
                for b in range(B):
                    s = take(pe, "ctx", b, i)
                    pe.wait_ge(done["v"], i * B + (b + 1))
                    pe.wait_ge(done["kT"], i * B + (b + 1))
                    for a in range(PAIRS):
                        for t in range(TPB):
                            f = slice(P * a, P * (a + 1))
                            last = mm(s[:, f], vv[:, TPB * b + t, f], ek[:, TPB * b + t, f], start=(t == 0),
                                      stop=(t == TPB - 1))
                    last.then_inc(full["ctx"], 1)
                for b in range(B):
                    s = take(pe, "qT", b, i)
                    pe.wait_ge(qs_set, i * B + (b + 1))
                    for a in range(PAIRS):
                        for t in range(TPB):
                            q = qs[:, TPB * b + t, 2 * a:2 * a + 2, :].rearrange("p h d -> p (h d)")
                            at = N * a + P * t
                            last = tr(s[:, at:at + P], q, ident[:, :])
                    last.then_inc(full["qT"], 1)
                pe.wait_ge(out_in, i * 32 + 16)
                for b in range(B):
                    s = take(pe, "ctxw", b, i)
                    pe.wait_ge(done["ctx"], i * B + (b + 1))
                    for a in range(PAIRS):
                        last = mm(s[:, D * a:D * (a + 1)], ctxT[:, b, a, :], w_out[:, a, :], start=True, stop=True)
                    last.then_inc(full["ctxw"], 1)
                for b in range(B):
                    s = take(pe, "att", b, i)
                    pe.wait_ge(done["qT"], i * B + (b + 1))
                    pe.wait_ge(done["ctxw"], i * B + (b + 1))
                    for t in range(TPB):
                        for a in range(PAIRS):
                            last = mm(s[:, D * t:D * (t + 1)], qT[:, b, a, P * t:P * (t + 1)], ctxw[:, b, a, :],
                                      start=(a == 0), stop=(a == PAIRS - 1))
                    last.then_inc(full["att"], 1)
                for name, b in LN2F:
                    s = take(pe, name, b, i, "ln2T" if name == "ff1" else None)
                    if name == "ln2T":
                        pe.wait_ge(normed, i * (2 * B) + (B + b + 1))
                        norm_128(b, s, "ln2T")
                    else:
                        if b == 0:
                            pe.wait_ge(ff1_in, i * 16 + 16)
                        for m in range(PAIRS):
                            last = mm(s[:, N * m:N * (m + 1)], w_ff1[:, P * m:P * (m + 1)], yT[:, b, :], start=True,
                                      stop=True)
                        last.then_inc(full["ff1"], 1)
                pe.wait_ge(ff2_in, i * 32 + 16)
                for b in range(B):
                    s = take(pe, "ff2", b, i, "ff1")
                    for t in range(TPB):
                        for m in range(PAIRS):
                            last = mm(s[:, D * t:D * (t + 1)], hidT[:, b, m, P * t:P * (t + 1)], w_ff2[:, m, :],
                                      start=(m == 0), stop=(m == PAIRS - 1))
                    last.then_inc(full["ff2"], 1)

            k0 = B * (2 * L + 1)
            for b in range(B):
                s = take(pe, "lnfT", b)
                pe.wait_ge(normed, 2 * L * B + b + 1)
                norm_128(b, s, "lnfT")
            pe.wait_ge(a1_in, 48)
            for b in range(B):
                s = take(pe, "head", b)
                pe.wait_ge(done["lnfT"], b + 1)
                for t in range(TPB):
                    last = mm(s[:, 512 * t:512 * t + E], yT[:, b, P * t:P * (t + 1)], headw[:, :], start=True,
                              stop=True)
                last.then_inc(full["head"], 1)

            def transposed(name, b, src):
                s = take(pe, name, b)
                for c in range(2):
                    for t in range(TPB):
                        at = N * c + P * t
                        last = tr(s[0:EH, at:at + P], src[:, TPB * b + t, EH * c:EH * (c + 1)], ident[:, :])
                last.then_inc(full[name], 1)

            def features_out(name, b, w, groups, src):
                s = take(pe, name, b)
                for g in range(groups):
                    for c in range(2):
                        last = mm(s[:, N * g:N * (g + 1)], w[:, c, P * g:P * (g + 1)], src[:, b, c, :],
                                  start=(c == 0), stop=(c == 1))
                last.then_inc(full[name], 1)

            def tokens_out(name, b, w, src):
                s = take(pe, name, b)
                for t in range(TPB):
                    for c in range(2):
                        last = mm(s[:, 512 * t:512 * t + E], src[:, b, c, P * t:P * (t + 1)], w[:, c, :],
                                  start=(c == 0), stop=(c == 1))
                last.then_inc(full[name], 1)

            def spread_pairs(a, u, b):
                k = unit("rep", u, b)
                s = take(pe, a + ".rep", k)
                pe.wait_ge(parts_set, b + 1 + (B if a == "a2" else 0))
                for x in range(4):
                    kind = 0 if 4 * u + x < AP2 else 2
                    at = slice(64 * (x // 2), 64 * (x // 2) + 64)
                    for o in range(2):
                        last = mm(s[:, N * x:N * (x + 1)], selr[at, x % 2, kind + o, :], qk_parts[at, o, u, :],
                                  start=(o == 0), stop=(o == 1))
                last.then_inc(full[a + ".rep"], 1)

            def scores(name, u, b, stationary, moving):
                s = take(pe, name, 6 * b + u)
                t, g = u // G, u % G
                for x in range(2):
                    for r in range(2):
                        rows_ = slice(64 * r, 64 * r + 64)
                        at = 512 * r + N * x
                        last = mm(s[:, at:at + N], qk_wide[rows_, b % 2, stationary + 2 * g + x, P * t:P * (t + 1)],
                                  qk_wide[rows_, b % 2, moving + 2 * g + x, :], start=True, stop=True)
                last.then_inc(full[name], 1)

            def context(a, b):
                s = take(pe, a + ".pv", b)
                pe.wait_ge(done[a + ".s"], 6 * (b + 1))
                for g in range(G):
                    for t in range(TPB):
                        for j in range(4):
                            last = mm(s[32 * j:32 * j + 32, N * g:N * (g + 1)], av[:, TPB * b + t, 4 * g + j, :],
                                      probs[:, b % 2, G * t + g, j % 2, j // 2, :], start=(t == 0),
                                      stop=(t == TPB - 1))
                last.then_inc(full[a + ".pv"], 1)

            QUERIES, KEYS = 0, AP2
            pe.wait_ge(sel_cast, 1)
            for part, u, b in A1:
                if part == "xT":
                    pe.wait_ge(normed, k0 + b + 1)
                    transposed("a1.xT", b, nrm)
                elif part == "qk":
                    pe.wait_ge(done["a1.xT"], b + 1)
                    features_out("a1.qk", b, a_wqkv[0], G, xT)
                elif part == "v":
                    tokens_out("a1.v", b, a_wqkv[0][:, :, 2 * E:3 * E], xT)
                elif part == "rep":
                    spread_pairs("a1", u, b)
                elif part == "s":
                    pe.wait_ge(done["a1.rep"], 3 * (b + 1))
                    scores("a1.s", u, b, KEYS, QUERIES)
                elif part == "pv":
                    pe.wait_ge(av_set, b + 1)
                    context("a1", b)
                elif part == "o":
                    s = take(pe, "a1.o", b)
                    pe.wait_ge(done["a1.pv"], b + 1)
                    for t in range(TPB):
                        for g in range(G):
                            last = mm(s[:, 512 * t:512 * t + E], actxT[:, b, g, P * t:P * (t + 1)], a1_wo[:, g, :],
                                      start=(g == 0), stop=(g == G - 1))
                    last.then_inc(full["a1.o"], 1)

            pe.wait_ge(a2_in, 64)
            for part, u, b in A2:
                if part == "zT":
                    pe.wait_ge(normed, k0 + B + 2 * (b + 1))
                    transposed("a2.zT", b, nrm)
                elif part == "r1":
                    pe.wait_ge(xnormed, b + 1)
                    features_out("a2.r1", b, rinw, 1, xT)
                elif part == "rg":
                    s = take(pe, "a2.rg", 0)
                    pe.wait_ge(emean_set, 1)
                    mm(s[:, 0:B], row_[:, RH:2 * RH], emean[:, :], start=True, stop=True).then_inc(full["a2.rg"], 1)
                elif part == "r2":
                    s = take(pe, "a2.r2", b)
                    pe.wait_ge(done["a2.r1"], b + 1)
                    mm(s[:, 0:N], row_[:, 0:RH], eT[:, b, :], start=True, stop=True).then_inc(full["a2.r2"], 1)
                elif part == "r3":
                    s = take(pe, "a2.r3", b)
                    pe.wait_ge(done["a2.r2"], b + 1)
                    mm(s[0:RL, 0:N], row_[:, 2 * RH:2 * RH + RL], h1T[:, b, :], start=True,
                       stop=True).then_inc(full["a2.r3"], 1)
                elif part == "r4":
                    s = take(pe, "a2.r4", b)
                    pe.wait_ge(done["a2.r3"], b + 1)
                    for t in range(TPB):
                        last = mm(s[:, 4 * t:4 * t + 4], h2T[:, b, P * t:P * (t + 1)],
                                  row_[0:RL, 2 * RH + RL:2 * RH + RL + 4], start=True, stop=True)
                    last.then_inc(full["a2.r4"], 1)
                elif part == "qk":
                    pe.wait_ge(done["a2.zT"], b + 1)
                    features_out("a2.qk", b, a_wqkv[1], G, xaT)
                elif part == "v":
                    tokens_out("a2.v", b, a_wqkv[1][:, :, 2 * E:3 * E], xaT)
                elif part == "rep":
                    spread_pairs("a2", u, b)
                elif part == "m":
                    pe.wait_ge(done["a2.rep"], 3 * (b + 1))
                    scores("a2.m", u, b, QUERIES, KEYS)
                elif part == "mT":
                    k = unit("mT", u, b)
                    s = take(pe, "a2.mT", k)
                    pe.wait_ge(nm_set, b + 1)
                    for x in range(4 if u == 0 else 2):
                        for t in range(TPB):
                            at, h = N * x + P * t, 2 * (4 * u + x)
                            last = tr(s[:, at:at + P], negmax[:, t, h:h + 2, :].rearrange("p h e -> p (h e)"),
                                      ident[:, :])
                    last.then_inc(full["a2.mT"], 1)
                elif part == "s":
                    pe.wait_ge(done["a2.mT"], 2 * (b + 1))
                    scores("a2.s", u, b, KEYS, QUERIES)
                elif part == "pv":
                    pe.wait_ge(done["a2.v"], b + 1)
                    context("a2", b)
                elif part == "cT":
                    s = take(pe, "a2.cT", b)
                    pe.wait_ge(done["a2.pv"], b + 1)
                    for t in range(TPB):
                        for g in range(G):
                            at = 512 * t + P * g
                            last = tr(s[:, at:at + P], actxT[:, b, g, P * t:P * (t + 1)], ident[:, :])
                    last.then_inc(full["a2.cT"], 1)
                elif part == "nT":
                    pe.wait_ge(done["a2.cT"], b + 1)
                    transposed("a2.nT", b, catt)
                elif part == "o":
                    pe.wait_ge(done["a2.nT"], b + 1)
                    tokens_out("a2.o", b, a2_wo, xT)

            for b in range(B):
                pe.wait_ge(normed, k0 + 3 * B + b + 1)
                transposed("hT", b, nrm)
            pe.wait_ge(fc_in, 32)
            for x in range(2 * B):
                b, m0 = x // 2, 3 * (x % 2)
                s = take(pe, "fc1", x)
                pe.wait_ge(done["hT"], b + 1)
                for m in range(3):
                    for c in range(2):
                        last = mm(s[:, N * m:N * (m + 1)], fc1w[:, c, P * (m0 + m):P * (m0 + m + 1)], xT[:, b, c, :],
                                  start=(c == 0), stop=(c == 1))
                last.then_inc(full["fc1"], 1)
            for b in range(B):
                s = take(pe, "fc2", b)
                pe.wait_ge(done["fc1"], 2 * (b + 1))
                for t in range(TPB):
                    for m in range(HM):
                        last = mm(s[:, 512 * t:512 * t + E], hid2T[:, b, m, P * t:P * (t + 1)], fc2w[:, m, :],
                                  start=(m == 0), stop=(m == HM - 1))
                last.then_inc(full["fc2"], 1)
            for b in range(B):
                pe.wait_ge(done["fc2"], b + 1)
                transposed("outT", b, os_)
            pe.wait_ge(ad_in, 32)
            for b in range(B):
                pe.wait_ge(done["outT"], b + 1)
                tokens_out("down", b, downw, xT)
            for b in range(B):
                pe.wait_ge(done["down"], b + 1)
                transposed("selT", b, nrm)
            for b in range(B):
                pe.wait_ge(done["selT"], b + 1)
                tokens_out("up", b, upw, xT)


def spread(w):
    w = w.reshape(w.shape[:-1] + (AH, AD))
    wide = np.zeros(w.shape[:-1] + (32,), w.dtype)
    wide[..., :AD] = w
    return wide.reshape(w.shape[:-2] + (AH * 32,))


def halves(w):
    return np.ascontiguousarray(w.reshape(2, EH, -1).transpose(1, 0, 2))


def columns(v, n):
    c = np.zeros((P, n), v.dtype)
    c[:v.size // n] = v.reshape(n, -1).T
    return c


def selector_matrices():
    m = np.zeros((2, 64, 2, 4, 2, 64), np.float32)
    for kind, slots in enumerate(((0, 1), (2,), (0, 2), (1,))):
        for half in range(2):
            for head in range(2):
                for d in range(AD):
                    for s in slots:
                        m[:, 32 * half + AD * head + d, half, kind, head, AD * s + d] = AD ** -0.5 if kind < 2 else 1.0
    return m.reshape(P, 2 * 4 * P)


def kernel(**inputs):
    import concourse.bacc as bacc
    from concourse.bass_utils import run_bass_kernel_spmd

    v = {k: np.asarray(a) for k, a in inputs.items()}
    t = {k[len("L0_tok_"):]: a for k, a in v.items() if k.startswith("L0_tok_")}
    a = {k[len("L0_attn_"):]: x for k, x in v.items() if k.startswith("L0_attn_")}
    f = {k[len("L0_ffn_"):]: x for k, x in v.items() if k.startswith("L0_ffn_")}
    hp = IMG // PATCH
    im = v["x"].reshape(B, C_IN, hp, PATCH, hp, PATCH).transpose(1, 3, 5, 0, 2, 4).reshape(KC, P, 2, 512)
    im = im.transpose(2, 1, 0, 3)
    cw = t["conv_w"].reshape(D, KC // KG, KG, P).transpose(1, 3, 2, 0)
    wl = np.concatenate([
        t["qkv_w"],
        t["out_w"].reshape(L, PAIRS, P, D).transpose(0, 2, 1, 3).reshape(L, P, INNER),
        t["ff1_w"],
        t["ff2_w"].reshape(L, PAIRS, P, D).transpose(0, 2, 1, 3).reshape(L, P, M)], axis=2)
    lcols = np.stack([np.concatenate([columns(t["ln1_g"][i], 1), columns(t["ln1_b"][i], 1), columns(t["ln2_g"][i], 1),
                                      columns(t["ln2_b"][i], 1), columns(t["ff1_b"][i], PAIRS)], axis=1)
                      for i in range(L)])
    lrows = np.concatenate([t["out_b"], t["ff2_b"]], axis=1)

    def both(q, k):
        return np.concatenate([q.reshape(-1), k.reshape(-1)])

    max_rows = np.zeros((2, 64), np.float32)
    max_rows[:, MAXROW:MAXROW + 2] = 1.0
    col_values = {"conv_b": t["conv_b"], "lnf_g": t["lnf_g"], "lnf_b": t["lnf_b"], "qkb1": both(a["bq"], a["bk"]),
                  "r_g": f["r_ln_g"], "r_b": f["r_ln_b"], "g1": f["ln1_g"],
                  "b1": f["ln1_b"], "g2": f["ln2_g"], "b2": f["ln2_b"], "r_in_b": f["r_in_b"], "o1_b": f["r_o1_b"],
                  "o2_b": f["r_o2_b"], "qkb2": both(f["bq"], f["bk"]), "maxrows": max_rows.reshape(-1),
                  "fc1_b": f["fc1_b"]}
    cols = np.concatenate([columns(col_values[n], COL[n][1]) for n in COL], axis=1)
    row_values = {"head_b": t["head_b"], "bv1": a["bv"].reshape(-1), "bo1": a["bo"], "bv2": f["bv"], "bo2": f["bo"],
                  "fc2_b": f["fc2_b"], "o3_b": f["r_o3_b"]}
    rows = np.concatenate([row_values[n] for n in ROW])
    w_a1 = halves(np.concatenate([a[n].transpose(1, 0, 2).reshape(E, E) for n in ("Wq", "Wk", "Wv")], axis=1))
    wo_a1 = spread(a["Wo"].T).T.reshape(G, P, E).transpose(1, 0, 2)
    w_a2 = halves(np.concatenate([f["wq"].T, f["wk"].T, f["wv"].T], axis=1))
    w_ro = np.concatenate([f["r_o1_w"].T[:RH], f["r_o1_w"].T[RH:], f["r_o2_w"].T,
                           np.concatenate([f["r_o3_w"].T, np.zeros((RH - RL, 4), np.float32)])], axis=1)
    arrays = {
        "im0": im[0].reshape(P, KC // KG, KG, 512).transpose(1, 0, 2, 3),
        "im1": im[1].reshape(P, 2, KC // 2, 512).transpose(1, 0, 2, 3), "cw": cw, "wl": wl, "lcols": lcols, "lrows": lrows, "cols": cols, "rows": rows,
        "ident": np.eye(P, dtype=np.float32), "selectors": selector_matrices(), "w_head": t["head_w"], "w_a1": w_a1, "wo_a1": wo_a1, "w_a2": w_a2,
        "wo_a2": halves(f["wo"].T), "w_r": halves(f["r_in_w"].T), "w_ro": w_ro, "w_fc1": halves(f["fc1_w"].T),
        "w_fc2": f["fc2_w"].T.reshape(HM, P, E).transpose(1, 0, 2), "w_down": halves(f["lra_down"].reshape(E, E).T),
        "w_up": halves(f["lra_up"].transpose(0, 2, 1).reshape(E, E))}
    arrays = {k: np.ascontiguousarray(x) for k, x in arrays.items()}
    nc = bacc.Bacc("TRN2", target_bir_lowering=False, num_devices=1)
    args = [nc.dram_tensor(k, x.shape, mybir.dt.from_np(x.dtype), kind="ExternalInput").ap()
            for k, x in arrays.items()]
    args.append(nc.dram_tensor("out", (B, P, TPB, E), mybir.dt.float32, kind="ExternalOutput").ap())
    build(nc, *args)
    r = run_bass_kernel_spmd(nc, [arrays], core_ids=[0])
    got = r.results[0]["out"]
    return np.ascontiguousarray(got.transpose(0, 2, 1, 3)).reshape(B, N, E)
```

```python
import numpy as np
import concourse.bass as bass
from concourse import mybir
from contextlib import ExitStack

B, C_IN, IMG, PATCH = 4, 32, 128, 8
N = (IMG // PATCH) ** 2
P = 128
TPB = N // P
NT = B * TPB
D = 128
L, NH, DH, M = 2, 8, 64, 512
INNER = NH * DH
PAIRS = INNER // P
KC = C_IN * PATCH * PATCH // P
KG = 2
NSECOND = 4
E = 192
EH = E // 2
AH, AD = 12, 16
G = 3
AP2 = AH // 2
HID = 768
HM = HID // P
RH, RL, NA = 128, 64, 3
EPS = 1e-5
SUMROW = 16
MAXROW = 48

COL = {}
_at = 0
for _name, _n in [("conv_b", 1), ("lnf_g", 1), ("lnf_b", 1), ("qkb1", G), ("r_g", 2), ("r_b", 2),
                  ("g1", 2), ("b1", 2), ("g2", 2), ("b2", 2), ("r_in_b", 1), ("o1_b", 1), ("o2_b", 1),
                  ("qkb2", G), ("maxrows", 1), ("fc1_b", HM)]:
    COL[_name] = (_at, _n)
    _at += _n
NCOL = _at
LCOL = {"ln1_g": (0, 1), "ln1_b": (1, 1), "ln2_g": (2, 1), "ln2_b": (3, 1), "ff1_b": (4, PAIRS)}
NLCOL = 4 + PAIRS
ROW = {}
_at = 0
for _name, _n in [("head_b", E), ("bv1", E), ("bo1", E), ("bv2", E), ("bo2", E), ("fc2_b", E), ("o3_b", 4)]:
    ROW[_name] = (_at, _n)
    _at += _n
NROW = _at

PRE = [("conv", 0), ("conv", 1)] + [("embed", b) for b in range(B)]
QKV = [("ln1T", 0), ("ln1T", 1), ("k", 0), ("ln1T", 2), ("q", 0), ("k", 1), ("ln1T", 3), ("v", 0), ("q", 1), ("k", 2),
       ("v", 1), ("q", 2), ("k", 3), ("v", 2), ("q", 3), ("v", 3)]
LN2F = [("ln2T", 0), ("ln2T", 1), ("ff1", 0), ("ln2T", 2), ("ff1", 1), ("ln2T", 3), ("ff2", 0), ("ff1", 2), ("ff2", 1),
        ("ff1", 3), ("ff2", 2), ("ff2", 3)]
QKV_SCALAR = [("ln1T", 0), ("ln1T", 1), ("k", 0), ("ln1T", 2), ("k", 1), ("ln1T", 3), ("q", 0), ("v", 0), ("k", 2),
              ("q", 1), ("v", 1), ("k", 3), ("q", 2), ("v", 2), ("q", 3), ("v", 3)]
BODY = QKV + [(s, b) for s in ("kT", "ctx", "qT", "ctxw", "att") for b in range(B)] + LN2F

INSTANCES = [("a1", 0), ("a1", 1), ("a1", 2), ("a2", 0), ("a1", 3), ("a2", 1), ("a2", 2), ("a2", 3)]
UNITS = {"at.s": 6, "a2.m": 6, "a1.rep": 3, "a2.rep": 3, "a2.mT": 2, "fc1": 2}
NO_UNIT = ("an", "scale", "z", "zn", "pvout", "nm", "hn")


ORDER_TEXT = """
lnfT:0 head:0 lnfT:1 head:1 an:0 lnfT:2 head:2 lnfT:3 a1.xT:0 an:1 an:2 at.qk:0 at.v:0 a1.xT:1 a1.rep:0:0
a1.rep:0:1 a1.rep:0:2 at.v:1 at.s:0:0 at.s:0:1 at.s:0:2 at.qk:1 at.s:0:3 at.s:0:4 a1.rep:1:0 a1.rep:1:1 at.s:0:5
a1.rep:1:2 head:3 a1.xT:2 scale:0 at.s:1:0 at.s:1:1 at.s:1:2 at.qk:2 at.s:1:3 at.pv:0 at.s:1:4 pvout:0
a1.rep:2:0 at.s:1:5 a1.rep:2:1 a1.rep:2:2 a1.o:0 scale:1 at.s:2:0 z:0 at.s:2:1 at.pv:1 pvout:1 at.s:2:2 zn:0
an:3 a1.o:1 a2.zT:0 at.s:2:3 at.s:2:4 at.s:2:5 at.qk:3 at.v:2 at.v:3 z:1 a2.r1:0 a2.rep:0:0 a2.rep:0:1
a2.rep:0:2 a2.rg:0 a2.r2:0 a1.xT:3 scale:2 zn:1 a2.m:0:0 a2.m:0:1 a2.m:0:2 a2.m:0:3 at.pv:2 a2.r3:0 pvout:2
a2.m:0:4 a2.m:0:5 a2.zT:1 nm:0 at.qk:4 a2.r1:1 a2.mT:0:0 a2.mT:0:1 a1.o:2 a1.rep:3:0 at.s:3:0 at.s:3:1
a1.rep:3:1 at.s:3:2 at.s:3:3 at.s:3:4 z:2 a1.rep:3:2 zn:2 at.v:4 at.s:3:5 at.s:4:0 at.s:4:1 at.s:4:2 at.qk:5
at.pv:3 pvout:3 a2.zT:2 a2.rep:1:0 a2.cT:0 a2.rep:1:1 a2.r4:0 a2.rep:1:2 a2.nT:0 a2.rg:1 at.s:4:3 at.s:4:4
at.s:4:5 at.qk:6 scale:4 a2.r2:1 a2.o:0 a2.m:1:0 at.v:5 at.pv:4 a2.r3:1 pvout:4 a2.m:1:1 a2.rep:2:0 hn:0 a1.o:3
a2.rep:2:1 a2.m:1:2 hT:0 a2.m:1:3 a2.rep:2:2 z:3 a2.m:1:4 a2.m:1:5 nm:1 fc1:0:0 a2.r4:1 a2.m:2:0 fc1:0:1 zn:3
a2.mT:1:0 a2.mT:1:1 a2.m:2:1 a2.zT:3 fc2:0 a2.m:2:2 a2.r1:2 at.s:5:0 at.qk:7 outT:0 at.s:5:1 at.s:5:2 a2.m:2:3
at.s:5:3 down:0 at.s:5:4 a2.m:2:4 at.s:5:5 a2.m:2:5 a2.rep:3:0 nm:2 a2.rep:3:1 a2.rep:3:2 a2.rg:2 a2.mT:2:0
a2.mT:2:1 a2.m:3:0 at.pv:5 at.s:6:0 pvout:5 a2.m:3:1 at.s:6:1 a2.m:3:2 at.s:6:2 a2.cT:1 at.s:6:3 at.s:6:4
a2.m:3:3 at.v:6 at.s:6:5 a2.nT:1 a2.m:3:4 a2.m:3:5 a2.r2:2 a2.o:1 at.pv:6 a2.r3:2 nm:3 pvout:6 a2.r1:3 hn:1
a2.mT:3:0 hT:1 a2.mT:3:1 selT:0 a2.cT:2 at.s:7:0 at.v:7 a2.nT:2 a2.r4:2 at.s:7:1 at.s:7:2 at.s:7:3 a2.o:2
at.s:7:4 at.s:7:5 fc1:1:0 a2.rg:3 a2.r2:3 hn:2 fc1:1:1 at.pv:7 hT:2 pvout:7 a2.r3:3 fc2:1 a2.cT:3 fc1:2:0
a2.nT:3 a2.r4:3 fc1:2:1 a2.o:3 hn:3 outT:1 fc2:2 hT:3 down:1 fc1:3:0 fc1:3:1 up:0 selT:1 fc2:3 outT:2 up:1
outT:3 down:2 down:3 selT:2 selT:3 up:2 up:3
"""
ORDER = [(e.split(":")[0], int((e.split(":") + ["0"])[2]), int(e.split(":")[1])) for e in ORDER_TEXT.split()]


def unit(part, u, i):
    return UNITS.get(part, 1) * i + u


def numbers(names):
    return {(part, i): n + 1 for n, (part, i) in enumerate((part, i) for part, u, i in ORDER if part in names)}


TAIL = [(part, unit(part, u, i)) for part, u, i in ORDER if part not in NO_UNIT]
NORMS = B * (2 * L + 1)
STATS_OF = numbers(("head", "a1.o", "z", "a2.o"))
NORM_OF = numbers(("an", "z", "zn", "hn"))
NSLOT = 4
DVE_NORMS = (2, 3)


def build(nc, im0, im1, cw, wl, lcols, lrows, cols, rows, ident_d, selectors, w_head, w_a1, wo_a1, w_a2, wo_a2,
          w_r, w_ro, w_fc1, w_fc2, w_down, w_up, out):
    f32, f32r = mybir.dt.float32, mybir.dt.float32r
    ALU = mybir.AluOpType
    ACT = mybir.ActivationFunctionType
    X = mybir.AxisListType.X

    ctx = ExitStack()
    with ctx:
        def sb(name, n, dtype=f32):
            return ctx.enter_context(nc.sbuf_tensor(name, [P, n], dtype))

        names = sorted({n for n, _ in PRE + BODY + TAIL})
        full = {n: ctx.enter_context(nc.semaphore("full_" + n.replace(".", "_"))) for n in names}
        done = {n: ctx.enter_context(nc.semaphore("done_" + n.replace(".", "_"))) for n in names}

        def sem(name):
            return ctx.enter_context(nc.semaphore(name))

        big = sb("big", 16384)
        mid = sb("mid", 10240)
        image = big[:, :].rearrange("p (h k t) -> p h k t", h=2, k=KC)
        ekT = big[:, 0:4096].rearrange("p (b a n) -> p b a n", b=B, a=PAIRS)
        hidT = ekT
        vv = big[:, 4096:8192].rearrange("p (t f) -> p t f", t=NT)
        qs = big[:, 8192:12288].rearrange("p (t h d) -> p t h d", t=NT, h=NH)
        qT = big[:, 12288:16384].rearrange("p (b a n) -> p b a n", b=B, a=PAIRS)
        conv_w = mid[:, 0:KC * D].rearrange("p (k d) -> p k d", k=KC)
        embT = mid[:, 8192:9216]
        ek = mid[:, 0:4096].rearrange("p (t f) -> p t f", t=NT)
        ctxT = mid[:, 4096:6144].rearrange("p (b a d) -> p b a d", b=B, a=PAIRS)
        ctxw = mid[:, 6144:8192].rearrange("p (b a d) -> p b a d", b=B, a=PAIRS)
        yT = mid[:, 9216:10240].rearrange("p (b n) -> p b n", b=B)
        probs = big[:, 0:12288].rearrange("p (z u r x n) -> p z u r x n", z=2, u=6, r=2, x=2)
        eT, h1T = big[:, 15872:16128], big[:, 16128:16384]
        xT = big[0:EH, 12288:14336].rearrange("p (b c n) -> p b c n", b=B, c=2)
        negmax = big[:, 14336:15872].rearrange("p (t h e) -> p t h e", t=TPB, h=AH)
        av = mid[:, 0:3072].rearrange("p (t h e) -> p t h e", t=NT, h=AH)
        actxT = mid[:, 3072:6144].rearrange("p (b g n) -> p b g n", b=B, g=G)
        xaT = mid[0:EH, 6144:7168].rearrange("p (z c n) -> p z c n", z=2, c=2)
        catt = mid[:, 7168:8704].rearrange("p (t f) -> p t f", t=NT)
        hid2T = mid[:, 8704:10240].rearrange("p (m n) -> p m n", m=HM)
        xs_flat = sb("xs", NT * D)
        xs = xs_flat[:, :].rearrange("p (t d) -> p t d", t=NT)
        qkf = xs_flat[:, 0:G * N].rearrange("p (g n) -> p g n", g=G)
        h2T = xs_flat[0:RL, G * N:G * N + N]
        nrm = sb("nrm", NT * E)[:, :].rearrange("p (t d) -> p t d", t=NT)
        hs = sb("hs", NT * E)[:, :].rearrange("p (t d) -> p t d", t=NT)
        zs_flat = sb("zs", NT * E)
        zs = zs_flat[:, :].rearrange("p (t d) -> p t d", t=NT)
        sel_f32 = zs_flat[:, 0:1024]
        selr = sb("selr", 1024, f32r)[:, :].rearrange("p (v k m) -> p v k m", v=2, k=4)
        qk_parts = sb("qk_parts", 2 * G * N, f32r)[:, :].rearrange("p (o g n) -> p o g n", o=2, g=G)
        wide_flat = sb("qk_wide", 2 * 2 * AP2 * N, f32r)
        qk_wide = wide_flat[:, :].rearrange("p (z a n) -> p z a n", z=2, a=2 * AP2)
        qkv_parts = wide_flat[:, 0:3072].rearrange("p (o f) -> p o f", o=2)
        ff1_parts = wide_flat[:, 3072:4096].rearrange("p (o f) -> p o f", o=2)
        y_parts = wide_flat[:, 4096:6144].rearrange("p (o b n) -> p o b n", o=2, b=B)
        os_ = sb("os", NT * E)[:, :].rearrange("p (t d) -> p t d", t=NT)
        lw = sb("lw", 3 * INNER + INNER + M + M)
        w_qkv = lw[:, 0:1536]
        w_out = lw[:, 1536:2048].rearrange("p (a d) -> p a d", a=PAIRS)
        w_ff1 = lw[:, 2048:2560]
        w_ff2 = lw[:, 2560:3072].rearrange("p (m d) -> p m d", m=PAIRS)
        lc = sb("lc", NLCOL)
        lr = sb("lr", 2 * D)
        colp = sb("colp", NCOL)
        rowp = sb("rowp", NROW)
        ident = sb("identity", P)
        headw = sb("headw", E)
        a_w = [sb(f"a{n}_w", 2 * 3 * E) for n in (1, 2)]
        a_wqkv = [w[0:EH, :].rearrange("p (c f) -> p c f", c=2) for w in a_w]
        a1_wo = sb("a1_wo", G * E)[:, :].rearrange("p (g f) -> p g f", g=G)
        a2_wo = sb("a2_wo", 2 * E)[0:EH, :].rearrange("p (c f) -> p c f", c=2)
        rinw = sb("rinw", 2 * RH)[0:EH, :].rearrange("p (c f) -> p c f", c=2)
        row_ = sb("row", 2 * RH + RL + 4)
        fc1w = lw[0:EH, 0:2 * HID].rearrange("p (c f) -> p c f", c=2)
        fc2w = lw[:, 2 * HID:2 * HID + HM * E].rearrange("p (m f) -> p m f", m=HM)
        downw = sb("downw", 2 * E)[0:EH, :].rearrange("p (c f) -> p c f", c=2)
        upw = sb("upw", 2 * E)[0:EH, :].rearrange("p (c f) -> p c f", c=2)
        stats = sb("stats", NT * 6)[:, :].rearrange("p (t s) -> p t s", t=NT)
        moments = sb("moments", NT * 2)[:, :].rearrange("p (t s) -> p t s", t=NT)
        vareps = sb("vareps", NT)
        rstd = sb("rstd", NT)
        minushalf = sb("minushalf", TPB)
        epsilon = sb("epsilon", TPB)
        pause, pool_pause, act_pause = sb("pause", 1), sb("pool_pause", TPB), sb("act_pause", TPB)
        nkmax = sb("nkmax", B * PAIRS)[:, :].rearrange("p (b a) -> p b a", b=B)
        ksum = sb("ksum", B * PAIRS)[:, :].rearrange("p (b a) -> p b a", b=B)
        krec = sb("krec", B * PAIRS)[:, :].rearrange("p (b a) -> p b a", b=B)
        qmax = sb("qmax", NT * NH)[:, :].rearrange("p (t h) -> p t h", t=NT)
        qsum = sb("qsum", NT * NH)[:, :].rearrange("p (t h) -> p t h", t=NT)
        qrec = sb("qrec", NT * NH)[:, :].rearrange("p (t h) -> p t h", t=NT)
        smax = sb("smax", 2 * B * 24)[:, :].rearrange("p (b t h) -> p b t h", b=2 * B, t=TPB)
        ssum = sb("ssum", B * 24)[:, :].rearrange("p (b t h) -> p b t h", b=B, t=TPB)
        srec = sb("srec", B * 24)[:, :].rearrange("p (b t h) -> p b t h", b=B, t=TPB)
        crec = sb("crec", NT * AH)[:, :].rearrange("p (t h) -> p t h", t=NT)
        emean = sb("emean", B)
        h1bias = sb("h1bias", B)
        logits = sb("logits", NT * 4)[:, :].rearrange("p (t k c) -> p t k c", t=NT, k=2)
        bits = sb("bits", NT * 2)[:, :].rearrange("p (t k) -> p t k", t=NT)
        nbits = sb("nbits", NT * 2)[:, :].rearrange("p (t k) -> p t k", t=NT)
        sel = sb("sel", NT * NA)[:, :].rearrange("p (t k) -> p t k", t=NT)

        psum = ctx.enter_context(nc.psum_tensor("psum", [P, NSLOT * 1024], f32))

        def col(name, k=0, n=P):
            return colp[0:n, COL[name][0] + k:COL[name][0] + k + 1]

        def cols_of(name):
            return colp[:, COL[name][0]:COL[name][0] + COL[name][1]]

        def lcol(name, k=0):
            return lc[:, LCOL[name][0] + k:LCOL[name][0] + k + 1]

        def row(name):
            r = rowp[:, ROW[name][0]:ROW[name][0] + ROW[name][1]]
            return r.unsqueeze(1).broadcast_to([P, TPB, ROW[name][1]])

        def tiles(b):
            return slice(TPB * b, TPB * (b + 1))

        place, before = {}, {}
        for seq, start in ((PRE, 0), (BODY, len(PRE)), (TAIL, len(PRE) + len(BODY))):
            for k, key in enumerate(seq):
                place[key] = (start + k) % NSLOT
                if k >= NSLOT:
                    before[key] = seq[k - NSLOT]

        def slot(name, k):
            s = place[(name, k)]
            return psum[:, 1024 * s:1024 * (s + 1)]

        def take(pe, name, k, layer=None):
            who, n = before.get((name, k), (None, 0))
            if who is not None:
                pe.wait_ge(done[who], n + 1 if layer is None else layer * B + (n + 1))
            elif (name, k) not in PRE:
                at = max(1, BODY.index((name, k)) if layer is not None else TAIL.index((name, k)))
                pe.wait_ge(ln_stats, 2 * L * B + at + 1 if layer is None else layer * (2 * B) + (at + 1))
            return slot(name, k)

        first_in = [sem(f"first_in{k}") for k in range(KC // KG)]
        second_in = [sem(f"second_in{k}") for k in range(NSECOND)]
        ident_in, params_in, rows_in = sem("ident_in"), sem("params_in"), sem("rows_in")
        qkv_in, out_in, ff1_in, ff2_in, lc_in = (sem(n) for n in ("qkv_in", "out_in", "ff1_in", "ff2_in", "lc_in"))
        a1_in, a2_in, fc_in, ad_in = (sem(n) for n in ("a1_in", "a2_in", "fc_in", "ad_in"))
        half_set, ctxT_zeroed, av_zeroed = sem("half_set"), sem("ctxT_zeroed"), sem("av_zeroed")
        ln_stats, ln_moments, ln_eps, ln_rstd, normed = (
            sem(n) for n in ("ln_stats", "ln_moments", "ln_eps", "ln_rstd", "normed"))
        attbias_added, ffbias_added = sem("attbias_added"), sem("ffbias_added")
        nkmax_set, ksum_inv = sem("nkmax_set"), sem("ksum_inv")
        qmax_set, qexp_set, qsum_set, qrec_set, qs_set = (
            sem(n) for n in ("qmax_set", "qexp_set", "qsum_set", "qrec_set", "qs_set"))
        smax_set, srec_set, av_set = sem("smax_set"), sem("srec_set"), sem("av_set")
        sel_in, sel_cast, hi_set, parts_set = sem("sel_in"), sem("sel_cast"), sem("hi_set"), sem("parts_set")
        nmhi_set, nm_set = sem("nmhi_set"), sem("nm_set")
        hbias_added, xnormed = sem("hbias_added"), sem("xnormed")
        esum_set, emean_set, logits_set, bits_set, sel_set, nb_set = (
            sem(n) for n in ("esum_set", "emean_set", "logits_set", "bits_set", "sel_set", "nb_set"))
        bits_cmp = sem("bits_cmp")
        negmax_zeroed, ones_set, crec_set = sem("negmax_zeroed"), sem("ones_set"), sem("crec_set")
        whi_set, wlo_set, ylo_set, ydve_set = sem("whi_set"), sem("wlo_set"), sem("ylo_set"), sem("ydve_set")
        qinv_set, hmix_set, ffbias2_set = sem("qinv_set"), sem("hmix_set"), sem("ffbias2_set")
        hout_set, stored = sem("hout_set"), sem("stored")

        block = ctx.enter_context(nc.Block())

        @block.sync
        def _(sp):
            for k in range(KC // KG):
                sp.dma_start(image[:, 0, KG * k:KG * (k + 1), :], im0[k]).then_inc(first_in[k], 16)
            for k in range(NSECOND):
                at = slice(KC // NSECOND * k, KC // NSECOND * (k + 1))
                sp.dma_start(image[:, 1, at, :], im1[k]).then_inc(second_in[k], 16)
            sp.dma_start(w_qkv, wl[0, :, 0:1536]).then_inc(qkv_in, 16)
            sp.dma_start(lw[:, 1536:2048], wl[0, :, 1536:2048]).then_inc(out_in, 16)
            sp.dma_start(w_ff1, wl[0, :, 2048:2560]).then_inc(ff1_in, 16)
            sp.dma_start(lw[:, 2560:3072], wl[0, :, 2560:3072]).then_inc(ff2_in, 16)
            sp.dma_start(headw[:, :], w_head).then_inc(a1_in, 16)
            sp.dma_start(a_wqkv[0], w_a1).then_inc(a1_in, 16)
            sp.dma_start(a1_wo, wo_a1).then_inc(a1_in, 16)
            sp.dma_start(rinw, w_r).then_inc(a2_in, 16)
            sp.dma_start(row_[:, :], w_ro).then_inc(a2_in, 16)
            sp.dma_start(a_wqkv[1], w_a2).then_inc(a2_in, 16)
            sp.dma_start(a2_wo, wo_a2).then_inc(a2_in, 16)
            sp.dma_start(downw, w_down).then_inc(ad_in, 16)
            sp.dma_start(upw, w_up).then_inc(ad_in, 16)
            with sp.Fori(0, L - 1) as i:
                sp.wait_ge(wlo_set, i * 2 + 1)
                sp.dma_start(w_qkv, wl[i + 1, :, 0:1536]).then_inc(qkv_in, 16)
                sp.wait_ge(full["ctxw"], i * B + B)
                sp.wait_ge(attbias_added, i * B + B)
                sp.dma_start(lw[:, 1536:2048], wl[i + 1, :, 1536:2048]).then_inc(out_in, 16)
                sp.dma_start(lr[:, 0:D], lrows[i + 1, 0:D].partition_broadcast(P)).then_inc(out_in, 16)
                sp.wait_ge(done["ff1"], i * B + B)
                sp.wait_ge(wlo_set, i * 2 + 2)
                sp.dma_start(lc[:, :], lcols[i + 1]).then_inc(lc_in, 16)
                sp.dma_start(w_ff1, wl[i + 1, :, 2048:2560]).then_inc(ff1_in, 16)
                sp.wait_ge(full["ff2"], i * B + B)
                sp.wait_ge(ffbias_added, i * B + B)
                sp.dma_start(lw[:, 2560:3072], wl[i + 1, :, 2560:3072]).then_inc(ff2_in, 16)
                sp.dma_start(lr[:, D:2 * D], lrows[i + 1, D:2 * D].partition_broadcast(P)).then_inc(ff2_in, 16)
            sp.wait_ge(wlo_set, 2 * L - 1)
            sp.dma_start(w_qkv, wl[L - 1, :, 0:1536]).then_inc(qkv_in, 16)
            sp.wait_ge(wlo_set, 2 * L + 1)
            sp.wait_ge(full["ff2"], L * B)
            sp.dma_start(fc1w, w_fc1).then_inc(fc_in, 16)
            sp.dma_start(fc2w, w_fc2).then_inc(fc_in, 16)
            for b in range(B):
                sp.wait_ge(done["up"], b + 1)
                sp.dma_start(out[b], os_[:, tiles(b), :]).then_inc(stored, 16)
            sp.wait_ge(stored, 16 * B)

        @block.gpsimd
        def _(pool):
            nc.gpsimd.memset(epsilon[:, :], EPS)
            nc.gpsimd.memset(minushalf[:, :], -0.5).then_inc(half_set, 1)
            pool.wait_ge(half_set, 1)

            def inverse_std(k, b):
                pool.wait_ge(ln_moments, k)
                nc.gpsimd.tensor_tensor(vareps[:, tiles(b)], moments[:, tiles(b), 1], epsilon[:, :],
                                        ALU.add).then_inc(ln_eps, 1)
                pool.wait_ge(ln_eps, k)
                nc.gpsimd.tensor_tensor(rstd[:, tiles(b)], vareps[:, tiles(b)], minushalf[:, :],
                                        ALU.pow).then_inc(ln_rstd, 1)

            for b in range(B):
                if b == 2:
                    pool.wait_ge(full["conv"], 2)
                    nc.gpsimd.memset(mid[:, 4096:6144], 0.0).then_inc(ctxT_zeroed, 1)
                inverse_std(b + 1, b)
            pool.wait_ge(rows_in, 48)
            with pool.Fori(0, L) as i:
                for b in range(B):
                    pool.wait_ge(done["ln1T"], i * B + (b + 1))
                    nc.gpsimd.tensor_tensor(y_parts[:, 1, b, :], yT[:, b, :], y_parts[:, 0, b, :].bitcast(f32),
                                            ALU.subtract).then_inc(ylo_set, 1)
                pool.wait_ge(out_in, i * 32 + 16)
                for b in range(B):
                    pool.wait_ge(normed, i * (2 * B) + b + 1)
                    nc.gpsimd.tensor_tensor(xs[:, tiles(b), :], xs[:, tiles(b), :],
                                            lr[:, 0:D].unsqueeze(1).broadcast_to([P, TPB, D]),
                                            ALU.add).then_inc(attbias_added, 1)
                for b in range(B):
                    pool.wait_ge(qrec_set, i * B + b + 1)
                    nc.gpsimd.tensor_tensor(qs[:, tiles(b), :, :], qs[:, tiles(b), :, :],
                                            qrec[:, tiles(b), :].unsqueeze(3).broadcast_to([P, TPB, NH, DH]),
                                            ALU.mult).then_inc(qs_set, 1)
                pool.wait_ge(full["ctx"], i * B + B)
                nc.gpsimd.tensor_tensor(pool_pause[:, :], epsilon[:, :], epsilon[:, :], ALU.add)
                nc.gpsimd.memset(mid[:, 0:3072], 0.0).then_inc(av_zeroed, 1)
                for name, b in (("std", 0), ("std", 1), ("std", 2), ("lo", 0), ("std", 3), ("lo", 1), ("lo", 2),
                                ("lo", 3)):
                    if name == "lo":
                        pool.wait_ge(done["ln2T"], i * B + (b + 1))
                        nc.gpsimd.tensor_tensor(y_parts[:, 1, b, :], yT[:, b, :], y_parts[:, 0, b, :].bitcast(f32),
                                                ALU.subtract).then_inc(ylo_set, 1)
                    else:
                        pool.wait_ge(ln_moments, i * (2 * B) + B + b + 1)
                        nc.gpsimd.tensor_tensor(vareps[:, tiles(b)], moments[:, tiles(b), 1], epsilon[:, :],
                                                ALU.add).then_inc(ln_eps, 1)
                        pool.wait_ge(ln_eps, i * (2 * B) + B + b + 1)
                        nc.gpsimd.tensor_tensor(rstd[:, tiles(b)], vareps[:, tiles(b)], minushalf[:, :],
                                                ALU.pow).then_inc(ln_rstd, 1)
                for b in range(B):
                    pool.wait_ge(normed, i * (2 * B) + B + b + 1)
                    if b == 0:
                        pool.wait_ge(ff2_in, i * 32 + 16)
                    nc.gpsimd.tensor_tensor(xs[:, tiles(b), :], xs[:, tiles(b), :],
                                            lr[:, D:2 * D].unsqueeze(1).broadcast_to([P, TPB, D]),
                                            ALU.add).then_inc(ffbias_added, 1)
                for b in range(B):
                    pool.wait_ge(ln_moments, i * (2 * B) + 2 * B + b + 1)
                    nc.gpsimd.tensor_tensor(vareps[:, tiles(b)], moments[:, tiles(b), 1], epsilon[:, :],
                                            ALU.add).then_inc(ln_eps, 1)
                    pool.wait_ge(ln_eps, i * (2 * B) + 2 * B + b + 1)
                    nc.gpsimd.tensor_tensor(rstd[:, tiles(b)], vareps[:, tiles(b)], minushalf[:, :],
                                            ALU.pow).then_inc(ln_rstd, 1)
            pool.wait_ge(av_zeroed, L)
            nc.gpsimd.memset(av[:, :, :, SUMROW:SUMROW + 1], 1.0).then_inc(ones_set, 1)
            for part, u, b in ORDER:
                if (part, b) in STATS_OF:
                    inverse_std(NORMS + STATS_OF[part, b], b)
                elif part == "an":
                    pool.wait_ge(normed, NORMS + NORM_OF["an", b])
                    nc.gpsimd.tensor_tensor(hs[:, tiles(b), :], hs[:, tiles(b), :], row("bo1"),
                                            ALU.add).then_inc(hbias_added, 1)
                    if b == B - 1:
                        nc.gpsimd.memset(negmax, 0.0).then_inc(negmax_zeroed, 1)
                elif part == "a2.r4":
                    pool.wait_ge(bits_set, b + 1)
                    nc.gpsimd.tensor_scalar(nbits[:, tiles(b), :], bits[:, tiles(b), :], -1.0, 1.0, ALU.mult,
                                            ALU.add).then_inc(nb_set, 1)
                    pool.wait_ge(nb_set, b + 1)
                    for k, (b0, b1) in enumerate(((nbits, nbits), (nbits, bits), (bits, nbits))):
                        last = nc.gpsimd.tensor_tensor(sel[:, tiles(b), k], b0[:, tiles(b), 0], b1[:, tiles(b), 1],
                                                       ALU.mult)
                    last.then_inc(sel_set, 1)
                elif part == "fc2":
                    pool.wait_ge(done["fc2"], b + 1)
                    nc.gpsimd.tensor_tensor(hs[:, tiles(b), :], hs[:, tiles(b), :], os_[:, tiles(b), :],
                                            ALU.add).then_inc(hout_set, 1)

        @block.scalar
        def _(act):
            for k in range(KC // KG):
                act.dma_start(conv_w[:, KG * k:KG * (k + 1), :], cw[k]).then_inc(first_in[k], 16)
            act.dma_start(ident[:, :], ident_d).then_inc(ident_in, 16)
            act.dma_start(sel_f32, selectors).then_inc(sel_in, 16)
            act.dma_start(colp[:, :], cols).then_inc(params_in, 16)
            act.dma_start(rowp[:, :], rows.partition_broadcast(P)).then_inc(rows_in, 16)
            act.dma_start(lr[:, 0:D], lrows[0, 0:D].partition_broadcast(P)).then_inc(rows_in, 16)
            act.dma_start(lr[:, D:2 * D], lrows[0, D:2 * D].partition_broadcast(P)).then_inc(rows_in, 16)
            act.dma_start(lc[:, :], lcols[0]).then_inc(lc_in, 16)
            act.wait_ge(params_in, 16)
            for h in range(2):
                act.wait_ge(full["conv"], h + 1)
                nc.scalar.activation(embT[:, 512 * h:512 * (h + 1)], slot("conv", h)[:, 0:512], ACT.Identity,
                                     bias=col("conv_b")).then_inc(done["conv"], 1)
            act.wait_ge(qkv_in, 16)
            nc.scalar.copy(qkv_parts[:, 0, :], w_qkv).then_inc(whi_set, 1)
            act.wait_ge(half_set, 1)

            def load_table(function):
                nc.scalar.activation(act_pause[:, :], epsilon[:, :], function)

            with act.Fori(0, L) as i:
                load_table(ACT.Exp)
                act.wait_ge(lc_in, i * 16 + 16)
                for name, b in QKV_SCALAR:
                    if name == "q":
                        act.wait_ge(done["q"], i * B + (b + 1))
                        nc.scalar.activation(qs[:, tiles(b), :, :], qs[:, tiles(b), :, :],
                                             ACT.Exp).then_inc(qexp_set, 1)
                    elif name == "v":
                        act.wait_ge(full["v"], i * B + (b + 1))
                        nc.scalar.copy(vv[:, tiles(b), :],
                                       slot("v", b).rearrange("p (t f) -> p t f", t=TPB)).then_inc(done["v"], 1)
                    elif name == "ln1T":
                        act.wait_ge(full["ln1T"], i * B + (b + 1))
                        if b in DVE_NORMS:
                            act.wait_ge(ydve_set, i * 4 + (b - 1))
                        else:
                            nc.scalar.activation(yT[:, b, :], slot("ln1T", b)[:, 0:N], ACT.Identity,
                                                 scale=lcol("ln1_g"), bias=lcol("ln1_b"))
                        nc.scalar.activation(y_parts[:, 0, b, :], slot("ln1T", b)[:, 0:N], ACT.Identity,
                                             scale=lcol("ln1_g"), bias=lcol("ln1_b")).then_inc(done["ln1T"], 1)
                    else:
                        act.wait_ge(nkmax_set, i * B + (b + 1))
                        for a in range(PAIRS):
                            last = nc.scalar.activation(ekT[:, b, a, :], slot("k", b)[:, N * a:N * (a + 1)], ACT.Exp,
                                                        bias=nkmax[:, b, a:a + 1], accum_out=ksum[:, b, a:a + 1])
                        last.then_inc(done["k"], 1)
                for b in range(B):
                    act.wait_ge(full["kT"], i * B + (b + 1))
                    nc.scalar.copy(ek[:, tiles(b), :],
                                   slot("kT", b).rearrange("p (t f) -> p t f", t=TPB)).then_inc(done["kT"], 1)
                for b in range(B):
                    act.wait_ge(full["qT"], i * B + (b + 1))
                    nc.scalar.copy(qT[:, b, :, :],
                                   slot("qT", b).rearrange("p (a n) -> p a n", a=PAIRS)).then_inc(done["qT"], 1)
                act.wait_ge(ff1_in, i * 16 + 16)
                nc.scalar.copy(ff1_parts[:, 0, :], w_ff1).then_inc(whi_set, 1)
                act.wait_ge(qkv_in, i * 16 + 32)
                nc.scalar.copy(qkv_parts[:, 0, :], w_qkv).then_inc(whi_set, 1)
                load_table(ACT.Gelu)
                for name, b in LN2F:
                    if name == "ln2T":
                        act.wait_ge(full["ln2T"], i * B + (b + 1))
                        if b in DVE_NORMS:
                            act.wait_ge(ydve_set, i * 4 + (b - 1 + 2))
                        else:
                            nc.scalar.activation(yT[:, b, :], slot("ln2T", b)[:, 0:N], ACT.Identity,
                                                 scale=lcol("ln2_g"), bias=lcol("ln2_b"))
                        nc.scalar.activation(y_parts[:, 0, b, :], slot("ln2T", b)[:, 0:N], ACT.Identity,
                                             scale=lcol("ln2_g"), bias=lcol("ln2_b")).then_inc(done["ln2T"], 1)
                    elif name == "ff1":
                        act.wait_ge(full["ff1"], i * B + (b + 1))
                        for m in range(PAIRS):
                            last = nc.scalar.activation(hidT[:, b, m, :], slot("ff1", b)[:, N * m:N * (m + 1)],
                                                        ACT.Gelu, bias=lcol("ff1_b", m))
                        last.then_inc(done["ff1"], 1)
            def copy_halves(name, b):
                act.wait_ge(full[name], b + 1)
                nc.scalar.copy(xT[:, b, :, :], slot(name, b)[0:EH, 0:2 * N].rearrange("p (c n) -> p c n", c=2)
                               ).then_inc(done[name], 1)

            load_table(ACT.Exp)
            for part, u, b in ORDER:
                if part in ("a1.xT", "a2.nT", "outT", "selT"):
                    copy_halves(part, b)
                elif part == "lnfT":
                    act.wait_ge(full["lnfT"], b + 1)
                    nc.scalar.activation(yT[:, b, :], slot("lnfT", b)[:, 0:N], ACT.Identity, scale=col("lnf_g"),
                                         bias=col("lnf_b")).then_inc(done["lnfT"], 1)
                elif part == "at.s" and INSTANCES[b][0] == "a1":
                    p, b = b, INSTANCES[b][1]
                    act.wait_ge(smax_set, unit("at.s", u, b) + 1)
                    s = slot("at.s", unit("at.s", u, p)).rearrange("p (r x n) -> p r x n", r=2, x=2)
                    for r in range(2):
                        for x in range(2):
                            h = 4 * (u % G) + 2 * x + r
                            last = nc.scalar.activation(probs[:, p % 2, u, r, x, :], s[:, r, x, :], ACT.Exp,
                                                        bias=smax[:, p, u // G, h:h + 1],
                                                        accum_out=ssum[:, b, u // G, h:h + 1])
                    last.then_inc(done["at.s"], 1)
                elif part == "at.s":
                    k = unit("at.s", u, b)
                    act.wait_ge(full["at.s"], k + 1)
                    nc.scalar.activation(probs[:, b % 2, u, :, :, :],
                                         slot("at.s", k).rearrange("p (r x n) -> p r x n", r=2, x=2),
                                         ACT.Exp).then_inc(done["at.s"], 1)
                elif part == "a2.zT":
                    act.wait_ge(full["a2.zT"], b + 1)
                    for c in range(2):
                        last = nc.scalar.activation(xT[:, b, c, :], slot("a2.zT", b)[0:EH, N * c:N * (c + 1)],
                                                    ACT.Identity, scale=col("r_g", c, EH), bias=col("r_b", c, EH))
                    last.then_inc(xnormed, 1)
                elif part == "a2.r1":
                    act.wait_ge(full["a2.r1"], b + 1)
                    nc.scalar.activation(eT, slot("a2.r1", b)[:, 0:N], ACT.Gelu,
                                         bias=col("r_in_b")).then_inc(done["a2.r1"], 1)
                elif part == "a2.r2":
                    act.wait_ge(full["a2.r2"], b + 1)
                    act.wait_ge(done["a2.rg"], b + 1)
                    nc.scalar.activation(h1T, slot("a2.r2", b)[:, 0:N], ACT.Gelu,
                                         bias=h1bias[:, b:b + 1]).then_inc(done["a2.r2"], 1)
                elif part == "a2.r3":
                    act.wait_ge(full["a2.r3"], b + 1)
                    nc.scalar.activation(h2T, slot("a2.r3", b)[0:RL, 0:N], ACT.Gelu,
                                         bias=col("o2_b", 0, RL)).then_inc(done["a2.r3"], 1)
                elif part == "a2.rep":
                    k, z = unit("a2.rep", u, b), INSTANCES.index(("a2", b)) % 2
                    act.wait_ge(full["a2.rep"], k + 1)
                    s = slot("a2.rep", k).rearrange("p (a n) -> p a n", a=4)
                    nq = (4, 2, 0)[u]
                    for a0, a1, bias in ((0, nq, 0.0), (nq, 4, col("maxrows"))):
                        if a1 > a0:
                            last = nc.scalar.activation(qk_wide[:, z, 4 * u + a0:4 * u + a1, :], s[:, a0:a1, :],
                                                        ACT.Identity, bias=bias)
                    last.then_inc(done["a2.rep"], 1)
                elif part == "hT":
                    act.wait_ge(full["hT"], b + 1)
                    for c in range(2):
                        last = nc.scalar.activation(xT[:, b, c, :], slot("hT", b)[0:EH, N * c:N * (c + 1)],
                                                    ACT.Identity, scale=col("g2", c, EH), bias=col("b2", c, EH))
                    last.then_inc(done["hT"], 1)
                elif part == "fc1":
                    k, m0 = unit("fc1", u, b), 3 * u
                    act.wait_ge(full["fc1"], k + 1)
                    for m in range(3):
                        last = nc.scalar.activation(hid2T[:, m0 + m, :], slot("fc1", k)[:, N * m:N * (m + 1)],
                                                    ACT.Gelu, bias=col("fc1_b", m0 + m))
                    last.then_inc(done["fc1"], 1)

        @block.vector
        def _(dve):
            def norm_stats(k, b, src):
                for t in range(TPB):
                    last = nc.vector.bn_stats(stats[:, TPB * b + t, :], src[:, TPB * b + t, :])
                last.then_inc(ln_stats, 1)
                dve.wait_ge(ln_stats, k)
                nc.vector.memset(pause[:, :], 0.0)
                for t in range(TPB):
                    last = nc.vector.bn_aggr(moments[:, TPB * b + t, :], stats[:, TPB * b + t, :])
                last.then_inc(ln_moments, 1)

            def normalise(k, b, dst, src):
                dve.wait_ge(ln_rstd, k)
                for t in range(TPB * b, TPB * (b + 1)):
                    last = nc.vector.tensor_scalar(dst[:, t, :], src[:, t, :], moments[:, t, 0:1], rstd[:, t:t + 1],
                                                   ALU.subtract, ALU.mult)
                last.then_inc(normed, 1)

            def gain_and_shift(k, b, norm):
                dve.wait_ge(full[norm + "T"], k)
                nc.vector.tensor_scalar(yT[:, b, :], slot(norm + "T", b)[:, 0:N], lcol(norm + "_g"),
                                        lcol(norm + "_b"), ALU.mult, ALU.add).then_inc(ydve_set, 1)

            for b in range(B):
                dve.wait_ge(full["embed"], b + 1)
                nc.vector.tensor_copy(xs[:, tiles(b), :],
                                      slot("embed", b)[:, 0:TPB * D].rearrange("p (t d) -> p t d", t=TPB)
                                      ).then_inc(done["embed"], 1)
                dve.wait_ge(done["embed"], b + 1)
                norm_stats(b + 1, b, xs)
                if b == B - 1:
                    dve.wait_ge(whi_set, 1)
                    nc.vector.tensor_tensor(qkv_parts[:, 1, :], w_qkv, qkv_parts[:, 0, :].bitcast(f32),
                                            ALU.subtract).then_inc(wlo_set, 1)
                if b > 0:
                    normalise(b, b - 1, nrm[:, :, 0:D], xs)
                if b == 1:
                    dve.wait_ge(sel_in, 16)
                    nc.vector.tensor_copy(selr.rearrange("p v k m -> p (v k m)"), sel_f32).then_inc(sel_cast, 1)
            normalise(B, B - 1, nrm[:, :, 0:D], xs)
            dve.wait_ge(ctxT_zeroed, 1)

            with dve.Fori(0, L) as i:
                for name, b in QKV:
                    if name == "ln1T" and b in DVE_NORMS:
                        if b == DVE_NORMS[0]:
                            dve.wait_ge(lc_in, i * 16 + 16)
                        gain_and_shift(i * B + (b + 1), b, "ln1")
                    elif name == "k":
                        dve.wait_ge(full["k"], i * B + (b + 1))
                        nc.vector.tensor_reduce(nkmax[:, b, :], slot("k", b).rearrange("p (a n) -> p a n", a=PAIRS),
                                                X, ALU.max, negate=True).then_inc(nkmax_set, 1)
                    elif name == "q":
                        dve.wait_ge(full["q"], i * B + (b + 1))
                        q = slot("q", b).rearrange("p (t h d) -> p t h d", t=TPB, h=NH)
                        nc.vector.tensor_reduce(qmax[:, tiles(b), :], q, X, ALU.max).then_inc(qmax_set, 1)
                        dve.wait_ge(qmax_set, i * B + (b + 1))
                        nc.vector.tensor_tensor(qs[:, tiles(b), :, :], q,
                                                qmax[:, tiles(b), :].unsqueeze(3).broadcast_to([P, TPB, NH, DH]),
                                                ALU.subtract).then_inc(done["q"], 1)
                for b in range(B):
                    dve.wait_ge(qexp_set, i * B + (b + 1))
                    nc.vector.tensor_reduce(qsum[:, tiles(b), :], qs[:, tiles(b), :, :], X,
                                            ALU.add).then_inc(qsum_set, 1)
                    dve.wait_ge(qsum_set, i * B + (b + 1))
                    nc.vector.reciprocal(qrec[:, tiles(b), :], qsum[:, tiles(b), :]).then_inc(qinv_set, 1)
                    dve.wait_ge(qinv_set, i * B + (b + 1))
                    nc.vector.tensor_scalar(qrec[:, tiles(b), :], qrec[:, tiles(b), :], DH ** -0.5, None,
                                            ALU.mult).then_inc(qrec_set, 1)
                for b in range(B):
                    dve.wait_ge(full["ctx"], i * B + (b + 1))
                    c = slot("ctx", b)[:, 0:PAIRS * DH].rearrange("p (a d) -> p a d", a=PAIRS)
                    nc.vector.tensor_copy(ctxT[0:DH, b, :, 0:DH], c[0:DH, :, :])
                    nc.vector.tensor_copy(ctxT[DH:P, b, :, DH:P], c[DH:P, :, :]).then_inc(done["ctx"], 1)
                for b in range(B):
                    nc.vector.reciprocal(krec[:, b, :], ksum[:, b, :]).then_inc(ksum_inv, 1)
                    dve.wait_ge(ksum_inv, i * B + (b + 1))
                    dve.wait_ge(full["ctxw"], i * B + (b + 1))
                    nc.vector.tensor_tensor(ctxw[:, b, :, :],
                                            slot("ctxw", b)[:, 0:PAIRS * D].rearrange("p (a d) -> p a d", a=PAIRS),
                                            krec[:, b, :].unsqueeze(2).broadcast_to([P, PAIRS, D]),
                                            ALU.mult).then_inc(done["ctxw"], 1)
                for k, (parts, w) in enumerate(((ff1_parts, w_ff1), (qkv_parts, w_qkv))):
                    dve.wait_ge(whi_set, i * 2 + (k + 2))
                    nc.vector.tensor_tensor(parts[:, 1, :], w, parts[:, 0, :].bitcast(f32),
                                            ALU.subtract).then_inc(wlo_set, 1)
                for name, added, k0 in (("att", attbias_added, B), ("ff2", ffbias_added, 2 * B)):
                    for b in range(B):
                        dve.wait_ge(added, i * B + (b + 1))
                        dve.wait_ge(full[name], i * B + (b + 1))
                        nc.vector.tensor_tensor(xs[:, tiles(b), :],
                                                slot(name, b)[:, 0:TPB * D].rearrange("p (t d) -> p t d", t=TPB),
                                                xs[:, tiles(b), :], ALU.add).then_inc(done[name], 1)
                        dve.wait_ge(done[name], i * B + (b + 1))
                        norm_stats(i * (2 * B) + (k0 + b + 1), b, xs)
                        if b > 0:
                            normalise(i * (2 * B) + (k0 + b), b - 1, nrm[:, :, 0:D], xs)
                    normalise(i * (2 * B) + (k0 + B), B - 1, nrm[:, :, 0:D], xs)
                    if name == "att":
                        for b in DVE_NORMS:
                            gain_and_shift(i * B + (b + 1), b, "ln2")

            dve.wait_ge(ones_set, 1)
            for part, u, i in ORDER:
                p = i if part in ("at.qk", "at.v", "at.s", "scale", "pvout") else 0
                a, b = INSTANCES[p] if part in ("at.qk", "at.v", "at.s", "scale", "pvout") else (None, i)
                if part == "head":
                    dve.wait_ge(full["head"], b + 1)
                    nc.vector.tensor_tensor(hs[:, tiles(b), :],
                                            slot("head", b)[:, :].rearrange("p (t f) -> p t f", t=TPB)[:, :, 0:E],
                                            row("head_b"), ALU.add).then_inc(done["head"], 1)
                    dve.wait_ge(done["head"], b + 1)
                    norm_stats(NORMS + STATS_OF["head", b], b, hs)
                elif part == "an":
                    normalise(NORMS + STATS_OF["head", b], b, nrm, hs)
                elif part == "at.qk":
                    dve.wait_ge(full["at.qk"], p + 1)
                    if p > 0:
                        a0, b0 = INSTANCES[p - 1]
                        dve.wait_ge(parts_set, p)
                        dve.wait_ge(full[a0 + ".rep"], 3 * (b0 + 1))
                    nc.vector.tensor_tensor(qkf, slot("at.qk", p)[:, 0:G * N].rearrange("p (g n) -> p g n", g=G),
                                            cols_of("qkb" + a[1]).unsqueeze(2).broadcast_to([P, G, N]),
                                            ALU.add).then_inc(done["at.qk"], 1)
                    dve.wait_ge(done["at.qk"], p + 1)
                    nc.vector.tensor_copy(qk_parts[:, 0, :, :], qkf).then_inc(hi_set, 1)
                    dve.wait_ge(hi_set, p + 1)
                    nc.vector.tensor_tensor(qk_parts[:, 1, :, :], qkf, qk_parts[:, 0, :, :].bitcast(f32),
                                            ALU.subtract).then_inc(parts_set, 1)
                elif part == "at.v":
                    dve.wait_ge(full["at.v"], p + 1)
                    at = ROW["bv" + a[1]][0]
                    for t in range(TPB):
                        last = nc.vector.tensor_tensor(
                            av[:, TPB * b + t, :, 0:AD],
                            slot("at.v", p)[:, 512 * t:512 * t + E].rearrange("p (h e) -> p h e", h=AH),
                            rowp[:, at:at + E].rearrange("p (h e) -> p h e", h=AH), ALU.add)
                    last.then_inc(done["at.v"], 1)
                elif part == "a1.rep":
                    k, z = unit("a1.rep", u, b), INSTANCES.index(("a1", b)) % 2
                    dve.wait_ge(full["a1.rep"], k + 1)
                    nc.vector.tensor_copy(qk_wide[:, z, 4 * u:4 * u + 4, :],
                                          slot("a1.rep", k).rearrange("p (a n) -> p a n", a=4)
                                          ).then_inc(done["a1.rep"], 1)
                elif part == "at.s" and a == "a1" or part == "a2.m":
                    k = unit(part, u, i)
                    q = p if part == "at.s" else INSTANCES.index(("a2", b))
                    dve.wait_ge(full[part], k + 1)
                    nc.vector.tensor_reduce(
                        smax[:, q, u // G, 4 * (u % G):4 * (u % G) + 4].rearrange("p (x r) -> p r x", x=2),
                        slot(part, k).rearrange("p (r x n) -> p r x n", r=2, x=2), X,
                        ALU.max, negate=True).then_inc(smax_set if part == "at.s" else done["a2.m"], 1)
                elif part == "scale":
                    dve.wait_ge(done["at.s"], 6 * (p + 1))
                    nc.vector.reciprocal(srec[:, b, :, :], ssum[:, b, :, :]).then_inc(srec_set, 1)
                    dve.wait_ge(srec_set, b + 1)
                    dve.wait_ge(done["at.v"], p + 1)
                    nc.vector.tensor_tensor(
                        av[:, tiles(b), :, 0:AD], av[:, tiles(b), :, 0:AD],
                        srec[:, b, :, :].unsqueeze(3).broadcast_to([P, TPB, AH, AD]), ALU.mult).then_inc(av_set, 1)
                elif part == "pvout":
                    dve.wait_ge(full["at.pv"], p + 1)
                    nc.vector.tensor_copy(actxT[:, b, :, :],
                                          slot("at.pv", p)[:, 0:G * N].rearrange("p (g n) -> p g n", g=G)
                                          ).then_inc(done["at.pv"], 1)
                elif part == "a1.o":
                    dve.wait_ge(hbias_added, b + 1)
                    dve.wait_ge(full["a1.o"], b + 1)
                    nc.vector.tensor_tensor(hs[:, tiles(b), :],
                                            slot("a1.o", b)[:, :].rearrange("p (t f) -> p t f", t=TPB)[:, :, 0:E],
                                            hs[:, tiles(b), :], ALU.add).then_inc(done["a1.o"], 1)
                    dve.wait_ge(done["a1.o"], b + 1)
                    norm_stats(NORMS + STATS_OF[part, b], b, hs)
                elif part == "z":
                    normalise(NORMS + STATS_OF["a1.o", b], b, zs, hs)
                    dve.wait_ge(normed, NORMS + NORM_OF[part, b])
                    norm_stats(NORMS + STATS_OF[part, b], b, zs)
                elif part == "zn":
                    normalise(NORMS + STATS_OF["z", b], b, nrm, zs)
                elif part == "a2.zT":
                    dve.wait_ge(xnormed, b + 1)
                    for c in range(2):
                        last = nc.vector.tensor_scalar(xaT[:, b % 2, c, :], slot("a2.zT", b)[0:EH, N * c:N * (c + 1)],
                                                       col("g1", c, EH), col("b1", c, EH), ALU.mult, ALU.add)
                    last.then_inc(done["a2.zT"], 1)
                elif part == "a2.rg":
                    dve.wait_ge(done["a2.r1"], b + 1)
                    nc.vector.tensor_reduce(emean[:, b:b + 1], eT[:, 1:N], X, ALU.add).then_inc(esum_set, 1)
                    dve.wait_ge(esum_set, b + 1)
                    nc.vector.tensor_scalar(emean[:, b:b + 1], emean[:, b:b + 1], 1.0 / (N - 1), None,
                                            ALU.mult).then_inc(emean_set, 1)
                    dve.wait_ge(full["a2.rg"], b + 1)
                    nc.vector.tensor_scalar(h1bias[:, b:b + 1], slot("a2.rg", b)[:, 0:1], col("o1_b"), None,
                                            ALU.add).then_inc(done["a2.rg"], 1)
                elif part == "a2.r4":
                    dve.wait_ge(full["a2.r4"], b + 1)
                    nc.vector.tensor_tensor(
                        logits[:, tiles(b), :, :].rearrange("p t k c -> p t (k c)"),
                        slot("a2.r4", b)[:, 0:4 * TPB].rearrange("p (t c) -> p t c", t=TPB),
                        row("o3_b"), ALU.add).then_inc(done["a2.r4"], 1)
                    dve.wait_ge(done["a2.r4"], b + 1)
                    nc.vector.tensor_tensor(bits[:, tiles(b), :], logits[:, tiles(b), :, 1],
                                            logits[:, tiles(b), :, 0], ALU.is_gt).then_inc(bits_cmp, 1)
                    dve.wait_ge(bits_cmp, b + 1)
                    nc.vector.memset(bits[0:1, TPB * b, :], 1.0).then_inc(bits_set, 1)
                elif part == "nm":
                    q = INSTANCES.index(("a2", b))
                    dve.wait_ge(done["a2.m"], 6 * (b + 1))
                    if b > 0:
                        dve.wait_ge(full["a2.mT"], 2 * b)
                    else:
                        dve.wait_ge(negmax_zeroed, 1)
                    nc.vector.tensor_copy(negmax[:, :, :, MAXROW].bitcast(f32r),
                                          smax[:, q, :, :]).then_inc(nmhi_set, 1)
                    dve.wait_ge(nmhi_set, b + 1)
                    nc.vector.tensor_tensor(negmax[:, :, :, MAXROW + 1], smax[:, q, :, :], negmax[:, :, :, MAXROW],
                                            ALU.subtract).then_inc(nm_set, 1)
                elif part == "a2.mT":
                    k, z = unit("a2.mT", u, b), INSTANCES.index(("a2", b)) % 2
                    dve.wait_ge(full["a2.mT"], k + 1)
                    a0, n = (0, 4) if u == 0 else (4, 2)
                    q = qk_wide[:, z, a0:a0 + n, :]
                    nc.vector.tensor_tensor(q, slot("a2.mT", k)[:, 0:N * n].rearrange("p (a n) -> p a n", a=n),
                                            q.bitcast(f32), ALU.add).then_inc(done["a2.mT"], 1)
                elif part == "a2.cT":
                    dve.wait_ge(full["a2.cT"], b + 1)
                    for t in range(TPB):
                        c = slot("a2.cT", b)[:, 512 * t:512 * t + G * P].rearrange("p (h e) -> p h e", h=AH)
                        last = nc.vector.reciprocal(crec[:, TPB * b + t, :], c[:, :, SUMROW])
                    last.then_inc(crec_set, 1)
                    dve.wait_ge(crec_set, b + 1)
                    for t in range(TPB):
                        c = slot("a2.cT", b)[:, 512 * t:512 * t + G * P].rearrange("p (h e) -> p h e", h=AH)
                        last = nc.vector.tensor_tensor(
                            catt[:, TPB * b + t, :].rearrange("p (h e) -> p h e", h=AH), c[:, :, 0:AD],
                            crec[:, TPB * b + t, :].unsqueeze(2).broadcast_to([P, AH, AD]), ALU.mult)
                    last.then_inc(done["a2.cT"], 1)
                elif part == "a2.o":
                    dve.wait_ge(full["a2.o"], b + 1)
                    nc.vector.tensor_tensor(os_[:, tiles(b), :],
                                            slot("a2.o", b)[:, :].rearrange("p (t f) -> p t f", t=TPB)[:, :, 0:E],
                                            row("bo2"), ALU.add).then_inc(done["a2.o"], 1)
                    dve.wait_ge(done["a2.o"], b + 1)
                    dve.wait_ge(bits_set, b + 1)
                    for t in range(TPB * b, TPB * (b + 1)):
                        last = nc.vector.scalar_tensor_tensor(out=os_[:, t, :], in0=os_[:, t, :],
                                                              scalar=bits[:, t, 0:1], in1=zs[:, t, :],
                                                              op0=ALU.mult, op1=ALU.add)
                    last.then_inc(hmix_set, 1)
                    dve.wait_ge(hmix_set, b + 1)
                    norm_stats(NORMS + STATS_OF[part, b], b, os_)
                elif part == "hn":
                    normalise(NORMS + STATS_OF["a2.o", b], b, nrm, os_)
                elif part == "fc2":
                    dve.wait_ge(full["fc2"], b + 1)
                    nc.vector.tensor_tensor(zs[:, tiles(b), :],
                                            slot("fc2", b)[:, :].rearrange("p (t f) -> p t f", t=TPB)[:, :, 0:E],
                                            row("fc2_b"), ALU.add).then_inc(ffbias2_set, 1)
                    dve.wait_ge(ffbias2_set, b + 1)
                    for t in range(TPB * b, TPB * (b + 1)):
                        last = nc.vector.scalar_tensor_tensor(out=os_[:, t, :], in0=zs[:, t, :],
                                                              scalar=bits[:, t, 1:2], in1=os_[:, t, :],
                                                              op0=ALU.mult, op1=ALU.add)
                    last.then_inc(done["fc2"], 1)
                elif part == "down":
                    dve.wait_ge(full["down"], b + 1)
                    dve.wait_ge(sel_set, b + 1)
                    for t in range(TPB):
                        last = nc.vector.tensor_tensor(
                            nrm[:, TPB * b + t, :].rearrange("p (k r) -> p k r", k=NA),
                            slot("down", b)[:, 512 * t:512 * t + E].rearrange("p (k r) -> p k r", k=NA),
                            sel[:, TPB * b + t, :].unsqueeze(2).broadcast_to([P, NA, E // NA]), ALU.mult)
                    last.then_inc(done["down"], 1)
                elif part == "up":
                    dve.wait_ge(full["up"], b + 1)
                    dve.wait_ge(hout_set, b + 1)
                    nc.vector.tensor_tensor(os_[:, tiles(b), :],
                                            slot("up", b)[:, :].rearrange("p (t f) -> p t f", t=TPB)[:, :, 0:E],
                                            hs[:, tiles(b), :], ALU.add).then_inc(done["up"], 1)

        @block.tensor
        def _(pe):
            mm, tr = nc.tensor.matmul, nc.tensor.transpose

            def patch_products(h, ks):
                for k in ks:
                    if h == 0 and k % KG == 0:
                        pe.wait_ge(first_in[k // KG], 32)
                    if h == 1 and k % (KC // NSECOND) == 0:
                        pe.wait_ge(second_in[k // (KC // NSECOND)], 16)
                    last = mm(slot("conv", h)[:, 0:512], conv_w[:, k, :], image[:, h, k, :], start=(k == 0),
                              stop=(k == KC - 1))
                return last

            def embedding_tokens(b):
                s = take(pe, "embed", b)
                pe.wait_ge(done["conv"], b // 2 + 1)
                for t in range(TPB):
                    at = N * b + P * t
                    last = tr(s[:, P * t:P * (t + 1)], embT[:, at:at + P], ident[:, :])
                last.then_inc(full["embed"], 1)

            patch_products(0, range(KC)).then_inc(full["conv"], 1)
            patch_products(1, range(KC // 2))
            pe.wait_ge(ident_in, 16)
            embedding_tokens(0)
            embedding_tokens(1)
            patch_products(1, range(KC // 2, KC)).then_inc(full["conv"], 1)
            embedding_tokens(2)
            embedding_tokens(3)

            def norm_128(b, s, name):
                for t in range(TPB):
                    last = tr(s[:, P * t:P * (t + 1)], nrm[:, TPB * b + t, 0:D], ident[:, :])
                last.then_inc(full[name], 1)

            def in_parts(out_, stationary, moving):
                for n, (x, y) in enumerate(((0, 0), (0, 1), (1, 0))):
                    last = mm(out_, stationary(x), moving(y), start=(n == 0), stop=(n == 2))
                return last

            def tokens_512(s, b, at):
                for t in range(TPB):
                    last = in_parts(s[:, INNER * t:INNER * (t + 1)], lambda o: y_parts[:, o, b, P * t:P * (t + 1)],
                                    lambda o: qkv_parts[:, o, at:at + INNER])
                return last

            with pe.Fori(0, L) as i:
                for name, b in QKV:
                    s = take(pe, name, b, i)
                    if name == "ln1T":
                        pe.wait_ge(normed, i * (2 * B) + (b + 1))
                        norm_128(b, s, "ln1T")
                    elif name in ("q", "v"):
                        tokens_512(s, b, 0 if name == "q" else 2 * INNER).then_inc(full[name], 1)
                    else:
                        pe.wait_ge(ylo_set, i * (2 * B) + (b + 1))
                        if b == 0:
                            pe.wait_ge(wlo_set, i * 2 + 1)
                        for a in range(PAIRS):
                            at = INNER + P * a
                            last = in_parts(s[:, N * a:N * (a + 1)], lambda o: qkv_parts[:, o, at:at + P],
                                            lambda o: y_parts[:, o, b, :])
                        last.then_inc(full["k"], 1)
                for b in range(B):
                    s = take(pe, "kT", b, i)
                    pe.wait_ge(done["k"], i * B + (b + 1))
                    for t in range(TPB):
                        for a in range(PAIRS):
                            at = INNER * t + P * a
                            last = tr(s[:, at:at + P], ekT[:, b, a, P * t:P * (t + 1)], ident[:, :])
                    last.then_inc(full["kT"], 1)
                for b in range(B):
                    s = take(pe, "ctx", b, i)
                    pe.wait_ge(done["v"], i * B + (b + 1))
                    pe.wait_ge(done["kT"], i * B + (b + 1))
                    for a in range(PAIRS):
                        for t in range(TPB):
                            for h in range(2):
                                f = slice(P * a + DH * h, P * a + DH * (h + 1))
                                last = mm(s[DH * h:DH * (h + 1), DH * a:DH * (a + 1)], vv[:, TPB * b + t, f],
                                          ek[:, TPB * b + t, f], start=(t == 0), stop=(t == TPB - 1))
                    last.then_inc(full["ctx"], 1)
                for b in range(B):
                    s = take(pe, "qT", b, i)
                    pe.wait_ge(qs_set, i * B + (b + 1))
                    for a in range(PAIRS):
                        for t in range(TPB):
                            q = qs[:, TPB * b + t, 2 * a:2 * a + 2, :].rearrange("p h d -> p (h d)")
                            at = N * a + P * t
                            last = tr(s[:, at:at + P], q, ident[:, :])
                    last.then_inc(full["qT"], 1)
                pe.wait_ge(out_in, i * 32 + 16)
                for b in range(B):
                    s = take(pe, "ctxw", b, i)
                    pe.wait_ge(done["ctx"], i * B + (b + 1))
                    for a in range(PAIRS):
                        last = mm(s[:, D * a:D * (a + 1)], ctxT[:, b, a, :], w_out[:, a, :], start=True, stop=True)
                    last.then_inc(full["ctxw"], 1)
                for b in range(B):
                    s = take(pe, "att", b, i)
                    pe.wait_ge(done["qT"], i * B + (b + 1))
                    pe.wait_ge(done["ctxw"], i * B + (b + 1))
                    for t in range(TPB):
                        for a in range(PAIRS):
                            last = mm(s[:, D * t:D * (t + 1)], qT[:, b, a, P * t:P * (t + 1)], ctxw[:, b, a, :],
                                      start=(a == 0), stop=(a == PAIRS - 1))
                    last.then_inc(full["att"], 1)
                for name, b in LN2F:
                    s = take(pe, name, b, i)
                    if name == "ln2T":
                        pe.wait_ge(normed, i * (2 * B) + (B + b + 1))
                        norm_128(b, s, "ln2T")
                    elif name == "ff2":
                        if b == 0:
                            pe.wait_ge(ff2_in, i * 32 + 16)
                        pe.wait_ge(done["ff1"], i * B + (b + 1))
                        for t in range(TPB):
                            for m in range(PAIRS):
                                last = mm(s[:, D * t:D * (t + 1)], hidT[:, b, m, P * t:P * (t + 1)], w_ff2[:, m, :],
                                          start=(m == 0), stop=(m == PAIRS - 1))
                        last.then_inc(full["ff2"], 1)
                    else:
                        pe.wait_ge(ylo_set, i * (2 * B) + (B + b + 1))
                        if b == 0:
                            pe.wait_ge(wlo_set, i * 2 + 2)
                        for m in range(PAIRS):
                            last = in_parts(s[:, N * m:N * (m + 1)], lambda o: ff1_parts[:, o, P * m:P * (m + 1)],
                                            lambda o: y_parts[:, o, b, :])
                        last.then_inc(full["ff1"], 1)

            def transposed(name, b, src):
                s = take(pe, name, b)
                for c in range(2):
                    for t in range(TPB):
                        at = N * c + P * t
                        last = tr(s[0:EH, at:at + P], src[:, TPB * b + t, EH * c:EH * (c + 1)], ident[:, :])
                last.then_inc(full[name], 1)

            def features_out(name, k, w, groups, x):
                s = take(pe, name, k)
                for g in range(groups):
                    for c in range(2):
                        last = mm(s[:, N * g:N * (g + 1)], w[:, c, P * g:P * (g + 1)], x[:, c, :],
                                  start=(c == 0), stop=(c == 1))
                last.then_inc(full[name], 1)

            def tokens_out(name, k, w, x):
                s = take(pe, name, k)
                for t in range(TPB):
                    for c in range(2):
                        last = mm(s[:, 512 * t:512 * t + E], x[:, c, P * t:P * (t + 1)], w[:, c, :],
                                  start=(c == 0), stop=(c == 1))
                last.then_inc(full[name], 1)

            def scores(name, k, z, stationary, moving):
                s = take(pe, name, k)
                t, g = k % 6 // G, k % G
                for x in range(2):
                    for r in range(2):
                        rows_ = slice(64 * r, 64 * r + 64)
                        at = 512 * r + N * x
                        last = mm(s[:, at:at + N], qk_wide[rows_, z, stationary + 2 * g + x, P * t:P * (t + 1)],
                                  qk_wide[rows_, z, moving + 2 * g + x, :], start=True, stop=True)
                last.then_inc(full[name], 1)

            QUERIES, KEYS = 0, AP2
            pe.wait_ge(sel_cast, 1)
            pe.wait_ge(a1_in, 48)
            pe.wait_ge(a2_in, 64)
            for part, u, i in ORDER:
                by_instance = part in ("at.qk", "at.v", "at.s", "at.pv")
                p, (a, b) = i, INSTANCES[i] if by_instance else (None, i)
                if part == "lnfT":
                    s = take(pe, "lnfT", b)
                    pe.wait_ge(normed, 2 * L * B + b + 1)
                    norm_128(b, s, "lnfT")
                elif part == "head":
                    s = take(pe, "head", b)
                    pe.wait_ge(done["lnfT"], b + 1)
                    for t in range(TPB):
                        last = mm(s[:, 512 * t:512 * t + E], yT[:, b, P * t:P * (t + 1)], headw[:, :], start=True,
                                  stop=True)
                    last.then_inc(full["head"], 1)
                elif part == "a1.xT":
                    pe.wait_ge(normed, NORMS + NORM_OF["an", b])
                    transposed("a1.xT", b, nrm)
                elif part == "a2.zT":
                    pe.wait_ge(normed, NORMS + NORM_OF["zn", b])
                    transposed("a2.zT", b, nrm)
                elif part == "at.qk":
                    pe.wait_ge(done["a1.xT" if a == "a1" else "a2.zT"], b + 1)
                    features_out("at.qk", p, a_wqkv[0 if a == "a1" else 1], G,
                                 xT[:, b, :, :] if a == "a1" else xaT[:, b % 2, :, :])
                elif part == "at.v":
                    pe.wait_ge(done["a1.xT" if a == "a1" else "a2.zT"], b + 1)
                    tokens_out("at.v", p, a_wqkv[0 if a == "a1" else 1][:, :, 2 * E:3 * E],
                               xT[:, b, :, :] if a == "a1" else xaT[:, b % 2, :, :])
                elif part in ("a1.rep", "a2.rep"):
                    s = take(pe, part, unit(part, u, b))
                    pe.wait_ge(parts_set, INSTANCES.index((part[0:2], b)) + 1)
                    for x in range(4):
                        kind = 0 if 4 * u + x < AP2 else 2
                        at = slice(64 * (x // 2), 64 * (x // 2) + 64)
                        for o in range(2):
                            last = mm(s[:, N * x:N * (x + 1)], selr[at, x % 2, kind + o, :], qk_parts[at, o, u, :],
                                      start=(o == 0), stop=(o == 1))
                    last.then_inc(full[part], 1)
                elif part == "a2.m":
                    pe.wait_ge(done["a2.rep"], 3 * (b + 1))
                    scores("a2.m", unit("a2.m", u, b), INSTANCES.index(("a2", b)) % 2, QUERIES, KEYS)
                elif part == "a2.mT":
                    s = take(pe, "a2.mT", unit("a2.mT", u, b))
                    pe.wait_ge(nm_set, b + 1)
                    for x in range(4 if u == 0 else 2):
                        for t in range(TPB):
                            at, h = N * x + P * t, 2 * (4 * u + x)
                            last = tr(s[:, at:at + P], negmax[:, t, h:h + 2, :].rearrange("p h e -> p (h e)"),
                                      ident[:, :])
                    last.then_inc(full["a2.mT"], 1)
                elif part == "at.s":
                    pe.wait_ge(done["a1.rep"] if a == "a1" else done["a2.mT"], (3 if a == "a1" else 2) * (b + 1))
                    scores("at.s", unit("at.s", u, p), p % 2, KEYS, QUERIES)
                elif part == "at.pv":
                    s = take(pe, "at.pv", p)
                    pe.wait_ge(done["at.s"], 6 * (p + 1))
                    if a == "a1":
                        pe.wait_ge(av_set, b + 1)
                    else:
                        pe.wait_ge(done["at.v"], p + 1)
                    for g in range(G):
                        for t in range(TPB):
                            for j in range(4):
                                last = mm(s[32 * j:32 * j + 32, N * g:N * (g + 1)], av[:, TPB * b + t, 4 * g + j, :],
                                          probs[:, p % 2, G * t + g, j % 2, j // 2, :], start=(t == 0),
                                          stop=(t == TPB - 1))
                    last.then_inc(full["at.pv"], 1)
                elif part == "a1.o":
                    s = take(pe, "a1.o", b)
                    pe.wait_ge(done["at.pv"], INSTANCES.index(("a1", b)) + 1)
                    for t in range(TPB):
                        for g in range(G):
                            last = mm(s[:, 512 * t:512 * t + E], actxT[:, b, g, P * t:P * (t + 1)], a1_wo[:, g, :],
                                      start=(g == 0), stop=(g == G - 1))
                    last.then_inc(full["a1.o"], 1)
                elif part == "a2.r1":
                    pe.wait_ge(xnormed, b + 1)
                    features_out("a2.r1", b, rinw, 1, xT[:, b, :, :])
                elif part == "a2.rg":
                    s = take(pe, "a2.rg", b)
                    pe.wait_ge(emean_set, b + 1)
                    mm(s[:, 0:1], row_[:, RH:2 * RH], emean[:, b:b + 1], start=True,
                       stop=True).then_inc(full["a2.rg"], 1)
                elif part == "a2.r2":
                    s = take(pe, "a2.r2", b)
                    pe.wait_ge(done["a2.r1"], b + 1)
                    mm(s[:, 0:N], row_[:, 0:RH], eT, start=True, stop=True).then_inc(full["a2.r2"], 1)
                elif part == "a2.r3":
                    s = take(pe, "a2.r3", b)
                    pe.wait_ge(done["a2.r2"], b + 1)
                    mm(s[0:RL, 0:N], row_[:, 2 * RH:2 * RH + RL], h1T, start=True,
                       stop=True).then_inc(full["a2.r3"], 1)
                elif part == "a2.r4":
                    s = take(pe, "a2.r4", b)
                    pe.wait_ge(done["a2.r3"], b + 1)
                    for t in range(TPB):
                        last = mm(s[:, 4 * t:4 * t + 4], h2T[:, P * t:P * (t + 1)],
                                  row_[0:RL, 2 * RH + RL:2 * RH + RL + 4], start=True, stop=True)
                    last.then_inc(full["a2.r4"], 1)
                elif part == "a2.cT":
                    s = take(pe, "a2.cT", b)
                    pe.wait_ge(done["at.pv"], INSTANCES.index(("a2", b)) + 1)
                    for t in range(TPB):
                        for g in range(G):
                            at = 512 * t + P * g
                            last = tr(s[:, at:at + P], actxT[:, b, g, P * t:P * (t + 1)], ident[:, :])
                    last.then_inc(full["a2.cT"], 1)
                elif part == "a2.nT":
                    pe.wait_ge(done["a2.cT"], b + 1)
                    transposed("a2.nT", b, catt)
                elif part == "a2.o":
                    pe.wait_ge(done["a2.nT"], b + 1)
                    tokens_out("a2.o", b, a2_wo, xT[:, b, :, :])
                elif part == "hT":
                    pe.wait_ge(normed, NORMS + NORM_OF["hn", b])
                    transposed("hT", b, nrm)
                elif part == "fc1":
                    if b == 0 and u == 0:
                        pe.wait_ge(fc_in, 32)
                    s = take(pe, "fc1", unit("fc1", u, b))
                    pe.wait_ge(done["hT"], b + 1)
                    for m in range(3):
                        for c in range(2):
                            last = mm(s[:, N * m:N * (m + 1)], fc1w[:, c, P * (3 * u + m):P * (3 * u + m + 1)],
                                      xT[:, b, c, :], start=(c == 0), stop=(c == 1))
                    last.then_inc(full["fc1"], 1)
                elif part == "fc2":
                    s = take(pe, "fc2", b)
                    pe.wait_ge(done["fc1"], 2 * (b + 1))
                    for t in range(TPB):
                        for m in range(HM):
                            last = mm(s[:, 512 * t:512 * t + E], hid2T[:, m, P * t:P * (t + 1)], fc2w[:, m, :],
                                      start=(m == 0), stop=(m == HM - 1))
                    last.then_inc(full["fc2"], 1)
                elif part == "outT":
                    if b == 0:
                        pe.wait_ge(ad_in, 32)
                    pe.wait_ge(done["fc2"], b + 1)
                    transposed("outT", b, os_)
                elif part == "down":
                    pe.wait_ge(done["outT"], b + 1)
                    tokens_out("down", b, downw, xT[:, b, :, :])
                elif part == "selT":
                    pe.wait_ge(done["down"], b + 1)
                    transposed("selT", b, nrm)
                elif part == "up":
                    pe.wait_ge(done["selT"], b + 1)
                    tokens_out("up", b, upw, xT[:, b, :, :])


def spread(w):
    w = w.reshape(w.shape[:-1] + (AH, AD))
    wide = np.zeros(w.shape[:-1] + (32,), w.dtype)
    wide[..., :AD] = w
    return wide.reshape(w.shape[:-2] + (AH * 32,))


def halves(w):
    return np.ascontiguousarray(w.reshape(2, EH, -1).transpose(1, 0, 2))


def columns(v, n):
    c = np.zeros((P, n), v.dtype)
    c[:v.size // n] = v.reshape(n, -1).T
    return c


def selector_matrices():
    m = np.zeros((2, 64, 2, 4, 2, 64), np.float32)
    for kind, slots in enumerate(((0, 1), (2,), (0, 2), (1,))):
        for half in range(2):
            for head in range(2):
                for d in range(AD):
                    for s in slots:
                        m[:, 32 * half + AD * head + d, half, kind, head, AD * s + d] = AD ** -0.5 if kind < 2 else 1.0
    return m.reshape(P, 2 * 4 * P)


def kernel(**inputs):
    import concourse.bacc as bacc
    from concourse.bass_utils import run_bass_kernel_spmd

    v = {k: np.asarray(a) for k, a in inputs.items()}
    t = {k[len("L0_tok_"):]: a for k, a in v.items() if k.startswith("L0_tok_")}
    a = {k[len("L0_attn_"):]: x for k, x in v.items() if k.startswith("L0_attn_")}
    f = {k[len("L0_ffn_"):]: x for k, x in v.items() if k.startswith("L0_ffn_")}
    hp = IMG // PATCH
    im = v["x"].reshape(B, C_IN, hp, PATCH, hp, PATCH).transpose(1, 3, 5, 0, 2, 4).reshape(KC, P, 2, 512)
    im = im.transpose(2, 1, 0, 3)
    cw = t["conv_w"].reshape(D, KC // KG, KG, P).transpose(1, 3, 2, 0)
    wl = np.concatenate([
        t["qkv_w"],
        t["out_w"].reshape(L, PAIRS, P, D).transpose(0, 2, 1, 3).reshape(L, P, INNER),
        t["ff1_w"],
        t["ff2_w"].reshape(L, PAIRS, P, D).transpose(0, 2, 1, 3).reshape(L, P, M)], axis=2)
    lcols = np.stack([np.concatenate([columns(t["ln1_g"][i], 1), columns(t["ln1_b"][i], 1), columns(t["ln2_g"][i], 1),
                                      columns(t["ln2_b"][i], 1), columns(t["ff1_b"][i], PAIRS)], axis=1)
                      for i in range(L)])
    lrows = np.concatenate([t["out_b"], t["ff2_b"]], axis=1)

    def both(q, k):
        return np.concatenate([q.reshape(-1), k.reshape(-1)])

    max_rows = np.zeros((2, 64), np.float32)
    max_rows[:, MAXROW:MAXROW + 2] = 1.0
    col_values = {"conv_b": t["conv_b"], "lnf_g": t["lnf_g"], "lnf_b": t["lnf_b"], "qkb1": both(a["bq"], a["bk"]),
                  "r_g": f["r_ln_g"], "r_b": f["r_ln_b"], "g1": f["ln1_g"],
                  "b1": f["ln1_b"], "g2": f["ln2_g"], "b2": f["ln2_b"], "r_in_b": f["r_in_b"], "o1_b": f["r_o1_b"],
                  "o2_b": f["r_o2_b"], "qkb2": both(f["bq"], f["bk"]), "maxrows": max_rows.reshape(-1),
                  "fc1_b": f["fc1_b"]}
    cols = np.concatenate([columns(col_values[n], COL[n][1]) for n in COL], axis=1)
    row_values = {"head_b": t["head_b"], "bv1": a["bv"].reshape(-1), "bo1": a["bo"], "bv2": f["bv"], "bo2": f["bo"],
                  "fc2_b": f["fc2_b"], "o3_b": f["r_o3_b"]}
    rows = np.concatenate([row_values[n] for n in ROW])
    w_a1 = halves(np.concatenate([a[n].transpose(1, 0, 2).reshape(E, E) for n in ("Wq", "Wk", "Wv")], axis=1))
    wo_a1 = spread(a["Wo"].T).T.reshape(G, P, E).transpose(1, 0, 2)
    w_a2 = halves(np.concatenate([f["wq"].T, f["wk"].T, f["wv"].T], axis=1))
    w_ro = np.concatenate([f["r_o1_w"].T[:RH], f["r_o1_w"].T[RH:], f["r_o2_w"].T,
                           np.concatenate([f["r_o3_w"].T, np.zeros((RH - RL, 4), np.float32)])], axis=1)
    arrays = {
        "im0": im[0].reshape(P, KC // KG, KG, 512).transpose(1, 0, 2, 3),
        "im1": im[1].reshape(P, NSECOND, KC // NSECOND, 512).transpose(1, 0, 2, 3), "cw": cw, "wl": wl,
        "lcols": lcols, "lrows": lrows, "cols": cols, "rows": rows, "ident": np.eye(P, dtype=np.float32),
        "selectors": selector_matrices(), "w_head": t["head_w"], "w_a1": w_a1, "wo_a1": wo_a1, "w_a2": w_a2,
        "wo_a2": halves(f["wo"].T), "w_r": halves(f["r_in_w"].T), "w_ro": w_ro, "w_fc1": halves(f["fc1_w"].T),
        "w_fc2": f["fc2_w"].T.reshape(HM, P, E).transpose(1, 0, 2), "w_down": halves(f["lra_down"].reshape(E, E).T),
        "w_up": halves(f["lra_up"].transpose(0, 2, 1).reshape(E, E))}
    arrays = {k: np.ascontiguousarray(x) for k, x in arrays.items()}
    nc = bacc.Bacc("TRN2", target_bir_lowering=False, num_devices=1)
    args = [nc.dram_tensor(k, x.shape, mybir.dt.from_np(x.dtype), kind="ExternalInput").ap()
            for k, x in arrays.items()]
    args.append(nc.dram_tensor("out", (B, P, TPB, E), mybir.dt.float32, kind="ExternalOutput").ap())
    build(nc, *args)
    r = run_bass_kernel_spmd(nc, [arrays], core_ids=[0])
    got = r.results[0]["out"]
    return np.ascontiguousarray(got.transpose(0, 2, 1, 3)).reshape(B, N, E)
```
